# Optimizing a Trainium2 kernel written in Bass

```python
import numpy as np
import jax
import jax.numpy as jnp

def _softmax(x, axis=-1):
    return jax.nn.softmax(x, axis=axis)

def _gelu(x):
    return jax.nn.gelu(x, approximate=True)

def _silu(x):
    return jax.nn.silu(x)

def _sigmoid(x):
    return jax.nn.sigmoid(x)

def _layernorm(x, axis=-1, eps=1e-05):
    m = jnp.mean(x, axis=axis, keepdims=True)
    v = jnp.var(x, axis=axis, keepdims=True)
    return (x - m) / jnp.sqrt(v + eps)

def _scatter_add(tgt, idx, src, axis=0):
    return tgt.at[idx].add(src)

def _segment_sum(src, seg, n):
    return jax.ops.segment_sum(src, seg, n)
kernel_name = 'mk_gnn_preln_d4_gnn_r64_7e463f'

def setup_inputs(seed: int=0):
    np.random.seed(seed)
    _w = jnp.asarray

    def _rec_inputs():
        import jax
        import jax.numpy as jnp
        _gk = jax.random.key(seed)
        x = -0.000202 + 1 * jax.random.normal(jax.random.fold_in(_gk, 1), (100000, 64), jnp.float32)
        src = jax.random.randint(jax.random.fold_in(_gk, 2), (25000,), 0, 100000, jnp.int32)
        dst = jnp.minimum((100000 * jax.random.uniform(jax.random.fold_in(_gk, 3), (25000,)) ** 2.0).astype(jnp.int32), 99999)
        _o = jnp.argsort(dst, stable=True)
        src = src[_o]
        dst = dst[_o]
        edge_attr_16 = 0.000189758 + 1.00013 * jax.random.normal(jax.random.fold_in(_gk, 12), (25000, 16), jnp.float32)
        edge_attr_32 = 0.000102155 + 1.00015 * jax.random.normal(jax.random.fold_in(_gk, 13), (25000, 32), jnp.float32)
        edge_weight = -1.20086e-11 + 0.13101 * jax.random.normal(jax.random.fold_in(_gk, 15), (25000,), jnp.float32)
        return (x, src, dst, edge_attr_16, edge_attr_32, edge_weight)
    x, src, dst, edge_attr_16, edge_attr_32, edge_weight = _rec_inputs()

    def _L0_gnn_setup():
        import jax, jax.numpy as jnp
        import numpy as np
        N = 100000
        E = 50000
        D_IN = 64
        D_EDGE = 16
        H = 16

        def _edge_conv(h, src, dst, edge_attr, W, b, num_nodes):
            m = jnp.concatenate([h[src], edge_attr], axis=-1) @ W + b
            return jax.ops.segment_sum(m, dst, num_segments=num_nodes)
        key = jax.random.key(seed)
        ks = jax.random.split(key, 12)
        x = jax.random.normal(ks[0], (N, D_IN), dtype=jnp.float32)
        edge_index = jax.random.randint(ks[1], (2, E), 0, N, dtype=jnp.int32)
        edge_attr = jax.random.normal(ks[2], (E, D_EDGE), dtype=jnp.float32)
        s = 0.05
        W_msg1 = jax.random.normal(ks[3], (D_IN + D_EDGE, H), dtype=jnp.float32) * s
        b_msg1 = jnp.zeros((H,), dtype=jnp.float32)
        W_skip1 = jax.random.normal(ks[4], (D_IN, H), dtype=jnp.float32) * s
        b_skip1 = jnp.zeros((H,), dtype=jnp.float32)
        W_msg2 = jax.random.normal(ks[5], (H + D_EDGE, H), dtype=jnp.float32) * s
        b_msg2 = jnp.zeros((H,), dtype=jnp.float32)
        W_skip2 = jax.random.normal(ks[6], (H, H), dtype=jnp.float32) * s
        b_skip2 = jnp.zeros((H,), dtype=jnp.float32)
        W_lin3 = jax.random.normal(ks[7], (H, D_IN), dtype=jnp.float32) * s
        b_lin3 = jnp.zeros((D_IN,), dtype=jnp.float32)
        return {'x': x, 'edge_index': edge_index, 'edge_attr': edge_attr, 'W_msg1': W_msg1, 'b_msg1': b_msg1, 'W_skip1': W_skip1, 'b_skip1': b_skip1, 'W_msg2': W_msg2, 'b_msg2': b_msg2, 'W_skip2': W_skip2, 'b_skip2': b_skip2, 'W_lin3': W_lin3, 'b_lin3': b_lin3}
    _L0_gnn_all = _L0_gnn_setup()
    _L0_gnn_in = {k: v for k, v in _L0_gnn_all.items() if k in ('W_msg1', 'b_msg1', 'W_skip1', 'b_skip1', 'W_msg2', 'b_msg2', 'W_skip2', 'b_skip2', 'W_lin3', 'b_lin3')}
    del _L0_gnn_all

    def _L1_gnn_setup():
        import jax, jax.numpy as jnp
        import numpy as np
        N_NODES = 100000
        N_EDGES = 15625
        NODE_DIM = 64
        EDGE_DIM = 32
        HIDDEN = 64

        def _unif(key, shape, fan_in):
            bound = 1.0 / np.sqrt(fan_in)
            return jax.random.uniform(key, shape, jnp.float32, -bound, bound)
        key = jax.random.key(seed)
        ks = jax.random.split(key, 11)
        node_features = jax.random.normal(ks[0], (N_NODES, NODE_DIM), jnp.float32)
        edge_index = jax.random.randint(ks[1], (2, N_EDGES), 0, N_NODES, dtype=jnp.int64)
        edge_features = jax.random.normal(ks[2], (N_EDGES, EDGE_DIM), jnp.float32)
        in_dim = 2 * NODE_DIM + EDGE_DIM
        W1 = _unif(ks[3], (HIDDEN, in_dim), in_dim)
        b1 = _unif(ks[4], (HIDDEN,), in_dim)
        W2 = _unif(ks[5], (HIDDEN, HIDDEN), HIDDEN)
        b2 = _unif(ks[6], (HIDDEN,), HIDDEN)
        w_ih = _unif(ks[7], (3 * NODE_DIM, HIDDEN), NODE_DIM)
        w_hh = _unif(ks[8], (3 * NODE_DIM, NODE_DIM), NODE_DIM)
        b_ih = _unif(ks[9], (3 * NODE_DIM,), NODE_DIM)
        b_hh = _unif(ks[10], (3 * NODE_DIM,), NODE_DIM)
        return {'node_features': node_features, 'edge_index': edge_index, 'edge_features': edge_features, 'W1': W1, 'b1': b1, 'W2': W2, 'b2': b2, 'w_ih': w_ih, 'w_hh': w_hh, 'b_ih': b_ih, 'b_hh': b_hh}
    _L1_gnn_all = _L1_gnn_setup()
    _L1_gnn_in = {k: v for k, v in _L1_gnn_all.items() if k in ('W1', 'b1', 'W2', 'b2', 'w_ih', 'w_hh', 'b_ih', 'b_hh')}
    del _L1_gnn_all

    def _L2_gnn_setup():
        import jax, jax.numpy as jnp
        import numpy as np
        N = 100000
        E = 25000
        DIN = 64
        DOUT = 64
        K = 10
        T = 1.0
        key = jax.random.key(seed)
        k1, k2, k3 = jax.random.split(key, 3)
        x = jax.random.normal(k1, (N, DIN), dtype=jnp.float32)
        W = jax.random.normal(k2, (K + 1, DIN, DOUT), dtype=jnp.float32) / np.sqrt(DIN).astype(np.float32)
        bias = jnp.zeros((DOUT,), dtype=jnp.float32)
        edge_index = jax.random.randint(k3, (2, E), 0, N, dtype=jnp.int32)
        return {'x': x, 'W': W, 'bias': bias, 'edge_index': edge_index, 'num_nodes': N}
    _L2_gnn_all = _L2_gnn_setup()
    _L2_gnn_in = {k: v for k, v in _L2_gnn_all.items() if k in ('W', 'bias')}
    del _L2_gnn_all

    def _L3_gnn_setup():
        import jax, jax.numpy as jnp
        import numpy as np
        N = 50000
        C = 64
        E_OFF = 12500
        N_SUB = 4
        M_TERMS = 20

        def _expm_multiply(x, edge_src, edge_dst, edge_w, t):
            n = x.shape[0]
            scale = -(t[0] / N_SUB)

            def A_apply(v):
                return scale * jax.ops.segment_sum(edge_w[:, None] * v[edge_dst], edge_src, num_segments=n)
            ks = jnp.arange(1, M_TERMS + 1, dtype=x.dtype)

            def substep(v, _):

                def taylor(carry, k):
                    term, acc = carry
                    term = A_apply(term) / k
                    return ((term, acc + term), None)
                (_, acc), _ = jax.lax.scan(taylor, (v, v), ks)
                return (acc, None)
            out, _ = jax.lax.scan(substep, x, None, length=N_SUB)
            return out
        key = jax.random.key(seed)
        k1, k2, k3, k4, k5 = jax.random.split(key, 5)
        src = jax.random.randint(k1, (E_OFF,), 0, N)
        dst = jax.random.randint(k2, (E_OFF,), 0, N)
        w = jax.random.uniform(k3, (E_OFF,), dtype=jnp.float32) / 16.0
        deg = jax.ops.segment_sum(w, src, num_segments=N)
        edge_src = jnp.concatenate([src, jnp.arange(N, dtype=src.dtype)])
        edge_dst = jnp.concatenate([dst, jnp.arange(N, dtype=dst.dtype)])
        edge_w = jnp.concatenate([-w, deg])
        x = jax.random.normal(k4, (N, C), dtype=jnp.float32)
        t = jax.random.uniform(k5, (1,), dtype=jnp.float32) * 0.2 + 1e-08
        return {'x': x, 'edge_src': edge_src, 'edge_dst': edge_dst, 'edge_w': edge_w, 't': t}
    _L3_gnn_all = _L3_gnn_setup()
    _L3_gnn_in = {k: v for k, v in _L3_gnn_all.items() if k in ('t',)}
    del _L3_gnn_all
    return {'x': x, 'src': src, 'dst': dst, 'edge_attr_16': edge_attr_16, 'edge_attr_32': edge_attr_32, 'edge_weight': edge_weight, 'L0_gnn_W_msg1': _L0_gnn_in['W_msg1'], 'L0_gnn_b_msg1': _L0_gnn_in['b_msg1'], 'L0_gnn_W_skip1': _L0_gnn_in['W_skip1'], 'L0_gnn_b_skip1': _L0_gnn_in['b_skip1'], 'L0_gnn_W_msg2': _L0_gnn_in['W_msg2'], 'L0_gnn_b_msg2': _L0_gnn_in['b_msg2'], 'L0_gnn_W_skip2': _L0_gnn_in['W_skip2'], 'L0_gnn_b_skip2': _L0_gnn_in['b_skip2'], 'L0_gnn_W_lin3': _L0_gnn_in['W_lin3'], 'L0_gnn_b_lin3': _L0_gnn_in['b_lin3'], 'L1_gnn_W1': _L1_gnn_in['W1'], 'L1_gnn_b1': _L1_gnn_in['b1'], 'L1_gnn_W2': _L1_gnn_in['W2'], 'L1_gnn_b2': _L1_gnn_in['b2'], 'L1_gnn_w_ih': _L1_gnn_in['w_ih'], 'L1_gnn_w_hh': _L1_gnn_in['w_hh'], 'L1_gnn_b_ih': _L1_gnn_in['b_ih'], 'L1_gnn_b_hh': _L1_gnn_in['b_hh'], 'L2_gnn_W': _L2_gnn_in['W'], 'L2_gnn_bias': _L2_gnn_in['bias'], 'L3_gnn_t': _L3_gnn_in['t']}

def reference(x, src, dst, edge_attr_16, edge_attr_32, edge_weight, L0_gnn_W_msg1, L0_gnn_b_msg1, L0_gnn_W_skip1, L0_gnn_b_skip1, L0_gnn_W_msg2, L0_gnn_b_msg2, L0_gnn_W_skip2, L0_gnn_b_skip2, L0_gnn_W_lin3, L0_gnn_b_lin3, L1_gnn_W1, L1_gnn_b1, L1_gnn_W2, L1_gnn_b2, L1_gnn_w_ih, L1_gnn_w_hh, L1_gnn_b_ih, L1_gnn_b_hh, L2_gnn_W, L2_gnn_bias, L3_gnn_t):
    import jax
    import jax.numpy as jnp

    def _L0_gnn_ref(x, edge_index, edge_attr, W_msg1, b_msg1, W_skip1, b_skip1, W_msg2, b_msg2, W_skip2, b_skip2, W_lin3, b_lin3):
        import jax, jax.numpy as jnp
        import numpy as np
        N = 100000
        E = 50000
        D_IN = 64
        D_EDGE = 16
        H = 16

        def _edge_conv(h, src, dst, edge_attr, W, b, num_nodes):
            m = jnp.concatenate([h[src], edge_attr], axis=-1) @ W + b
            return jax.ops.segment_sum(m, dst, num_segments=num_nodes)
        src, dst = (edge_index[0], edge_index[1])
        n = x.shape[0]
        h = _edge_conv(x, src, dst, edge_attr, W_msg1, b_msg1, n) + (x @ W_skip1 + b_skip1)
        h = jax.nn.relu(h)
        h = _edge_conv(h, src, dst, edge_attr, W_msg2, b_msg2, n) + (h @ W_skip2 + b_skip2)
        return h @ W_lin3 + b_lin3

    def _L1_gnn_ref(node_features, edge_index, edge_features, W1, b1, W2, b2, w_ih, w_hh, b_ih, b_hh):
        import jax, jax.numpy as jnp
        import numpy as np
        N_NODES = 100000
        N_EDGES = 15625
        NODE_DIM = 64
        EDGE_DIM = 32
        HIDDEN = 64

        def _unif(key, shape, fan_in):
            bound = 1.0 / np.sqrt(fan_in)
            return jax.random.uniform(key, shape, jnp.float32, -bound, bound)
        src, dst = (edge_index[0], edge_index[1])
        x = jnp.concatenate([node_features[src], node_features[dst], edge_features], axis=-1)
        h = jax.nn.relu(x @ W1.T + b1)
        messages = h @ W2.T + b2
        agg = jax.ops.segment_sum(messages, dst, num_segments=node_features.shape[0])
        gi = agg @ w_ih.T + b_ih
        gh = node_features @ w_hh.T + b_hh
        i_r, i_z, i_n = jnp.split(gi, 3, axis=-1)
        h_r, h_z, h_n = jnp.split(gh, 3, axis=-1)
        r = jax.nn.sigmoid(i_r + h_r)
        z = jax.nn.sigmoid(i_z + h_z)
        n = jnp.tanh(i_n + r * h_n)
        return (1.0 - z) * n + z * node_features

    def _L2_gnn_ref(x, W, bias, edge_index, num_nodes):
        import jax, jax.numpy as jnp
        import numpy as np
        N = 100000
        E = 25000
        DIN = 64
        DOUT = 64
        K = 10
        T = 1.0
        row, col = (edge_index[0], edge_index[1])
        ones = jnp.ones((edge_index.shape[1],), dtype=x.dtype)
        deg = jax.ops.segment_sum(ones, row, num_segments=num_nodes)
        dinv = jnp.where(deg > 0, 1.0 / jnp.sqrt(jnp.where(deg > 0, deg, 1.0)), 0.0)
        norm = dinv[row] * dinv[col]

        def L_apply(h):
            msg = norm[:, None] * h[col]
            return h - jax.ops.segment_sum(msg, row, num_segments=num_nodes)
        out = jnp.zeros((num_nodes, W.shape[2]), dtype=x.dtype)
        h_k = x
        inv_f = 1.0
        for k in range(K + 1):
            out = out + h_k @ W[k] * inv_f
            if k < K:
                h_k = -T * L_apply(h_k)
                inv_f = inv_f / (k + 1)
        return out + bias

    def _L3_gnn_ref(x, edge_src, edge_dst, edge_w, t):
        import jax, jax.numpy as jnp
        import numpy as np
        N = 50000
        C = 64
        E_OFF = 12500
        N_SUB = 4
        M_TERMS = 20

        def _expm_multiply(x, edge_src, edge_dst, edge_w, t):
            n = x.shape[0]
            scale = -(t[0] / N_SUB)

            def A_apply(v):
                return scale * jax.ops.segment_sum(edge_w[:, None] * v[edge_dst], edge_src, num_segments=n)
            ks = jnp.arange(1, M_TERMS + 1, dtype=x.dtype)

            def substep(v, _):

                def taylor(carry, k):
                    term, acc = carry
                    term = A_apply(term) / k
                    return ((term, acc + term), None)
                (_, acc), _ = jax.lax.scan(taylor, (v, v), ks)
                return (acc, None)
            out, _ = jax.lax.scan(substep, x, None, length=N_SUB)
            return out
        t = jnp.clip(t, 1e-08)
        return _expm_multiply(x, edge_src, edge_dst, edge_w, t)
    edge_index = jnp.stack([src, dst])
    h = jnp.maximum(_layernorm(x, axis=-1), 0.0)
    x = x + _L0_gnn_ref(h, edge_index, edge_attr_16, L0_gnn_W_msg1, L0_gnn_b_msg1, L0_gnn_W_skip1, L0_gnn_b_skip1, L0_gnn_W_msg2, L0_gnn_b_msg2, L0_gnn_W_skip2, L0_gnn_b_skip2, L0_gnn_W_lin3, L0_gnn_b_lin3)
    h = jnp.maximum(_layernorm(x, axis=-1), 0.0)
    x = x + _L1_gnn_ref(h, edge_index, edge_attr_32, L1_gnn_W1, L1_gnn_b1, L1_gnn_W2, L1_gnn_b2, L1_gnn_w_ih, L1_gnn_w_hh, L1_gnn_b_ih, L1_gnn_b_hh)
    h = jnp.maximum(_layernorm(x, axis=-1), 0.0)
    x = x + _L2_gnn_ref(h, L2_gnn_W, L2_gnn_bias, edge_index, 100000)
    h = jnp.maximum(_layernorm(x, axis=-1), 0.0)
    x = x + _L3_gnn_ref(h, src, dst, edge_weight, L3_gnn_t)
    return x

_drawn_inputs = setup_inputs


def setup_inputs(seed=0):
    import zlib

    import numpy as np

    out = dict(_drawn_inputs(seed))
    spreads = {'L0_gnn_b_msg1': (0.0, 0.8),
     'L0_gnn_b_skip1': (0.0, 0.8),
     'L0_gnn_b_msg2': (0.0, 0.529),
     'L0_gnn_b_skip2': (0.0, 0.475),
     'L0_gnn_b_lin3': (0.0, 0.1),
     'L2_gnn_bias': (0.0, 0.1)}
    factors = {'edge_attr_32': 5.288,
     'edge_weight': 64.0,
     'L0_gnn_W_msg1': 8.0,
     'L0_gnn_W_skip1': 8.0,
     'L0_gnn_W_skip2': 6.652,
     'L1_gnn_W1': 2.94,
     'L1_gnn_b1': 31.83,
     'L1_gnn_b2': 5.021,
     'L1_gnn_b_hh': 3.293}
    for name, (base, spread) in spreads.items():
        noise = np.random.default_rng([zlib.crc32(name.encode()), seed]).standard_normal(out[name].shape)
        drawn = base * np.exp(spread * noise) if base else spread * noise
        out[name] = jnp.asarray(drawn.astype(out[name].dtype))
    for name, factor in factors.items():
        out[name] = (out[name] * factor).astype(out[name].dtype)
    return out
```

```python
from contextlib import ExitStack, nullcontext
from math import comb, factorial

import concourse.bass as bass
from concourse import mybir

F32 = mybir.dt.float32
I32 = mybir.dt.int32
U32 = mybir.dt.uint32
ALU = mybir.AluOpType
ACT = mybir.ActivationFunctionType
AX = mybir.AxisListType

P = 128
N, D, E = 100000, 64, 25000
TILES = -(-E // P)
EP = TILES * P
PAD = (1 << 17) - 1
DIGITS = [(0, 6), (6, 6), (12, 5)]
BINS = 64
GROUP = 7
GROUPS = TILES // GROUP
NO_ROW = 1 << 20
assert N < PAD and GROUPS * GROUP == TILES and GROUPS % 2 == 0

BANK = 512

NP, NC = 125, 16
CHUNKS = N // (NP * NC)
assert CHUNKS % 2 == 0 and CHUNKS * NP * NC == N


class Stage:

    def __init__(self, nc, name):
        self.nc, self.name, self.ctx = nc, name, ExitStack()
        self.sems, self.bank = [], 0
        self.passed = self.sem("wait_passed")

    def sb(self, name, shape, dt=F32):
        return self.ctx.enter_context(self.nc.sbuf_tensor(f"{self.name}_{name}", shape, dt))

    def ps(self, name, shape, dt=F32):
        at = self.bank * BANK
        self.bank += -(-shape[1] // BANK)
        assert self.bank <= 8
        return Stage.psum[0:shape[0], at:at + shape[1]]

    def sem(self, name):
        self.sems.append(self.nc.alloc_semaphore(f"{self.name}_{name}"))
        return self.sems[-1]

    def block(self):
        return self.ctx.enter_context(self.nc.Block())

    def close(self):
        self.ctx.close()
        self.nc.clear_and_free_semaphores(self.sems)
        self.nc.all_engine_barrier()

    def gate(self, eng, sem, value):
        eng.wait_ge(sem, value)
        if not isinstance(value, int):
            eng.sem_inc(self.passed, 1)


class Chain:

    def __init__(self, stage, eng, sem):
        self.stage, self.eng, self.sem, self.n, self.base = stage, eng, sem, 0, 0

    def link(self, ins):
        self.n += 1
        ins.then_inc(self.sem, 1)
        self.stage.gate(self.eng, self.sem, self.base + self.n)


def halves(eng, count, body):
    body(0, True, False)
    with eng.Fori(1, count - 1) as i:
        body(i, False, False)
    body(count - 1, False, True)


def identity(st, eng, tile, sem):
    eng.memset(tile[:, :], 0.0).then_inc(sem, 1)
    eng.wait_ge(sem, 1)
    eng.affine_select(out=tile[:, :], in_=tile[:, :], compare_op=ALU.not_equal, fill=1.0, base=0,
                      pattern=[[-1, P]], channel_multiplier=1).then_inc(sem, 1)


SRC, DST, WGT, EA16, EA32, REC = 0, 1, 2, 3, 19, 52
NARROW = 4


def sort_edges(nc, name, width, key, ping, pong, inputs=None, table=None):
    st = Stage(nc, name)
    rec = st.sb("records", [P, TILES, width])
    onehot = st.sb("onehot", [P, BINS, TILES])
    count = st.sb("count", [P, BINS, TILES])
    bins = st.sb("bins", [P, BINS])
    digit_i = st.sb("digit_i", [P, TILES], I32)
    digit = st.sb("digit", [P, TILES])
    inbin = st.sb("inbin", [P, BINS])
    base = st.sb("base", [P, BINS])
    upto = st.sb("upto", [P, BINS])
    rank = st.sb("rank", [P, TILES])
    rank_i = st.sb("rank_i", [P, TILES], U32)
    below = st.sb("below", [P, P])
    ones = st.sb("ones", [P, P])
    stage_i = [st.sb(f"stage_i{h}", [P, GROUP], U32) for h in (0, 1)]
    stage_r = [st.sb(f"stage_r{h}", [P, GROUP, width]) for h in (0, 1)]
    sums = st.ps("sums", [P, 2 * BINS])
    loaded, blank, consts, step, counted, summed = (st.sem(x) for x in ("loaded", "blank", "consts", "step", "counted", "summed"))
    staged = [st.sem(f"staged{h}") for h in (0, 1)]
    written = [st.sem(f"written{h}") for h in (0, 1)]
    rec_key = rec[:, :, key].bitcast(I32)
    passes = len(DIGITS)
    tables = [ping if (passes - 1 - n) % 2 == 0 else pong for n in range(passes)]
    block = st.block()
    half = GROUPS // 2

    full, rest = E // TILES, E % TILES

    if inputs:
        src, dst, weight, ea16, ea32 = inputs
        column = st.sb("column", [P, 3, TILES])
        first_loads = 16 * 10
    else:
        wide = st.sb("wide", [P, TILES, REC])
        first_loads = 16
    loads = [first_loads + 16 * n for n in range(passes)]

    @block.sync
    def _(sync):
        if inputs:
            sync.wait_ge(blank, 3)
            for a, to in ((src.bitcast(F32), column[:, 0, :]), (dst.bitcast(F32), column[:, 1, :]),
                          (weight, column[:, 2, :])):
                sync.dma_start(to[0:full, :], a[0:full * TILES].rearrange("(p t) -> p t", p=full)).then_inc(loaded, 16)
                sync.dma_start(to[full:full + 1, 0:rest], a[full * TILES:E].rearrange("(p t) -> p t", p=1)).then_inc(loaded, 16)
            for a, to in ((ea16, rec[:, :, EA16:EA16 + 16]), (ea32, rec[:, :, EA32:EA32 + 32])):
                sync.dma_start(to[0:full, :, :], a[0:full * TILES, :].rearrange("(p t) w -> p t w", p=full)).then_inc(loaded, 16)
                sync.dma_start(to[full:full + 1, 0:rest, :], a[full * TILES:E, :].rearrange("(p t) w -> p t w", p=1)).then_inc(loaded, 16)
        else:
            sync.dma_start(wide[:, :, :], table[0:EP, :].rearrange("(p t) w -> p t w", p=P)).then_inc(loaded, 16)
        for n in range(1, passes):
            for h in (0, 1):
                sync.wait_ge(written[h], 16 * GROUP * half * n)
            sync.dma_start(rec[:, :, :], tables[n - 1][0:EP, :].rearrange("(p t) w -> p t w", p=P)).then_inc(loaded, 16)

    @block.gpsimd
    def _(pool):
        if inputs:
            pool.memset(rec[:, :, :], 0.0).then_inc(blank, 1)
            pool.memset(column[:, 0:2, rest:].bitcast(I32), PAD).then_inc(blank, 1)
            pool.memset(column[:, 2, rest:], 0.0).then_inc(blank, 1)
        pool.iota(bins[:, :], pattern=[[1, BINS]], base=0, channel_multiplier=0,
                  allow_small_or_imprecise_dtypes=True).then_inc(consts, 1)
        pool.memset(ones[:, :], 1.0).then_inc(consts, 1)
        pool.memset(below[:, :], 1.0).then_inc(consts, 1)
        pool.wait_ge(consts, 3)
        pool.affine_select(out=below[:, :], in_=below[:, :], compare_op=ALU.is_gt, fill=0.0, base=0,
                           pattern=[[1, P]], channel_multiplier=-1).then_inc(consts, 1)
        for n in range(passes):
            def scatter(i, first, last):
                for h in (0, 1):
                    st.gate(pool, staged[h], (i + half * n) + 1)
                    for j in range(GROUP):
                        pool.indirect_dma_start(
                            tables[n][:, :], bass.IndirectOffsetOnAxis(ap=stage_i[h][:, j:j + 1], axis=0),
                            stage_r[h][:, j, :], None, bounds_check=EP - 1, oob_is_err=False,
                        ).then_inc(written[h], 16)
            halves(pool, half, scatter)
        for h in (0, 1):
            pool.wait_ge(written[h], 16 * GROUP * half * passes)

    @block.tensor
    def _(pe):
        pe.wait_ge(consts, 4)
        for n in range(passes):
            pe.wait_ge(counted, n + 1)
            nc.tensor.matmul(sums[:, 0:BINS], below[:, :], inbin[:, :], start=True, stop=True)
            nc.tensor.matmul(sums[:, BINS:], ones[:, :], inbin[:, :], start=True, stop=True).then_inc(summed, 1)

    @block.vector
    def _(dve):
        ch = Chain(st, dve, step)
        link = ch.link
        dve.wait_ge(consts, 4)
        for n, (shift, bits) in enumerate(DIGITS):
            dve.wait_ge(loaded, loads[n])
            if n == 0 and inputs:
                for at, c in ((SRC, 0), (DST, 1), (WGT, 2)):
                    link(nc.vector.tensor_copy(rec[:, :, at], column[:, c, :]))
            elif n == 0:
                link(nc.vector.tensor_copy(rec[:, :, :], wide[:, :, 0:width]))
            link(nc.vector.tensor_scalar(digit_i[:, :], rec_key, shift, (1 << bits) - 1,
                                         ALU.logical_shift_right, ALU.bitwise_and))
            link(nc.vector.tensor_copy(digit[:, :], digit_i[:, :]))
            link(nc.vector.tensor_tensor(onehot[:, :, :], digit[:, None, :].to_broadcast([P, BINS, TILES]),
                                         bins[:, :, None].to_broadcast([P, BINS, TILES]), ALU.is_equal))
            flat1 = onehot[:, :, :].rearrange("p b t -> p (b t)")
            flat2 = count[:, :, :].rearrange("p b t -> p (b t)")
            link(nc.vector.tensor_tensor_scan(flat2, flat1, flat1, 0.0, ALU.add, ALU.max))
            link(nc.vector.tensor_copy(upto[:, :], count[:, :, TILES - 1]))
            nc.vector.tensor_copy(inbin[:, 0:1], upto[:, 0:1])
            ins = nc.vector.tensor_tensor(inbin[:, 1:], upto[:, 1:], upto[:, 0:BINS - 1], ALU.subtract)
            ins.then_inc(counted, 1)
            dve.wait_ge(summed, n + 1)
            link(nc.vector.tensor_tensor_scan(base[:, :], sums[:, BINS:], bins[:, :], 0.0, ALU.add, ALU.bypass))
            link(nc.vector.tensor_tensor(base[:, :], base[:, :], sums[:, BINS:], ALU.subtract))
            link(nc.vector.tensor_tensor(base[:, :], base[:, :], sums[:, 0:BINS], ALU.add))
            link(nc.vector.tensor_tensor(base[:, 1:], base[:, 1:], upto[:, 0:BINS - 1], ALU.subtract))
            link(nc.vector.tensor_tensor(count[:, :, :], count[:, :, :],
                                         base[:, :, None].to_broadcast([P, BINS, TILES]), ALU.add))
            link(nc.vector.tensor_tensor(count[:, :, :], count[:, :, :], onehot[:, :, :], ALU.mult))
            link(nc.vector.tensor_reduce(rank[:, :], count[:, :, :].rearrange("p b t -> p t b"), AX.X, ALU.add))
            link(nc.vector.tensor_scalar(rank_i[:, :], rank[:, :], -1.0, None, ALU.add))

            def put(i, first, last):
                for h in (0, 1):
                    if n or not first:
                        st.gate(dve, written[h], (i + half * n) * (16 * GROUP))
                    g = (2 * i + h) * GROUP
                    nc.vector.tensor_copy(stage_i[h][:, :], rank_i[:, bass.ds(g, GROUP)])
                    nc.vector.tensor_copy(stage_r[h][:, :, :], rec[:, bass.ds(g, GROUP), :]).then_inc(staged[h], 1)
            halves(dve, half, put)
    st.close()


def broadcast(vector, partitions):
    return vector.rearrange("(a n) -> a n", a=1).to_broadcast([partitions, vector.shape[0]])


def by_chunk(table):
    return table[0:N, :].rearrange("(p c j) w -> p c j w", p=NP, c=CHUNKS)


class Norm:

    def __init__(self, st, nc):
        self.st, self.nc = st, nc
        self.total = [st.sb(f"ln_total{h}", [NP, NC]) for h in (0, 1)]
        self.var = [st.sb(f"ln_var{h}", [NP, NC]) for h in (0, 1)]
        self.std = [st.sb(f"ln_std{h}", [NP, NC]) for h in (0, 1)]
        self.centred = [st.sb(f"ln_centred{h}", [NP, NC, D]) for h in (0, 1)]
        self.square = [st.sb(f"ln_square{h}", [NP, NC, D]) for h in (0, 1)]
        self.eps = st.sb("ln_eps", [NP, 1])
        self.is_centred, self.is_squared, self.is_var, self.is_std = (
            st.sem(f"ln_{x}") for x in ("centred", "squared", "var", "std"))

    def vector(self, ch, h, chunk, x, out):
        nc, st, dve = self.nc, self.st, ch.eng
        row = lambda t: t[:, :, None].to_broadcast([NP, NC, D])
        ch.link(nc.vector.tensor_reduce(self.total[h][:, :], x, AX.X, ALU.add))
        ch.link(nc.vector.tensor_scalar(self.total[h][:, :], self.total[h][:, :], -1.0 / D, None, ALU.mult))
        nc.vector.tensor_tensor(self.centred[h][:, :, :], x, row(self.total[h]), ALU.add).then_inc(self.is_centred, 1)
        st.gate(dve, self.is_squared, chunk + 1)
        nc.vector.tensor_reduce(self.var[h][:, :], self.square[h][:, :, :], AX.X, ALU.add).then_inc(self.is_var, 1)
        st.gate(dve, self.is_std, chunk + 1)
        ch.link(nc.vector.reciprocal(self.std[h][:, :], self.std[h][:, :]))
        return nc.vector.scalar_tensor_tensor(out=out, in0=self.centred[h][:, :, :], scalar=0.0,
                                              in1=row(self.std[h]), op0=ALU.max, op1=ALU.mult)

    def scalar(self, act, h, chunk):
        nc, st = self.nc, self.st
        st.gate(act, self.is_centred, chunk + 1)
        nc.scalar.activation(self.square[h][:, :, :], self.centred[h][:, :, :], ACT.Square).then_inc(self.is_squared, 1)
        st.gate(act, self.is_var, chunk + 1)
        nc.scalar.activation(self.std[h][:, :], self.var[h][:, :], ACT.Sqrt, bias=self.eps[:, :],
                             scale=1.0 / D).then_inc(self.is_std, 1)


def node_stage(nc, name, ins, outs, units, at_once, cols, weights, biases, setup):
    st = Stage(nc, name)
    steps = units // at_once
    parts = [(k, n, table, w) for k, (tables, w) in ins.items() for n, table in enumerate(tables)]
    tin = {k: [st.sb(f"in_{k}{h}", [NP, NC, w * len(ts)]) for h in (0, 1)] for k, (ts, w) in ins.items()}
    tout = {k: [st.sb(f"out_{k}{h}", [NP, NC, w]) for h in (0, 1)] for k, (_, w) in outs.items()}
    wt = st.sb("weights", [P, cols])
    bias = {k: st.sb(f"bias_{k}", [P, v.shape[0]]) for k, v in biases.items()}
    ident = st.sb("ident", [P, P])
    turned = [st.sb(f"turned{b}", [P, at_once, NP]) for b in (0, 1)]
    pturn = [st.ps(f"turn{b}", [P, 512]) for b in (0, 1)]
    banks = -(-at_once * cols // 512)
    pout = [st.ps(f"product{b}", [P, banks * 512]) for b in (0, 1)]
    zeroed, const, loaded_w, step = (st.sem(x) for x in ("zeroed", "const", "loaded_w", "dve_step"))
    loaded = [st.sem(f"loaded{h}") for h in (0, 1)]
    stored = [st.sem(f"stored{h}") for h in (0, 1)]
    ready, moved, copied, done, used, finished = (
        st.sem(x) for x in ("source_ready", "transposed", "copied", "multiplied", "product_used", "chunk_done"))
    hook = setup(st, tin, tout, bias)
    block = st.block()
    half = CHUNKS // 2
    src = hook["source"]

    def chunk_done(n):
        return (finished, n) if "vector_post" in hook else (used, n * steps)

    @block.gpsimd
    def _(pool):
        pool.memset(wt[:, :], 0.0).then_inc(zeroed, 1)
        if "eps" in hook:
            pool.memset(hook["eps"][:, :], 1e-5).then_inc(zeroed, 1)
        identity(st, pool, ident, const)

    @block.sync
    def _(sync):
        pool_sets = 2 if "eps" in hook else 1
        sync.wait_ge(zeroed, pool_sets)
        for r, c, a in weights:
            sync.dma_start(wt[r:r + a.shape[0], c:c + a.shape[1]], a).then_inc(loaded_w, 16)
        for k, v in biases.items():
            sync.dma_start(bias[k][:, :], broadcast(v, P)).then_inc(loaded_w, 16)

        def load(i, h, first):
            if not first:
                st.gate(sync, *chunk_done(2 * i - 1 + h))
            for k, n, table, w in parts:
                sync.dma_start(tin[k][h][:, :, n * w:(n + 1) * w], by_chunk(table)[:, bass.ds(2 * i + h, 1), :, :]
                               .rearrange("p c j w -> p (c j) w")).then_inc(loaded[h], 16)

        def body(i, first, last):
            for h in (0, 1):
                load(i, h, first)
        halves(sync, half, body)

    @block.scalar
    def _(act):
        act.wait_ge(zeroed, 2 if "eps" in hook else 1)

        def copies(i, h, first, last):
            for s in range(steps):
                n = (2 * i + h) * steps + s
                b = (h * steps + s) % 2
                st.gate(act, moved, n + 1)
                if not (first and h * steps + s < 2):
                    st.gate(act, done, n - 1)
                nc.scalar.activation(turned[b][:, :, :], pturn[b][:, 0:at_once * NP].rearrange("p (u n) -> p u n", n=NP),
                                     ACT.Copy).then_inc(copied, 1)

        def store(i, h):
            st.gate(act, *chunk_done(2 * i + h + 1))
            for k, (table, w) in outs.items():
                act.dma_start(by_chunk(table)[:, bass.ds(2 * i + h, 1), :, :].rearrange("p c j w -> p (c j) w"),
                              tout[k][h][:, :, :]).then_inc(stored[h], 16)

        def body(i, first, last):
            for h in (0, 1):
                if "act_pre" in hook:
                    hook["act_pre"](act, i, h)
                copies(i, h, first, last)
                if "act_post" in hook:
                    hook["act_post"](act, i, h)
                store(i, h)
        halves(act, half, body)
        for h in (0, 1):
            act.wait_ge(stored[h], 16 * len(outs) * half)

    @block.tensor
    def _(pe):
        pe.wait_ge(const, 2)
        pe.wait_ge(loaded_w, 16 * (len(weights) + len(biases)))

        def turn(i, h, s, first):
            n = (2 * i + h) * steps + s
            b = (h * steps + s) % 2
            if s == 0:
                if ready is not None and "vector_pre" in hook:
                    st.gate(pe, ready, 2 * i + h + 1)
                else:
                    st.gate(pe, loaded[h], (i + 1) * 16 * len(parts))
            if not (first and h * steps + s < 2):
                st.gate(pe, copied, n - 1)
            for u in range(at_once):
                ins_ = nc.tensor.transpose(pturn[b][:, u * NP:(u + 1) * NP], src(h, s * at_once + u), ident[0:NP, 0:NP])
            ins_.then_inc(moved, 1)

        def multiply(i, h, s, first):
            n = (2 * i + h) * steps + s
            b = (h * steps + s) % 2
            st.gate(pe, copied, n + 1)
            if not (first and h * steps + s < 2):
                st.gate(pe, used, n - 1)
            for u in range(at_once):
                ins_ = nc.tensor.matmul(pout[b][0:NP, u * cols:(u + 1) * cols], turned[b][:, u, :], wt[:, :],
                                        start=True, stop=True)
            ins_.then_inc(done, 1)

        def body(i, first, last):
            for h in (0, 1):
                turn(i, h, 0, first)
                for s in range(steps):
                    if s + 1 < steps:
                        turn(i, h, s + 1, first)
                    multiply(i, h, s, first)
        halves(pe, half, body)

    @block.vector
    def _(dve):
        ch = Chain(st, dve, step)
        dve.wait_ge(zeroed, 2 if "eps" in hook else 1)
        dve.wait_ge(loaded_w, 16 * (len(weights) + len(biases)))
        if "vector_start" in hook:
            hook["vector_start"](dve)

        def body(i, first, last):
            ch.n, ch.base = 0, i * body.links
            for h in (0, 1):
                st.gate(dve, loaded[h], (i + 1) * 16 * len(parts))
                if not first:
                    st.gate(dve, stored[h], i * 16 * len(outs))
                if "vector_pre" in hook:
                    hook["vector_pre"](ch, i, h).then_inc(ready, 1)
                for s in range(steps):
                    n = (2 * i + h) * steps + s
                    b = (h * steps + s) % 2
                    st.gate(dve, done, n + 1)
                    hook["vector_step"](ch, i, h, s, pout[b][0:NP, 0:at_once * cols]).then_inc(used, 1)
                if "vector_post" in hook:
                    st.gate(dve, used, (2 * i + h + 1) * steps)
                    hook["vector_post"](ch, i, h).then_inc(finished, 1)
            body.links = ch.n
        body.links = 0
        halves(dve, half, body)
    st.close()


def projection_stage(nc, name, ins, p_table, q_table, w_msg, w_skip, b_skip, per_unit, normed):
    width = P // per_unit

    def setup(st, tin, tout, bias):
        hid = [st.sb(f"hidden{h}", [NP, NC, width]) for h in (0, 1)]
        flat = [t[:, :, :].rearrange("p j w -> p (j w)") for t in hid]
        at_once = 4 if normed else 2
        hook = {"source": lambda h, u: flat[h][:, u * P:(u + 1) * P]}
        if normed:
            ln = Norm(st, nc)
            hook["eps"] = ln.eps
            hook["act_pre"] = lambda act, i, h: ln.scalar(act, h, 2 * i + h)
            hook["vector_pre"] = lambda ch, i, h: ln.vector(ch, h, 2 * i + h, tin["x"][h][:, :, :], hid[h][:, :, :])
        else:
            def pre(ch, i, h):
                ch.link(nc.vector.tensor_tensor(hid[h][:, :, :], tin["agg"][h][:, :, :], tin["q"][h][:, :, :], ALU.add))
                return nc.vector.tensor_scalar(hid[h][:, :, :], hid[h][:, :, :], 0.0, None, ALU.max)
            hook["vector_pre"] = pre

        def step(ch, i, h, s, prod):
            m = at_once * per_unit
            o = prod.rearrange("p (j w) -> p j w", w=32)
            nc.vector.tensor_copy(tout["p"][h][:, s * m:(s + 1) * m, :], o[:, :, 0:16])
            return nc.vector.tensor_tensor(tout["q"][h][:, s * m:(s + 1) * m, :], o[:, :, 16:32],
                                           bias["skip"][0:NP, None, :].to_broadcast([NP, m, 16]), ALU.add)
        hook["vector_step"] = step
        return hook

    weights = [(k * width, k * 32 + c, a) for k in range(per_unit) for c, a in ((0, w_msg), (16, w_skip))]
    node_stage(nc, name, ins, {"p": (p_table, 16), "q": (q_table, 16)}, NC // per_unit, 4 if normed else 2,
               32 * per_unit, weights, {"skip": b_skip}, setup)


def lin3_stage(nc, x, agg, q, w_lin3, b_lin3, x1, h1):
    def setup(st, tin, tout, bias):
        ln = Norm(st, nc)
        hid = [st.sb(f"hidden{h}", [NP, NC, 16]) for h in (0, 1)]
        flat = [t[:, :, :].rearrange("p j w -> p (j w)") for t in hid]

        def pre(ch, i, h):
            ch.link(nc.vector.tensor_tensor(tout["x1"][h][:, :, :], tin["x"][h][:, :, :],
                                            bias["lin3"][0:NP, None, :].to_broadcast([NP, NC, D]), ALU.add))
            return nc.vector.tensor_tensor(hid[h][:, :, :], tin["agg"][h][:, :, :], tin["q"][h][:, :, :], ALU.add)

        def step(ch, i, h, s, prod):
            part = tout["x1"][h][:, :, :].rearrange("p j w -> p (j w)")
            return nc.vector.tensor_tensor(part, part, prod, ALU.add)

        return {"source": lambda h, u: flat[h][:, u * P:(u + 1) * P], "eps": ln.eps, "vector_pre": pre,
                "vector_step": step,
                "act_post": lambda act, i, h: ln.scalar(act, h, 2 * i + h),
                "vector_post": lambda ch, i, h: ln.vector(ch, h, 2 * i + h, tout["x1"][h][:, :, :], tout["h1"][h][:, :, :])}

    node_stage(nc, "lin3", {"x": ([x], D), "agg": ([agg], 16), "q": ([q], 16)}, {"x1": (x1, D), "h1": (h1, D)}, 2, 2, 512,
               [(16 * k, D * k, w_lin3) for k in range(8)], {"lin3": b_lin3}, setup)


KEY, PREV, LAST, OWN, OTHER, WEIGHT, WEIGHT2, META = range(8)


def order_stage(nc, name, table, key, other, meta, zeroed_tables, degree=None):
    st = Stage(nc, name)
    keys, nxt, oth = (st.sb(n, [P, TILES], I32) for n in ("keys", "next", "other"))
    m = st.sb("meta", [P, META, TILES])
    mi = m[:, :, :].bitcast(U32)
    nextf, same, bumped = (st.sb(n, [P, TILES]) for n in ("next_f", "same", "bumped"))
    lastp = st.sb("last_partition", [P, 1])
    zero = st.sb("zero", [P, 4096])
    loaded, zeroed, set_, step, made, written = (
        st.sem(n) for n in ("loaded", "zeroed", "set", "step", "made", "written"))
    if degree is not None:
        key_a, nxt_a = st.sb("key_a", [P, TILES], I32), st.sb("next_a", [P, TILES], I32)
        after, deg, start, before = st.sb("after", [P, TILES]), st.sb("deg", [P, TILES]), st.sb("start", [P, 1]), st.sb("before", [1, P + 1])
        ident = st.sb("ident", [P, P])
        prow, pcol = st.ps("prow", [P, P]), st.ps("pcol", [P, P])
        const, ends, turned, counted, set_a = (st.sem(n) for n in ("const", "ends", "turned", "counted", "set_a"))
    block = st.block()
    rows = table[0:EP, :].rearrange("(t p) w -> p t w", p=P)
    zero_dmas = []
    for z in zeroed_tables:
        flat = z.rearrange("n w -> (n w)")
        size, at = flat.shape[0], 0
        while at < size:
            part = min(size - at, P * 4096) if size - at >= P else size - at
            lanes = P if part % P == 0 else 125
            assert part % lanes == 0
            zero_dmas.append((flat[at:at + part].rearrange("(p n) -> p n", p=lanes), lanes, part // lanes))
            at += part

    @block.gpsimd
    def _(pool):
        pool.memset(zero[:, :], 0.0).then_inc(zeroed, 1)
        pool.memset(lastp[:, :], 1.0).then_inc(zeroed, 1)
        pool.wait_ge(zeroed, 2)
        pool.affine_select(out=lastp[:, :], in_=lastp[:, :], compare_op=ALU.is_ge, fill=0.0, base=-(P - 1),
                           pattern=[[0, 1]], channel_multiplier=1).then_inc(zeroed, 1)
        if degree is not None:
            pool.iota(after[:, :], pattern=[[1, TILES]], base=1, channel_multiplier=TILES,
                      allow_small_or_imprecise_dtypes=True).then_inc(zeroed, 1)
            pool.memset(nxt_a[:, :], PAD).then_inc(set_a, 1)
            identity(st, pool, ident, const)

    @block.sync
    def _(sync):
        sync.wait_ge(set_, 1)
        with nc.allow_non_contiguous_dma("one word of each record"):
            sync.dma_start(keys[:, :], rows[:, :, key].bitcast(I32)).then_inc(loaded, 16)
            sync.dma_start(oth[:, :], rows[:, :, other].bitcast(I32)).then_inc(loaded, 16)
            sync.dma_start(nxt[0:P - 1, :], rows[1:P, :, key].bitcast(I32)).then_inc(loaded, 16)
            sync.dma_start(nxt[P - 1:P, 0:TILES - 1], rows[0:1, 1:TILES, key].bitcast(I32)).then_inc(loaded, 16)
            sync.dma_start(m[:, WEIGHT, :], rows[:, :, WGT]).then_inc(loaded, 16)
            if degree is not None:
                sync.wait_ge(set_a, 1)
                rows_a = table[0:EP, :].rearrange("(p t) w -> p t w", p=P)
                sync.dma_start(key_a[:, :], rows_a[:, :, key].bitcast(I32)).then_inc(loaded, 16)
                rows_n = table[1:EP, :].rearrange("(a n) w -> a n w", a=1)
                sync.dma_start(nxt_a[0:P - 1, :], table[1:1 + (P - 1) * TILES, :].rearrange("(p t) w -> p t w", p=P - 1)[:, :, key].bitcast(I32)).then_inc(loaded, 16)
                sync.dma_start(nxt_a[P - 1:P, 0:TILES - 1], rows_n[:, (P - 1) * TILES:, key].bitcast(I32)).then_inc(loaded, 16)
        sync.wait_ge(zeroed, 3)
        for to, lanes, n in zero_dmas:
            sync.dma_start(to, zero[0:lanes, 0:n]).then_inc(written, 16)
        sync.wait_ge(made, 1)
        sync.dma_start(meta, m[:, :, :]).then_inc(written, 16)
        if degree is not None:
            sync.wait_ge(counted, 1)
            sync.dma_start(degree.rearrange("(p t) -> p t", p=P), deg[:, :]).then_inc(written, 16)
        sync.wait_ge(written, 16 * (len(zero_dmas) + (1 if degree is None else 2)))

    if degree is not None:
        @block.tensor
        def _(pe):
            pe.wait_ge(const, 2)
            pe.wait_ge(ends, 1)
            nc.tensor.transpose(prow[0:1, 0:P], deg[:, TILES - 1:TILES], ident[:, :]).then_inc(turned, 1)
            pe.wait_ge(ends, 2)
            nc.tensor.transpose(pcol[:, 0:1], before[0:1, 0:P], ident[0:1, 0:1]).then_inc(turned, 1)

    @block.vector
    def _(dve):
        ch = Chain(st, dve, step)
        nc.vector.memset(nxt[:, :], PAD).then_inc(set_, 1)
        dve.wait_ge(loaded, 16 * (5 if degree is None else 8))
        dve.wait_ge(zeroed, 3 if degree is None else 4)
        ch.link(nc.vector.tensor_copy(m[:, KEY, :], keys[:, :]))
        ch.link(nc.vector.tensor_copy(nextf[:, :], nxt[:, :]))
        ch.link(nc.vector.tensor_tensor(same[:, :], m[:, KEY, :], nextf[:, :], ALU.is_equal))
        ch.link(nc.vector.scalar_tensor_tensor(out=bumped[:, :], in0=same[:, :], scalar=float(NO_ROW),
                                               in1=m[:, KEY, :], op0=ALU.mult, op1=ALU.add))
        ch.link(nc.vector.tensor_copy(mi[:, LAST, :], bumped[:, :]))
        ch.link(nc.vector.tensor_scalar(mi[:, OWN, :], m[:, KEY, :], float(N - 1), None, ALU.min))
        ch.link(nc.vector.tensor_copy(nextf[:, :], oth[:, :]))
        ch.link(nc.vector.tensor_scalar(mi[:, OTHER, :], nextf[:, :], float(N - 1), None, ALU.min))
        ch.link(nc.vector.tensor_scalar(same[:, :], m[:, KEY, :], 1.0, lastp[:, 0:1], ALU.add, ALU.mult))
        ch.link(nc.vector.memset(m[:, PREV, :], -1.0))
        ch.link(nc.vector.memset(m[:, WEIGHT2, :], 0.0))
        nc.vector.tensor_scalar(m[:, PREV, 1:], same[:, 0:TILES - 1], -1.0, None, ALU.add).then_inc(made, 1)
        if degree is None:
            return
        dve.wait_ge(loaded, 16 * 8)
        dve.wait_ge(zeroed, 4)
        ch.link(nc.vector.tensor_copy(nextf[:, :], nxt_a[:, :]))
        ch.link(nc.vector.tensor_copy(bumped[:, :], key_a[:, :]))
        ch.link(nc.vector.tensor_tensor(same[:, :], bumped[:, :], nextf[:, :], ALU.not_equal))
        ch.link(nc.vector.tensor_tensor(same[:, :], same[:, :], after[:, :], ALU.mult))
        nc.vector.tensor_tensor_scan(deg[:, :], same[:, :], same[:, :], 0.0, ALU.max, ALU.max).then_inc(ends, 1)
        dve.wait_ge(turned, 1)
        ch.link(nc.vector.memset(before[:, :], 0.0))
        nc.vector.tensor_tensor_scan(before[0:1, 1:], prow[0:1, 0:P], zero[0:1, 0:P], 0.0, ALU.max, ALU.max).then_inc(ends, 1)
        dve.wait_ge(turned, 2)
        ch.link(nc.vector.tensor_copy(start[:, :], pcol[:, 0:1]))
        ch.link(nc.vector.tensor_scalar(bumped[:, 1:], deg[:, 0:TILES - 1], start[:, 0:1], None, ALU.max))
        ch.link(nc.vector.tensor_copy(bumped[:, 0:1], start[:, :]))
        nc.vector.tensor_tensor(deg[:, :], after[:, :], bumped[:, :], ALU.subtract).then_inc(counted, 1)
    st.close()


def by_group(table, g, lo, hi):
    return table[bass.ds(g * (GROUP * P), GROUP * P), lo:hi].rearrange("(j p) w -> p j w", p=P)


def edge_features_stage(nc, by_dst, w_e1, w_e2, b1, b2, eaw1, eaw2, ea32t):
    st = Stage(nc, "edge_features")
    attr = [st.sb(f"attr{h}", [P, GROUP, 48]) for h in (0, 1)]
    attr16 = [st.sb(f"attr16_{h}", [P, GROUP * 16]) for h in (0, 1)]
    t16 = [st.sb(f"t16_{h}", [GROUP * 16, P]) for h in (0, 1)]
    t32 = [st.sb(f"t32_{h}", [32, GROUP * P]) for h in (0, 1)]
    o1 = [st.sb(f"o1_{h}", [P, GROUP, 16]) for h in (0, 1)]
    o2 = [st.sb(f"o2_{h}", [P, GROUP, 16]) for h in (0, 1)]
    wt = st.sb("weights", [GROUP * 16, GROUP * 32])
    bias = st.sb("bias", [P, 32])
    ident = st.sb("ident", [P, P])
    p16 = st.ps("p16", [P, 512])
    p32 = st.ps("p32", [32, 1024])
    pout = st.ps("pout", [P, 512])
    zeroed, const, loaded_w, packed, turned, copied, multiplied, added = (
        st.sem(n) for n in ("zeroed", "const", "loaded_w", "packed", "turned", "copied", "multiplied", "added"))
    loaded = [st.sem(f"loaded{h}") for h in (0, 1)]
    stored = [st.sem(f"stored{h}") for h in (0, 1)]
    block = st.block()
    half = GROUPS // 2

    @block.gpsimd
    def _(pool):
        pool.memset(wt[:, :], 0.0).then_inc(zeroed, 1)
        identity(st, pool, ident, const)

    @block.sync
    def _(sync):
        sync.wait_ge(zeroed, 1)
        for j in range(GROUP):
            for c, a in ((0, w_e1), (16, w_e2)):
                sync.dma_start(wt[16 * j:16 * j + 16, 32 * j + c:32 * j + c + 16], a).then_inc(loaded_w, 16)
        sync.dma_start(bias[:, 0:16], broadcast(b1, P)).then_inc(loaded_w, 16)
        sync.dma_start(bias[:, 16:32], broadcast(b2, P)).then_inc(loaded_w, 16)

        def body(i, first, last):
            for h in (0, 1):
                if not first:
                    st.gate(sync, turned, 2 * i - 1 + h)
                sync.dma_start(attr[h][:, :, :], by_group(by_dst, 2 * i + h, EA16, EA16 + 48)).then_inc(loaded[h], 16)
        halves(sync, half, body)

    @block.tensor
    def _(pe):
        pe.wait_ge(const, 2)
        pe.wait_ge(loaded_w, 16 * (2 * GROUP + 2))

        def body(i, first, last):
            for h in (0, 1):
                g = 2 * i + h
                st.gate(pe, packed, g + 1)
                if not (first and h == 0):
                    st.gate(pe, copied, g)
                nc.tensor.transpose(p16[0:GROUP * 16, 0:P], attr16[h][:, :], ident[:, :])
                for j in range(GROUP):
                    ins = nc.tensor.transpose(p32[:, j * P:(j + 1) * P], attr[h][:, j, 16:48], ident[:, :])
                ins.then_inc(turned, 1)
                st.gate(pe, copied, g + 1)
                if not (first and h == 0):
                    st.gate(pe, added, g)
                nc.tensor.matmul(pout[:, 0:GROUP * 32], t16[h][:, :], wt[:, :], start=True, stop=True).then_inc(multiplied, 1)
        halves(pe, half, body)

    @block.scalar
    def _(act):
        def body(i, first, last):
            for h in (0, 1):
                g = 2 * i + h
                st.gate(act, turned, g + 1)
                if not first:
                    st.gate(act, multiplied, g - 1)
                    st.gate(act, stored[h], i * 48)
                nc.scalar.activation(t16[h][:, :], p16[0:GROUP * 16, 0:P], ACT.Copy)
                nc.scalar.activation(t32[h][:, :], p32[:, 0:GROUP * P], ACT.Copy).then_inc(copied, 1)
                st.gate(act, copied, g + 1)
                act.dma_start(ea32t[:, bass.ds(g * (GROUP * P), GROUP * P)], t32[h][:, :]).then_inc(stored[h], 16)
                st.gate(act, added, g + 1)
                act.dma_start(by_group(eaw1, g, 0, 16), o1[h][:, :, :]).then_inc(stored[h], 16)
                act.dma_start(by_group(eaw2, g, 0, 16), o2[h][:, :, :]).then_inc(stored[h], 16)
        halves(act, half, body)
        for h in (0, 1):
            act.wait_ge(stored[h], 48 * half)

    @block.vector
    def _(dve):
        dve.wait_ge(loaded_w, 16 * (2 * GROUP + 2))

        def body(i, first, last):
            for h in (0, 1):
                g = 2 * i + h
                st.gate(dve, loaded[h], (i + 1) * 16)
                if not first:
                    st.gate(dve, turned, g - 1)
                    st.gate(dve, stored[h], i * 48)
                nc.vector.tensor_copy(attr16[h][:, :].rearrange("p (j w) -> p j w", w=16), attr[h][:, :, 0:16]).then_inc(packed, 1)
                st.gate(dve, multiplied, g + 1)
                o = pout[:, 0:GROUP * 32].rearrange("p (j w) -> p j w", w=32)
                for c, t in ((0, o1), (16, o2)):
                    ins = nc.vector.tensor_tensor(t[h][:, :, :], o[:, :, c:c + 16],
                                                  bias[:, None, c:c + 16].to_broadcast([P, GROUP, 16]), ALU.add)
                ins.then_inc(added, 1)
        halves(dve, half, body)
    st.close()


def edge_stage(nc, name, meta, gathers, gathered, width, setup, scatter=None, add=False):
    st = Stage(nc, name)
    m = st.sb("meta", [P, META, TILES])
    mi = m[:, :, :].bitcast(U32)
    ident = st.sb("ident", [P, P])
    index = [st.sb(f"index{h}", [P, len(gathers), GROUP], U32) for h in (0, 1)]
    to = [st.sb(f"to{h}", [P, GROUP], U32) for h in (0, 1)]
    keyslot = [st.sb(f"keyslot{h}", [P, GROUP]) for h in (0, 1)]
    rows = [st.sb(f"rows{h}", [P, GROUP, gathered]) for h in (0, 1)]
    values = [st.sb(f"values{h}", [P, GROUP, width]) for h in (0, 1)]
    same = [st.sb(f"same{h}", [P, GROUP, P]) for h in (0, 1)]
    carry = [st.sb(f"carry{h}", [P, GROUP, P]) for h in (0, 1)]
    sums = [st.sb(f"sums{h}", [P, GROUP, width]) for h in (0, 1)]
    pkey = st.ps("pkey", [P, 1024])
    psum = [st.ps(f"psum{b}", [P, 512]) for b in (0, 1)]
    (const, loaded_m, idx_ready, to_ready, key_turned, same_made, values_ready, summed, copied, posted, cleared) = (
        st.sem(n) for n in ("const", "loaded_meta", "index_ready", "to_ready", "key_turned", "same_made",
                            "values_ready", "summed", "sum_copied", "posted", "cleared"))
    got = [st.sem(f"gathered{h}") for h in (0, 1)]
    put = [st.sem(f"scattered{h}") for h in (0, 1)]
    half = GROUPS // 2
    per = 16 * GROUP
    hook = setup(st, dict(m=m, rows=rows, values=values, sums=sums, got=got, values_ready=values_ready,
                          per=per * len(gathers), ident=ident, copied=copied, posted=posted, put=put, put_per=per, half=half))
    prep_loads = hook.get("sync_start")
    block = st.block()

    @block.sync
    def _(sync):
        sync.dma_start(m[:, :, :], meta).then_inc(loaded_m, 16)
        if prep_loads:
            prep_loads(sync)
        if "sync" in hook:
            halves(sync, half, lambda i, first, last: [hook["sync"](sync, i, h, first) for h in (0, 1)])
        if "sync_end" in hook:
            hook["sync_end"](sync)

    @block.gpsimd
    def _(pool):
        identity(st, pool, ident, const)
        pool.memset(sums[1][:, GROUP - 1, :], 0.0).then_inc(cleared, 1)
        if "pool_start" in hook:
            hook["pool_start"](pool)

        def gather(i, h, first):
            g = 2 * i + h
            st.gate(pool, idx_ready, g + 1)
            if not first:
                st.gate(pool, values_ready, g - 1)
            for n, (table, _, at, wd) in enumerate(gathers):
                for j in range(GROUP):
                    pool.indirect_dma_start(rows[h][:, j, at:at + wd], None, table,
                                            bass.IndirectOffsetOnAxis(ap=index[h][:, n, j:j + 1], axis=0)).then_inc(got[h], 16)

        def send(i, h):
            g = 2 * i + h
            st.gate(pool, to_ready, g + 1)
            if add:
                st.gate(pool, posted, g + 1)
            else:
                st.gate(pool, copied, (g + 1) * GROUP)
            for j in range(GROUP):
                at = bass.IndirectOffsetOnAxis(ap=to[h][:, j:j + 1], axis=0)
                if add:
                    pool.indirect_dma_start(scatter, at, hook["sent"][h][:, j, :], None, compute_op=ALU.add).then_inc(put[h], 16)
                else:
                    pool.indirect_dma_start(scatter, at, sums[h][:, j, :], None, bounds_check=N - 1,
                                            oob_is_err=False).then_inc(put[h], 16)

        def body(i, first, last):
            gather(i, 1, first)
            if scatter is not None:
                send(i, 0)
            if not last:
                gather(i + 1, 0, False)
            if scatter is not None:
                send(i, 1)
        gather(0, 0, True)
        halves(pool, half, body)
        if scatter is not None:
            for h in (0, 1):
                pool.wait_ge(put[h], per * half)

    @block.tensor
    def _(pe):
        pe.wait_ge(const, 2)
        pe.wait_ge(cleared, 1)
        if "pe_start" in hook:
            hook["pe_start"](pe)

        def turn_keys(i, h, first):
            g = 2 * i + h
            st.gate(pe, idx_ready, g + 1)
            if not (first and h == 0):
                st.gate(pe, same_made, g)
            for j in range(GROUP):
                ins = nc.tensor.transpose(pkey[:, j * P:(j + 1) * P], keyslot[h][:, j:j + 1].to_broadcast([P, P]), ident[:, :])
            ins.then_inc(key_turned, 1)

        def sum_up(i, h, first):
            g = 2 * i + h
            st.gate(pe, values_ready, g + 1)
            for j in range(GROUP):
                tile = g * GROUP + j
                b = (h * GROUP + j) % 2
                if not (first and h == 0 and j < 2):
                    st.gate(pe, copied, tile - 1)
                nc.tensor.matmul(psum[b][:, 0:width], same[h][:, j, :], values[h][:, j, :], start=True, stop=False)
                if not (first and h == 0 and j == 0):
                    st.gate(pe, copied, tile)
                before = sums[h][:, j - 1, :] if j else sums[1 - h][:, GROUP - 1, :]
                nc.tensor.matmul(psum[b][:, 0:width], carry[h][:, j, :], before, start=False, stop=True).then_inc(summed, 1)

        def body(i, first, last):
            for h in (0, 1):
                if h == 0:
                    turn_keys(i, 1, first)
                elif not last:
                    turn_keys(i + 1, 0, False)
                if "pe" in hook:
                    hook["pe"](pe, i, h, first)
                sum_up(i, h, first)
                if "pe_post" in hook:
                    hook["pe_post"](pe, i, h, first)
        turn_keys(0, 0, True)
        halves(pe, half, body)

    @block.scalar
    def _(act):
        if "act_start" in hook:
            hook["act_start"](act)
        def body(i, first, last):
            for h in (0, 1):
                g = 2 * i + h
                if "act" in hook:
                    hook["act"](act, i, h, first)
                if not first:
                    if scatter is not None and not add:
                        st.gate(act, put[h], i * per)
                    if "post" in hook:
                        st.gate(act, posted, g - 1)
                    if "act_reuse" in hook:
                        hook["act_reuse"](act, i, h)
                elif h == 1:
                    act.wait_ge(cleared, 1)
                for j in range(GROUP):
                    st.gate(act, summed, g * GROUP + j + 1)
                    nc.scalar.activation(sums[h][:, j, :], psum[(h * GROUP + j) % 2][:, 0:width], ACT.Copy).then_inc(copied, 1)
                if "act_post" in hook:
                    hook["act_post"](act, i, h, first)
        halves(act, half, body)

    @block.vector
    def _(dve):
        dve.wait_ge(loaded_m, 16)
        if "vector_start" in hook:
            hook["vector_start"](dve)

        def stage(i, h, first):
            g = 2 * i + h
            if not first:
                st.gate(dve, got[h], i * (per * len(gathers)))
                st.gate(dve, key_turned, g - 1)
            for n, (_, row, _, _) in enumerate(gathers):
                nc.vector.tensor_copy(index[h][:, n, :], mi[:, row, bass.ds(g * GROUP, GROUP)])
            nc.vector.tensor_copy(keyslot[h][:, :], m[:, KEY, bass.ds(g * GROUP, GROUP)]).then_inc(idx_ready, 1)

        def stage_to(i, h, first):
            if not first:
                st.gate(dve, put[h], i * per)
            nc.vector.tensor_copy(to[h][:, :], mi[:, LAST, bass.ds((2 * i + h) * GROUP, GROUP)]).then_inc(to_ready, 1)

        def compare(i, h, first):
            g = 2 * i + h
            st.gate(dve, key_turned, g + 1)
            if not first:
                st.gate(dve, summed, (g - 1) * GROUP)
            turned = pkey[:, 0:GROUP * P].rearrange("p (j e) -> p j e", e=P)
            for row, mat in ((KEY, same), (PREV, carry)):
                ins = nc.vector.tensor_tensor(mat[h][:, :, :], turned,
                                              m[:, row, bass.ds(g * GROUP, GROUP)].unsqueeze(2).to_broadcast([P, GROUP, P]),
                                              ALU.is_equal)
            ins.then_inc(same_made, 1)

        def body(i, first, last):
            for h in (0, 1):
                if h == 0:
                    stage(i, 1, first)
                elif not last:
                    stage(i + 1, 0, False)
                compare(i, h, first)
                hook["values"](dve, i, h, first).then_inc(values_ready, 1)
                if scatter is not None:
                    stage_to(i, h, first)
            if "post" in hook:
                for h in (0, 1):
                    hook["post"](dve, i, h, first).then_inc(posted, 1)
        stage(0, 0, True)
        halves(dve, half, body)
    st.close()


def conv_edges(nc, name, meta, p_table, eaw, agg):
    def setup(st, c):
        feat = [st.sb(f"feat{h}", [P, GROUP, 16]) for h in (0, 1)]
        arrived = [st.sem(f"feat_arrived{h}") for h in (0, 1)]

        def sync(eng, i, h, first):
            if not first:
                st.gate(eng, c["values_ready"], 2 * i - 1 + h)
            eng.dma_start(feat[h][:, :, :], by_group(eaw, 2 * i + h, 0, 16)).then_inc(arrived[h], 16)

        def values(dve, i, h, first):
            st.gate(dve, c["got"][h], (i + 1) * c["per"])
            st.gate(dve, arrived[h], (i + 1) * 16)
            return nc.vector.tensor_tensor(c["values"][h][:, :, :], c["rows"][h][:, :, :], feat[h][:, :, :], ALU.add)
        return {"sync": sync, "values": values}
    edge_stage(nc, name, meta, [(p_table, OTHER, 0, 16)], 16, 16, setup, scatter=agg)


def message_edges(nc, meta, h_table, ea32t, w1t, b1, w2t, b2, agg):
    def setup(st, c):
        w_nodes, w_edge, w_out = st.sb("w_nodes", [P, D]), st.sb("w_edge", [32, D]), st.sb("w_out", [D, D])
        bias1, bias2 = st.sb("bias1", [D, 1]), st.sb("bias2", [P, D])
        attr = [st.sb(f"attr{h}", [32, GROUP * P]) for h in (0, 1)]
        ht = st.sb("rows_t", [P, GROUP * P])
        zt = st.sb("hidden_turned", [D, GROUP * P])
        pt = st.ps("turn", [P, 1024])
        pm = st.ps("message", [P, 512])
        arrived = [st.sem(f"attr_arrived{h}") for h in (0, 1)]
        loaded_w, turned, moved, hidden, rectified, done = (
            st.sem(n) for n in ("loaded_w", "rows_turned", "rows_copied", "hidden_done", "rectified", "message_done"))
        cuts = ((0, 512), (512, GROUP * P))

        def sync_start(eng):
            eng.dma_start(w_nodes[:, :], w1t[0:P, :]).then_inc(loaded_w, 16)
            eng.dma_start(w_edge[:, :], w1t[P:P + 32, :]).then_inc(loaded_w, 16)
            eng.dma_start(w_out[:, :], w2t).then_inc(loaded_w, 16)
            eng.dma_start(bias1[:, :], b1.rearrange("(n a) -> n a", a=1)).then_inc(loaded_w, 16)
            eng.dma_start(bias2[:, :], broadcast(b2, P)).then_inc(loaded_w, 16)

        def sync(eng, i, h, first):
            if not first:
                st.gate(eng, hidden, 2 * i - 1 + h)
            eng.dma_start(attr[h][:, :], ea32t[:, bass.ds((2 * i + h) * (GROUP * P), GROUP * P)]).then_inc(arrived[h], 16)

        def pe(eng, i, h, first):
            g, start = 2 * i + h, first and h == 0
            st.gate(eng, c["got"][h], (i + 1) * c["per"])
            if not start:
                st.gate(eng, rectified, g)
            for j in range(GROUP):
                ins = nc.tensor.transpose(pt[:, j * P:(j + 1) * P], c["rows"][h][:, j, :], c["ident"][:, :])
            ins.then_inc(turned, 1)
            st.gate(eng, moved, g + 1)
            st.gate(eng, arrived[h], (i + 1) * 16)
            for a, b in cuts:
                nc.tensor.matmul(pt[0:D, a:b], w_nodes[:, :], ht[:, a:b], start=True, stop=False)
                ins = nc.tensor.matmul(pt[0:D, a:b], w_edge[:, :], attr[h][:, a:b], start=False, stop=True)
            ins.then_inc(hidden, 1)
            st.gate(eng, rectified, g + 1)
            if not start:
                st.gate(eng, c["values_ready"], g)
            for j in range(GROUP):
                ins = nc.tensor.matmul(pm[:, j * D:(j + 1) * D], zt[:, j * P:(j + 1) * P], w_out[:, :], start=True, stop=True)
            ins.then_inc(done, 1)

        def act(eng, i, h, first):
            g = 2 * i + h
            st.gate(eng, turned, g + 1)
            for a, b in cuts:
                ins = nc.scalar.activation(ht[:, a:b], pt[:, a:b], ACT.Copy)
            ins.then_inc(moved, 1)
            st.gate(eng, hidden, g + 1)
            if not (first and h == 0):
                st.gate(eng, done, g)
            for a, b in cuts:
                ins = nc.scalar.activation(zt[:, a:b], pt[0:D, a:b], ACT.Relu, bias=bias1[:, :])
            ins.then_inc(rectified, 1)

        def values(eng, i, h, first):
            st.gate(eng, done, 2 * i + h + 1)
            return nc.vector.tensor_tensor(c["values"][h][:, :, :], pm[:, 0:GROUP * D].rearrange("p (j w) -> p j w", w=D),
                                           bias2[:, None, :].to_broadcast([P, GROUP, D]), ALU.add)
        wait_w = lambda eng: eng.wait_ge(loaded_w, 16 * 5)
        return {"sync_start": sync_start, "sync": sync, "pe": pe, "pe_start": wait_w, "act_start": wait_w,
                "act": act, "vector_start": wait_w, "values": values}
    edge_stage(nc, "messages", meta, [(h_table, OTHER, 0, D), (h_table, OWN, D, D)], P, D, setup, scatter=agg)


def gru_stage(nc, x1, h1, agg, w_iht, w_hht, b_ih, b_hh, x2, h2):
    def setup(st, tin, tout, bias):
        ln = Norm(st, nc)
        gates = [st.sb(f"gates{h}", [NP, NC, 4 * D]) for h in (0, 1)]
        new = [st.sb(f"new{h}", [NP, NC, D]) for h in (0, 1)]
        mix = [st.sb(f"mix{h}", [NP, NC, D]) for h in (0, 1)]
        both = st.sb("bias_both", [NP, 4 * D])
        opened, pre, tanhed, bstep, stepped = (st.sem(n) for n in ("gates_open", "new_before", "new_done", "bias_step", "steps_seen"))

        def vector_start(dve):
            ch = Chain(st, dve, bstep)
            ch.link(nc.vector.tensor_tensor(both[:, 0:2 * D], bias["ih"][0:NP, 0:2 * D], bias["hh"][0:NP, 0:2 * D], ALU.add))
            ch.link(nc.vector.tensor_copy(both[:, 2 * D:3 * D], bias["ih"][0:NP, 2 * D:3 * D]))
            ch.link(nc.vector.tensor_copy(both[:, 3 * D:4 * D], bias["hh"][0:NP, 2 * D:3 * D]))

        def step(ch, i, h, s, prod):
            return nc.vector.tensor_tensor(gates[h][:, 4 * s:4 * s + 4, :], prod.rearrange("p (u w) -> p u w", u=4),
                                           both[:, None, :].to_broadcast([NP, 4, 4 * D]), ALU.add)

        def act_post(act, i, h):
            chunk = 2 * i + h
            st.gate(act, stepped, chunk + 1)
            nc.scalar.activation(gates[h][:, :, 0:2 * D], gates[h][:, :, 0:2 * D], ACT.Sigmoid).then_inc(opened, 1)
            st.gate(act, pre, chunk + 1)
            nc.scalar.activation(new[h][:, :, :], new[h][:, :, :], ACT.Tanh).then_inc(tanhed, 1)
            ln.scalar(act, h, chunk)

        def post(ch, i, h):
            dve, chunk, g = ch.eng, 2 * i + h, gates[h]
            dve.sem_inc(stepped, 1)
            st.gate(dve, opened, chunk + 1)
            ch.link(nc.vector.tensor_tensor(new[h][:, :, :], g[:, :, 0:D], g[:, :, 3 * D:4 * D], ALU.mult))
            nc.vector.tensor_tensor(new[h][:, :, :], new[h][:, :, :], g[:, :, 2 * D:3 * D], ALU.add).then_inc(pre, 1)
            st.gate(dve, tanhed, chunk + 1)
            ch.link(nc.vector.tensor_tensor(mix[h][:, :, :], tin["state"][h][:, :, 0:D], new[h][:, :, :], ALU.subtract))
            ch.link(nc.vector.tensor_tensor(mix[h][:, :, :], mix[h][:, :, :], g[:, :, D:2 * D], ALU.mult))
            ch.link(nc.vector.tensor_tensor(mix[h][:, :, :], mix[h][:, :, :], new[h][:, :, :], ALU.add))
            ch.link(nc.vector.tensor_tensor(tout["x2"][h][:, :, :], mix[h][:, :, :], tin["x1"][h][:, :, :], ALU.add))
            return ln.vector(ch, h, chunk, tout["x2"][h][:, :, :], tout["h2"][h][:, :, :])
        return {"source": lambda h, u: tin["state"][h][:, u, :], "eps": ln.eps, "vector_start": vector_start,
                "vector_step": step, "act_post": act_post, "vector_post": post}
    node_stage(nc, "gru", {"state": ([h1, agg], D), "x1": ([x1], D)}, {"x2": (x2, D), "h2": (h2, D)}, NC, 4, 4 * D,
               [(0, 0, w_hht[:, 0:2 * D]), (0, 3 * D, w_hht[:, 2 * D:3 * D]), (D, 0, w_iht)],
               {"ih": b_ih, "hh": b_hh}, setup)


def cheb_weights_stage(nc, w, taylor):
    st = Stage(nc, "cheb_weights")
    terms = w.shape[0]
    wk, v = st.sb("w", [D, terms, D]), st.sb("v", [D, terms, D])
    loaded, step, stored = st.sem("loaded"), st.sem("step"), st.sem("stored")
    block = st.block()

    @block.sync
    def _(sync):
        sync.dma_start(wk[:, :, :], w.rearrange("k i o -> i k o")).then_inc(loaded, 16)
        sync.wait_ge(step, terms * (terms + 1) // 2)
        sync.dma_start(taylor.rearrange("(k i) o -> i k o", i=D), v[:, :, :]).then_inc(stored, 16)
        sync.wait_ge(stored, 16)

    @block.vector
    def _(dve):
        ch = Chain(st, dve, step)
        dve.wait_ge(loaded, 16)
        for j in range(terms):
            for k in range(j, terms):
                c = (-1) ** (k - j) * comb(k, j) / factorial(k)
                if k == j:
                    ch.link(nc.vector.tensor_scalar(v[:, j, :], wk[:, k, :], c, None, ALU.mult))
                else:
                    ch.link(nc.vector.scalar_tensor_tensor(out=v[:, j, :], in0=wk[:, k, :], scalar=c, in1=v[:, j, :],
                                                           op0=ALU.mult, op1=ALU.add))
    st.close()


def cheb_stage(nc, x2, h2, agg, info, w0, bias_, h3, out):
    def setup(st, tin, tout, bias):
        ln = Norm(st, nc)
        flat = [t[:, :, :].rearrange("p j w -> p (j w)") for t in tin["h2"]]
        x3 = [st.sb(f"x3_{h}", [NP, NC, D]) for h in (0, 1)]

        root = [st.sb(f"root{h}", [NP, NC]) for h in (0, 1)]
        clamped, rooted = st.sem("degree_clamped"), st.sem("degree_rooted")

        def act_pre(act, i, h):
            st.gate(act, clamped, 2 * i + h + 1)
            nc.scalar.activation(root[h][:, :], root[h][:, :], ACT.Sqrt).then_inc(rooted, 1)

        def pre(ch, i, h):
            nc.vector.tensor_scalar(root[h][:, :], tin["info"][h][:, :, 1], 1.0, None, ALU.max).then_inc(clamped, 1)
            st.gate(ch.eng, rooted, 2 * i + h + 1)
            ch.link(nc.vector.reciprocal(root[h][:, :], root[h][:, :]))
            ch.link(nc.vector.tensor_tensor(x3[h][:, :, :], tin["agg"][h][:, :, :],
                                            root[h][:, :, None].to_broadcast([NP, NC, D]), ALU.mult))
            ch.link(nc.vector.tensor_tensor(x3[h][:, :, :], x3[h][:, :, :], tin["x2"][h][:, :, :], ALU.add))
            return nc.vector.tensor_tensor(x3[h][:, :, :], x3[h][:, :, :],
                                           bias["cheb"][0:NP, None, :].to_broadcast([NP, NC, D]), ALU.add)

        def step(ch, i, h, s, prod):
            part = x3[h][:, 8 * s:8 * s + 8, :].rearrange("p j w -> p (j w)")
            return nc.vector.tensor_tensor(part, part, prod, ALU.add)

        def post(ch, i, h):
            ch.link(ln.vector(ch, h, 2 * i + h, x3[h][:, :, :], tout["h3"][h][:, :, :]))
            return nc.vector.tensor_tensor(tout["out"][h][:, :, :], x3[h][:, :, :], tout["h3"][h][:, :, :], ALU.add)
        return {"source": lambda h, u: flat[h][:, u * P:(u + 1) * P], "eps": ln.eps, "vector_pre": pre, "vector_step": step,
                "act_pre": act_pre, "act_post": lambda act, i, h: ln.scalar(act, h, 2 * i + h), "vector_post": post}
    node_stage(nc, "cheb", {"h2": ([h2], D), "x2": ([x2], D), "agg": ([agg], D), "info": ([info], 2)}, {"h3": (h3, D), "out": (out, D)},
               NC // 2, 4, 2 * D, [(0, 0, w0), (D, D, w0)], {"cheb": bias_}, setup)


CHEB_K = 10
SUBSTEPS, SERIES = 4, 20
EXPM_K = SUBSTEPS * SERIES
assert CHEB_K % 2 == 0 and EXPM_K % 2 == 0

LIST = 8
BODY = 2 * GROUP * P
BODIES = EP // BODY
ZERO_ROW = EP


def rounds(st, eng, bodies, body):
    with eng.Fori(0, BODIES) as i:
        with nullcontext() if isinstance(bodies, int) else eng.If(i < bodies):
            body(i)


def link_stage(nc, name, source, degree, info, bodies_in, meta, next_list, bodies_out):
    st = Stage(nc, name)
    first = degree is not None
    m = st.sb("meta", [P, META, TILES])
    mi = m[:, :, :].bitcast(U32)
    nxt, dst, same, low, last, pos, flag, tmp, rank = (
        st.sb(n, [P, TILES]) for n in ("next", "dst", "same", "low", "last", "pos", "flag", "tmp", "rank"))
    pointer, deg, std, npos = (st.sb(n, [P, TILES]) for n in ("pointer", "deg", "std", "npos"))
    at_node, at_dst, at_rank = (st.sb(n, [P, TILES], U32) for n in ("at_node", "at_dst", "at_rank"))
    pair, found = st.sb("pair", [P, TILES, 2]), st.sb("found", [P, TILES, 2])
    rec = st.sb("records", [P, TILES, LIST])
    blank = st.sb("blank", [P, TILES, LIST])
    blank_info = st.sb("blank_info", [NP, N // NP, 2])
    slot_i = [st.sb(f"slot_i{h}", [P, GROUP], U32) for h in (0, 1)]
    slot_r = [st.sb(f"slot_r{h}", [P, GROUP, LIST]) for h in (0, 1)]
    slot_2 = [st.sb(f"slot_2{h}", [P, GROUP, 2]) for h in (0, 1)]
    lastp = st.sb("last_partition", [P, 1])
    below, ones = st.sb("below", [P, P]), st.sb("ones", [P, P])
    starts, counted, total = st.sb("starts", [P, BODIES]), st.sb("counted", [P, BODIES]), st.sb("total", [P, 1])
    bodies_f, bodies_i, given = st.sb("bodies_f", [P, 1]), st.sb("bodies_i", [P, 1], I32), st.sb("given", [1, 1], I32)
    pranks, ptotals = st.ps("ranks", [P, TILES]), st.ps("totals", [P, TILES])
    loaded, const, step, staged, moved, moves, cleared, flagged, ranked, rooted, made, stored, asked, set_ = (
        st.sem(n) for n in ("loaded", "const", "step", "staged", "moved", "moves", "cleared", "flagged", "ranked",
                            "rooted", "made", "stored", "asked", "set"))
    block = st.block()
    n_loads = 2 if first else 8

    def load(sync):
        if first:
            sync.dma_start(m[:, :, :], source).then_inc(loaded, 16)
            sync.dma_start(deg[:, :], degree.rearrange("(t p) -> p t", p=P)).then_inc(loaded, 16)
        else:
            rows = source[0:EP, :].rearrange("(t p) w -> p t w", p=P)
            for to, w in ((m[:, KEY, :], 0), (dst[:, :], 1), (m[:, WEIGHT, :], 2), (m[:, WEIGHT2, :], 3), (pointer[:, :], 4)):
                sync.dma_start(to, rows[:, :, w]).then_inc(loaded, 16)
            sync.dma_start(nxt[0:P - 1, :], rows[1:P, :, 0]).then_inc(loaded, 16)
            sync.dma_start(nxt[P - 1:P, 0:TILES - 1], rows[0:1, 1:TILES, 0]).then_inc(loaded, 16)
            sync.dma_start(given[:, :], bodies_in).then_inc(loaded, 16)

    def fill_and_store(sync):
        sync.dma_start(info.rearrange("(p n) w -> p n w", p=NP), blank_info[:, :, :]).then_inc(cleared, 16)
        if next_list is not None:
            sync.dma_start(next_list.rearrange("(t p) w -> p t w", p=P), blank[:, :, :]).then_inc(cleared, 16)
        sync.wait_ge(made, 1)
        sync.dma_start(meta, m[:, :, :]).then_inc(stored, 16)
        if next_list is not None:
            sync.wait_ge(made, 2)
            sync.dma_start(bodies_out, bodies_i[0:1, :]).then_inc(stored, 16)
        sync.wait_ge(stored, 16 if next_list is None else 32)

    @block.sync
    def _(sync):
        sync.wait_ge(set_, 1)
        with nc.allow_non_contiguous_dma("one word of each record"):
            load(sync)
        sync.wait_ge(const, 9)
        fill_and_store(sync)

    passes = 2 if next_list is None else 3

    @block.gpsimd
    def _(pool):
        pool.memset(lastp[:, :], 1.0).then_inc(const, 1)
        pool.memset(ones[:, :], 1.0).then_inc(const, 1)
        pool.memset(below[:, :], 1.0).then_inc(const, 1)
        pool.memset(blank[:, :, :], 0.0).then_inc(const, 1)
        pool.memset(blank_info[:, :, :], 0.0).then_inc(const, 1)
        pool.iota(pos[:, :], pattern=[[P, TILES]], base=0, channel_multiplier=1,
                  allow_small_or_imprecise_dtypes=True).then_inc(const, 1)
        pool.iota(starts[:, :], pattern=[[BODY, BODIES]], base=0, channel_multiplier=0,
                  allow_small_or_imprecise_dtypes=True).then_inc(const, 1)
        pool.wait_ge(const, 7)
        pool.affine_select(out=below[:, :], in_=below[:, :], compare_op=ALU.is_gt, fill=0.0, base=0,
                           pattern=[[1, P]], channel_multiplier=-1).then_inc(rooted, 1)
        pool.affine_select(out=lastp[:, :], in_=lastp[:, :], compare_op=ALU.is_ge, fill=0.0, base=-(P - 1),
                           pattern=[[0, 1]], channel_multiplier=1).then_inc(rooted, 1)
        pool.memset(blank[:, :, 0:2], float(PAD)).then_inc(rooted, 1)
        pool.memset(blank[:, :, 4:5], float(ZERO_ROW)).then_inc(rooted, 1)
        pool.memset(blank_info[:, :, 0:1], float(ZERO_ROW)).then_inc(rooted, 1)
        pool.wait_ge(rooted, 5)
        pool.sem_inc(const, 2)
        pool.wait_ge(loaded, 16 * n_loads)
        bodies = BODIES if first else pool.value_load(given[0:1, 0:1], min_val=1, max_val=BODIES)
        pool.wait_ge(cleared, 16 if next_list is None else 32)
        for n in range(passes):
            def move(i):
                c = i + bodies * n
                st.gate(pool, staged, c + 1)
                for h in (0, 1):
                    for j in range(GROUP):
                        at = bass.IndirectOffsetOnAxis(ap=slot_i[h][:, j:j + 1], axis=0)
                        if n == 0:
                            pool.indirect_dma_start(info, at, slot_2[h][:, j, :], None, bounds_check=N - 1,
                                                    oob_is_err=False).then_inc(moves, 16)
                        elif n == 1:
                            pool.indirect_dma_start(slot_2[h][:, j, :], None, info, at).then_inc(moves, 16)
                        else:
                            pool.indirect_dma_start(next_list, at, slot_r[h][:, j, :], None, bounds_check=EP - 1,
                                                    oob_is_err=False).then_inc(moves, 16)
                st.gate(pool, moves, (c + 1) * (32 * GROUP))
                pool.sem_inc(moved, 1)
            rounds(st, pool, bodies, move)

    if next_list is not None:
        @block.tensor
        def _(pe):
            pe.wait_ge(rooted, 5)
            pe.wait_ge(flagged, 1)
            nc.tensor.matmul(pranks[:, :], below[:, :], flag[:, :], start=True, stop=True)
            nc.tensor.matmul(ptotals[:, :], ones[:, :], flag[:, :], start=True, stop=True).then_inc(ranked, 1)

    if first:
        @block.scalar
        def _(act):
            act.wait_ge(asked, 1)
            nc.scalar.activation(std[:, :], tmp[:, :], ACT.Sqrt).then_inc(asked, 1)

    @block.vector
    def _(dve):
        ch = Chain(st, dve, step)
        link, v = ch.link, nc.vector
        v.memset(nxt[:, :], float(PAD)).then_inc(set_, 1)
        dve.sem_inc(moved, 1)
        dve.wait_ge(loaded, 16 * n_loads)
        dve.wait_ge(rooted, 5)
        bodies = BODIES if first else dve.value_load(given[0:1, 0:1], min_val=1, max_val=BODIES)
        if first:
            link(v.tensor_copy(tmp[:, :], mi[:, LAST, :]))
            link(v.tensor_scalar(last[:, :], tmp[:, :], float(NO_ROW), None, ALU.is_lt))
            link(v.tensor_copy(dst[:, :], mi[:, OTHER, :]))
        else:
            link(v.tensor_tensor(last[:, :], m[:, KEY, :], nxt[:, :], ALU.not_equal))
            link(v.tensor_scalar(same[:, :], m[:, KEY, :], 1.0, lastp[:, 0:1], ALU.add, ALU.mult))
            link(v.memset(m[:, PREV, 0:1], -1.0))
            link(v.tensor_scalar(m[:, PREV, 1:], same[:, 0:TILES - 1], -1.0, None, ALU.add))
            link(v.memset(deg[:, :], 0.0))
            link(v.tensor_copy(mi[:, OTHER, :], pointer[:, :]))
        link(v.tensor_scalar(low[:, :], m[:, KEY, :], float(N), None, ALU.is_lt))
        link(v.tensor_tensor(last[:, :], last[:, :], low[:, :], ALU.mult))
        link(v.tensor_scalar(npos[:, :], pos[:, :], float(N), None, ALU.add))
        link(v.tensor_tensor(tmp[:, :], m[:, KEY, :], npos[:, :], ALU.subtract))
        link(v.tensor_tensor(tmp[:, :], tmp[:, :], last[:, :], ALU.mult))
        link(v.tensor_tensor(tmp[:, :], tmp[:, :], npos[:, :], ALU.add))
        link(v.tensor_copy(mi[:, LAST, :], tmp[:, :]))
        link(v.tensor_scalar(tmp[:, :], m[:, KEY, :], -float(NO_ROW), None, ALU.add))
        link(v.tensor_tensor(tmp[:, :], tmp[:, :], last[:, :], ALU.mult))
        link(v.tensor_scalar(at_node[:, :], tmp[:, :], float(NO_ROW), None, ALU.add))
        link(v.tensor_scalar(at_dst[:, :], dst[:, :], float(N - 1), None, ALU.min))
        link(v.tensor_copy(pair[:, :, 0], pos[:, :]))
        link(v.tensor_copy(pair[:, :, 1], deg[:, :]))

        def send(index, rows, slots, n):
            def body(i):
                c = i + bodies * n
                st.gate(dve, moved, c + 1)
                for h in (0, 1):
                    g = (2 * i + h) * GROUP
                    ins = v.tensor_copy(slot_i[h][:, :], index[:, bass.ds(g, GROUP)])
                    if rows is not None:
                        ins = v.tensor_copy(slots[h][:, :, :], rows[:, bass.ds(g, GROUP), :])
                ins.then_inc(staged, 1)
                if rows is None:
                    st.gate(dve, moved, c + 2)
                    for h in (0, 1):
                        ins = v.tensor_copy(found[:, bass.ds((2 * i + h) * GROUP, GROUP), :], slot_2[h][:, :, :])
                    ch.n, ch.base = 0, i + after_head
                    link(ins)
            rounds(st, dve, bodies, body)

        send(at_node, pair, slot_2, 0)
        after_head = ch.n
        link(v.memset(found[:, :, 1:2], 0.0))
        link(v.memset(found[:, :, 0:1], float(ZERO_ROW)))
        after_head = ch.n
        send(at_dst, None, None, 1)
        ch.n, ch.base = after_head, bodies
        link(v.tensor_copy(m[:, OWN, :].bitcast(U32), found[:, :, 0]))
        link(v.tensor_scalar(flag[:, :], found[:, :, 0], float(ZERO_ROW), None, ALU.is_lt))
        v.tensor_tensor(flag[:, :], flag[:, :], low[:, :], ALU.mult).then_inc(flagged, 1)
        if first:
            ch.link(v.tensor_scalar(tmp[:, :], found[:, :, 1], 1.0, None, ALU.max))
            dve.sem_inc(asked, 1)
            dve.wait_ge(asked, 2)
            link(v.reciprocal(std[:, :], std[:, :]))
            link(v.tensor_scalar(tmp[:, :], found[:, :, 1], 0.0, None, ALU.is_gt))
            link(v.tensor_tensor(m[:, WEIGHT2, :], std[:, :], tmp[:, :], ALU.mult))
            link(v.tensor_tensor(rec[:, :, 3], m[:, WEIGHT2, :], m[:, WEIGHT2, :], ALU.mult))
        elif next_list is not None:
            link(v.tensor_copy(rec[:, :, 3], m[:, WEIGHT2, :]))
        dve.sem_inc(made, 1)
        if next_list is None:
            return
        link(v.memset(rec[:, :, 5:LIST], 0.0))
        for w, a in ((0, m[:, KEY, :]), (1, dst[:, :]), (2, m[:, WEIGHT, :]), (4, found[:, :, 0])):
            link(v.tensor_copy(rec[:, :, w], a))
        dve.wait_ge(ranked, 1)
        link(v.tensor_tensor_scan(rank[:, :], ptotals[:, :], pos[:, :], 0.0, ALU.add, ALU.bypass))
        link(v.tensor_copy(total[:, :], rank[:, TILES - 1:TILES]))
        link(v.tensor_tensor(rank[:, :], rank[:, :], ptotals[:, :], ALU.subtract))
        link(v.tensor_tensor(rank[:, :], rank[:, :], pranks[:, :], ALU.add))
        link(v.tensor_scalar(rank[:, :], rank[:, :], -float(NO_ROW), None, ALU.add))
        link(v.tensor_tensor(rank[:, :], rank[:, :], flag[:, :], ALU.mult))
        link(v.tensor_scalar(at_rank[:, :], rank[:, :], float(NO_ROW), None, ALU.add))
        link(v.tensor_scalar(counted[:, :], starts[:, :], total[:, 0:1], None, ALU.is_lt))
        link(v.tensor_reduce(bodies_f[:, :], counted[:, :], AX.X, ALU.add))
        link(v.tensor_scalar(bodies_i[:, :], bodies_f[:, :], 1.0, None, ALU.max))
        dve.sem_inc(made, 1)
        send(at_rank, rec, slot_r, 2)
    st.close()


def first_cheb_edges(nc, meta, h_table, taylor, sums_table, target):
    def setup(st, c):
        w1 = st.sb("taylor1", [D, D])
        turned = st.sb("sums_t", [D, GROUP * P])
        sent = [st.sb(f"sent{h}", [P, GROUP, D]) for h in (0, 1)]
        pt, pr = st.ps("turn", [P, 1024]), st.ps("product", [P, 512])
        loaded_w, moved, tcopied, done = (st.sem(n) for n in ("loaded_w", "sums_turned", "turned_copied", "product_done"))
        stored = [st.sem(f"stored{h}") for h in (0, 1)]

        def sync(eng, i, h, first):
            st.gate(eng, c["copied"], (2 * i + h + 1) * GROUP)
            eng.dma_start(by_group(sums_table, 2 * i + h, 0, D), c["sums"][h][:, :, :]).then_inc(stored[h], 16)

        def pe_post(eng, i, h, first):
            g, start = 2 * i + h, first and h == 0
            st.gate(eng, c["copied"], (g + 1) * GROUP)
            if not start:
                st.gate(eng, tcopied, g)
            for j in range(GROUP):
                ins = nc.tensor.transpose(pt[0:D, j * P:(j + 1) * P], c["sums"][h][:, j, :], c["ident"][:, :])
            ins.then_inc(moved, 1)
            st.gate(eng, tcopied, g + 1)
            if not start:
                st.gate(eng, c["posted"], g)
            for j in range(GROUP):
                ins = nc.tensor.matmul(pr[:, j * D:(j + 1) * D], turned[:, j * P:(j + 1) * P], w1[:, :], start=True, stop=True)
            ins.then_inc(done, 1)

        def act_post(eng, i, h, first):
            g = 2 * i + h
            st.gate(eng, moved, g + 1)
            if not (first and h == 0):
                st.gate(eng, done, g)
            nc.scalar.activation(turned[:, :], pt[0:D, 0:GROUP * P], ACT.Copy).then_inc(tcopied, 1)

        def values(eng, i, h, first):
            st.gate(eng, c["got"][h], (i + 1) * c["per"])
            w = c["m"][:, WEIGHT2, bass.ds((2 * i + h) * GROUP, GROUP)].unsqueeze(2).to_broadcast([P, GROUP, D])
            return nc.vector.tensor_tensor(c["values"][h][:, :, :], c["rows"][h][:, :, :], w, ALU.mult)

        def post(eng, i, h, first):
            st.gate(eng, done, 2 * i + h + 1)
            if not first:
                st.gate(eng, c["put"][h], i * c["put_per"])
            return nc.vector.tensor_copy(sent[h][:, :, :], pr[:, 0:GROUP * D].rearrange("p (j w) -> p j w", w=D))

        def sync_end(eng):
            for h in (0, 1):
                eng.wait_ge(stored[h], 16 * c["half"])
        return {"sync_start": lambda eng: eng.dma_start(w1[:, :], taylor[D:2 * D, :]).then_inc(loaded_w, 16),
                "sync": sync, "sync_end": sync_end, "pe_start": lambda eng: eng.wait_ge(loaded_w, 16),
                "pe_post": pe_post, "act_post": act_post,
                "act_reuse": lambda eng, i, h: st.gate(eng, stored[h], i * 16),
                "values": values, "post": post, "sent": sent}
    edge_stage(nc, "cheb_first", meta, [(h_table, OTHER, 0, D)], D, D, setup, scatter=target, add=True)


def rate(nc, dve, st, sem, t_tile, out, inverse, coef):
    ch = Chain(st, dve, sem)
    ch.link(nc.vector.tensor_scalar(out[:, :], t_tile[:, :], 1e-8, -1.0, ALU.max, ALU.mult))
    ch.link(nc.vector.tensor_scalar(coef[:, :], inverse, out[:, 0:1], None, ALU.mult))


def first_expm_edges(nc, meta, h_table, t, factors, terms_table, target):
    def setup(st, c):
        K1 = factors.shape[1]
        sent = [st.sb(f"sent{h}", [P, GROUP, D]) for h in (0, 1)]
        fac, tt, mt, coef = st.sb("factors", [P, K1]), st.sb("t", [P, 1]), st.sb("minus_t", [P, 1]), st.sb("coef", [P, K1])
        loaded_w, cstep = st.sem("loaded_w"), st.sem("coef_step")
        stored = [st.sem(f"stored{h}") for h in (0, 1)]

        def sync_start(eng):
            eng.dma_start(fac[:, :], broadcast(factors[0, :], P)).then_inc(loaded_w, 16)
            eng.dma_start(tt[:, :], broadcast(t, P)).then_inc(loaded_w, 16)

        def vector_start(eng):
            eng.wait_ge(loaded_w, 32)
            rate(nc, eng, st, cstep, tt, mt, fac[:, :], coef)

        def sync(eng, i, h, first):
            st.gate(eng, c["posted"], 2 * i + h + 1)
            eng.dma_start(by_group(terms_table, 2 * i + h, 0, D), sent[h][:, :, :]).then_inc(stored[h], 16)

        def values(eng, i, h, first):
            st.gate(eng, c["got"][h], (i + 1) * c["per"])
            w = c["m"][:, WEIGHT, bass.ds((2 * i + h) * GROUP, GROUP)].unsqueeze(2).to_broadcast([P, GROUP, D])
            return nc.vector.tensor_tensor(c["values"][h][:, :, :], c["rows"][h][:, :, :], w, ALU.mult)

        def post(eng, i, h, first):
            st.gate(eng, c["copied"], (2 * i + h + 1) * GROUP)
            if not first:
                st.gate(eng, c["put"][h], i * c["put_per"])
                st.gate(eng, stored[h], i * 16)
            return nc.vector.tensor_scalar(sent[h][:, :, :], c["sums"][h][:, :, :], coef[:, 1:2], None, ALU.mult)

        def sync_end(eng):
            for h in (0, 1):
                eng.wait_ge(stored[h], 16 * c["half"])
        return {"sync_start": sync_start, "vector_start": vector_start, "sync": sync, "sync_end": sync_end,
                "values": values, "post": post, "sent": sent}
    edge_stage(nc, "expm_first", meta, [(h_table, OTHER, 0, D)], D, D, setup, scatter=target, add=True)


def tier_stage(nc, name, meta, bodies_in, before, tables, level, pairs, target, taylor=None, expm=None):
    st = Stage(nc, name)
    m = st.sb("meta", [P, META, TILES])
    mi = m[:, :, :].bitcast(U32)
    acc = st.sb("acc", [P, TILES, D])
    ident, ones = st.sb("ident", [P, P]), st.sb("ones", [P, P])
    two = lambda n, shape, dt=F32: [st.sb(f"{n}{h}", shape, dt) for h in (0, 1)]
    index, keyslot, rows, values = two("index", [P, GROUP], U32), two("keyslot", [P, GROUP]), two("rows", [P, GROUP, D]), two("values", [P, GROUP, D])
    same, carry, sums = two("same", [P, GROUP, P]), two("carry", [P, GROUP, P]), two("sums", [P, GROUP, D])
    nonzero = st.sb("nonzero", [P, GROUP, D])
    some, any_, flag = st.sb("some", [P, 1]), st.sb("any", [P, 1]), st.sb("flag", [P, 1], I32)
    given = st.sb("given", [1, 1], I32)
    pkey = st.ps("pkey", [P, 1024])
    psum = [st.ps(f"psum{b}", [P, 512]) for b in (0, 1)]
    (const, loaded, staged, got, key_turned, same_made, values_ready, summed, copied, stored, step, cleared, scaled,
     turned_s, tcopied, product, checked, tested, level_ready, sent, put, placed, cstep) = (st.sem(n) for n in (
         "const", "loaded", "staged", "gathered", "key_turned", "same_made", "values_ready", "summed", "sum_copied",
         "stored", "step", "cleared", "scaled", "sums_turned", "turned_copied", "product", "checked", "tested",
         "level_ready", "sent", "put", "placed", "coef_step"))
    placed_free = st.sem("added")
    if taylor is not None:
        v = st.sb("taylor", [D, taylor.shape[0] // D, D])
        turned = st.sb("turned", [D, GROUP * P])
        pt = st.ps("turn", [P, 1024])
        kept = sums
        n_loads = 3
    else:
        t, factors = expm
        K1 = factors.shape[1]
        fac, tt, mt, coef = st.sb("factors", [P, 2 * K1]), st.sb("t", [P, 1]), st.sb("minus_t", [P, 1]), st.sb("coef", [P, K1])
        kept = two("term", [P, GROUP, D])
        n_loads = 5
    pr = st.ps("product", [P, 512])
    weight = WEIGHT2 if taylor is not None else WEIGHT
    block = st.block()
    per = 2 * GROUP * 16

    def levels(eng, run):
        run(0, level, before, tables[0], OTHER)
        if eng is vec[0]:
            eng.sem_inc(level_ready, 1)
        if not pairs:
            return
        with eng.Fori(0, pairs) as q:
            for par in (0, 1):
                n = 2 * q + (1 + par)
                st.gate(eng, level_ready, n)
                on = eng.value_load(flag[0:1, 0:1], min_val=0, max_val=1)
                with eng.If(on > 0):
                    run(n, n + level, tables[par], tables[1 - par], OWN)
                if eng is vec[0]:
                    eng.sem_inc(level_ready, 1)
    vec = [None]

    def count(eng):
        eng.wait_ge(loaded, 16 * n_loads)
        return eng.value_load(given[0:1, 0:1], min_val=1, max_val=BODIES)

    @block.sync
    def _(sync):
        sync.dma_start(m[:, :, :], meta).then_inc(loaded, 16)
        sync.dma_start(given[:, :], bodies_in).then_inc(loaded, 16)
        if taylor is not None:
            sync.dma_start(v[:, :, :], taylor.rearrange("(k i) o -> i k o", i=D)).then_inc(loaded, 16)
        else:
            for n in (0, 1):
                sync.dma_start(fac[:, n * K1:(n + 1) * K1], broadcast(factors[n, :], P)).then_inc(loaded, 16)
            sync.dma_start(tt[:, :], broadcast(t, P)).then_inc(loaded, 16)
        bodies = count(sync)

        def run(n, k, source, into, row):
            def body(i):
                c = n * bodies + i
                for h in (0, 1):
                    if taylor is not None:
                        st.gate(sync, copied, c * (2 * GROUP) + (h + 1) * GROUP)
                    else:
                        st.gate(sync, scaled, c * 2 + (h + 1))
                    sync.dma_start(by_group(into, 2 * i + h, 0, D), kept[h][:, :, :]).then_inc(stored, 16)
            rounds(st, sync, bodies, body)
        levels(sync, run)
        st.gate(sync, stored, bodies * 32)

    @block.gpsimd
    def _(pool):
        pool.memset(sums[1][:, :, :], 0.0).then_inc(cleared, 1)
        pool.memset(ones[:, :], 1.0).then_inc(cleared, 1)
        pool.memset(acc[:, :, :], 0.0).then_inc(cleared, 1)
        pool.memset(some[:, :], 0.0).then_inc(cleared, 1)
        identity(st, pool, ident, const)
        bodies = count(pool)

        def run(n, k, source, into, row):
            def body(i):
                c = n * bodies + i
                st.gate(pool, staged, c + 1)
                for h in (0, 1):
                    for j in range(GROUP):
                        pool.indirect_dma_start(rows[h][:, j, :], None, source,
                                                bass.IndirectOffsetOnAxis(ap=index[h][:, j:j + 1], axis=0)).then_inc(got, 16)
            rounds(st, pool, bodies, body)
        levels(pool, run)

        def add(i):
            st.gate(pool, sent, i + 1)
            for h in (0, 1):
                for j in range(GROUP):
                    pool.indirect_dma_start(target, bass.IndirectOffsetOnAxis(ap=index[h][:, j:j + 1], axis=0),
                                            rows[h][:, j, :], None, compute_op=ALU.add).then_inc(put, 16)
            st.gate(pool, put, (i + 1) * per)
            pool.sem_inc(placed_free, 1)
        rounds(st, pool, bodies, add)

    @block.tensor
    def _(pe):
        pe.wait_ge(const, 2)
        pe.wait_ge(cleared, 4)
        bodies = count(pe)

        def run(n, k, source, into, row):
            def body(i):
                c = n * bodies + i
                st.gate(pe, staged, c + 1)
                for h in (0, 1):
                    if h:
                        st.gate(pe, same_made, c * 2 + 1)
                    for j in range(GROUP):
                        ins = nc.tensor.transpose(pkey[:, j * P:(j + 1) * P], keyslot[h][:, j:j + 1].to_broadcast([P, P]), ident[:, :])
                    ins.then_inc(key_turned, 1)
                for h in (0, 1):
                    st.gate(pe, values_ready, c * 2 + h + 1)
                    for j in range(GROUP):
                        tile = h * GROUP + j
                        if tile >= 2:
                            st.gate(pe, copied, c * (2 * GROUP) + (tile - 1))
                        nc.tensor.matmul(psum[tile % 2][:, 0:D], same[h][:, j, :], values[h][:, j, :], start=True, stop=False)
                        if tile:
                            st.gate(pe, copied, c * (2 * GROUP) + tile)
                        prior = sums[h][:, j - 1, :] if j else sums[1 - h][:, GROUP - 1, :]
                        nc.tensor.matmul(psum[tile % 2][:, 0:D], carry[h][:, j, :], prior, start=False, stop=True).then_inc(summed, 1)
                if taylor is None:
                    return
                for h in (0, 1):
                    st.gate(pe, copied, c * (2 * GROUP) + (h + 1) * GROUP)
                    if h:
                        st.gate(pe, tcopied, c * 2 + 1)
                    for j in range(GROUP):
                        ins = nc.tensor.transpose(pt[0:D, j * P:(j + 1) * P], sums[h][:, j, :], ident[:, :])
                    ins.then_inc(turned_s, 1)
                    st.gate(pe, tcopied, c * 2 + h + 1)
                    if h:
                        st.gate(pe, placed, c * 2 + 1)
                    for j in range(GROUP):
                        ins = nc.tensor.matmul(pr[:, j * D:(j + 1) * D], turned[:, j * P:(j + 1) * P],
                                               v[:, bass.ds(k, 1), :].rearrange("i k o -> i (k o)"), start=True, stop=True)
                    ins.then_inc(product, 1)
            rounds(st, pe, bodies, body)
            st.gate(pe, checked, n + 1)
            nc.tensor.matmul(pr[:, 0:1], ones[:, :], some[:, :], start=True, stop=True).then_inc(tested, 1)
        levels(pe, run)

    @block.scalar
    def _(act):
        act.wait_ge(cleared, 4)
        bodies = count(act)

        def run(n, k, source, into, row):
            def body(i):
                c = n * bodies + i
                for h in (0, 1):
                    for j in range(GROUP):
                        st.gate(act, summed, c * (2 * GROUP) + (h * GROUP + j + 1))
                        nc.scalar.activation(sums[h][:, j, :], psum[(h * GROUP + j) % 2][:, 0:D], ACT.Copy).then_inc(copied, 1)
                if taylor is None:
                    return
                for h in (0, 1):
                    st.gate(act, turned_s, c * 2 + h + 1)
                    if h:
                        st.gate(act, product, c * 2 + 1)
                    nc.scalar.activation(turned[:, :], pt[0:D, 0:GROUP * P], ACT.Copy).then_inc(tcopied, 1)
            rounds(st, act, bodies, body)
        levels(act, run)

    @block.vector
    def _(dve):
        vec[0] = dve
        vx = nc.vector
        dve.wait_ge(cleared, 4)
        bodies = count(dve)
        if taylor is None:
            rate(nc, dve, st, cstep, tt, mt, fac[:, 0:K1], coef)
        steps_body, steps_level = 6, 2

        def run(n, k, source, into, row):
            def chain(i, at):
                return (n * bodies + i) * steps_body + n * steps_level + at

            def body(i):
                c = n * bodies + i
                for h in (0, 1):
                    g = (2 * i + h) * GROUP
                    vx.tensor_copy(index[h][:, :], mi[:, row, bass.ds(g, GROUP)])
                    ins = vx.tensor_copy(keyslot[h][:, :], m[:, KEY, bass.ds(g, GROUP)])
                ins.then_inc(staged, 1)
                for h in (0, 1):
                    st.gate(dve, key_turned, c * 2 + h + 1)
                    turned_k = pkey[:, 0:GROUP * P].rearrange("p (j e) -> p j e", e=P)
                    for r, mat in ((KEY, same), (PREV, carry)):
                        ins = vx.tensor_tensor(mat[h][:, :, :], turned_k,
                                               m[:, r, bass.ds((2 * i + h) * GROUP, GROUP)].unsqueeze(2).to_broadcast([P, GROUP, P]), ALU.is_equal)
                    ins.then_inc(same_made, 1)
                st.gate(dve, got, (c + 1) * per)
                for h in (0, 1):
                    w = m[:, weight, bass.ds((2 * i + h) * GROUP, GROUP)].unsqueeze(2).to_broadcast([P, GROUP, D])
                    vx.tensor_tensor(values[h][:, :, :], rows[h][:, :, :], w, ALU.mult).then_inc(values_ready, 1)
                for h in (0, 1):
                    part = acc[:, bass.ds((2 * i + h) * GROUP, GROUP), :]
                    if taylor is not None:
                        st.gate(dve, product, c * 2 + h + 1)
                        vx.tensor_tensor(part, part, pr[:, 0:GROUP * D].rearrange("p (j w) -> p j w", w=D), ALU.add).then_inc(placed, 1)
                    else:
                        st.gate(dve, copied, c * (2 * GROUP) + (h + 1) * GROUP)
                        vx.tensor_scalar(kept[h][:, :, :], sums[h][:, :, :], coef[:, bass.ds(k, 1)], None, ALU.mult).then_inc(scaled, 1)
                        st.gate(dve, scaled, c * 2 + h + 1)
                        vx.scalar_tensor_tensor(out=part, in0=kept[h][:, :, :], scalar=fac[:, bass.ds(k + K1, 1)], in1=part,
                                                op0=ALU.mult, op1=ALU.add).then_inc(placed, 1)
                    vx.tensor_scalar(nonzero[:, :, :], kept[h][:, :, :], 0.0, None, ALU.not_equal).then_inc(step, 1)
                    st.gate(dve, step, chain(i, 3 * h + 1))
                    vx.tensor_reduce(any_[:, :], nonzero[:, :, :].rearrange("p j w -> p (j w)"), AX.X, ALU.max).then_inc(step, 1)
                    st.gate(dve, step, chain(i, 3 * h + 2))
                    vx.tensor_tensor(some[:, :], some[:, :], any_[:, :], ALU.max).then_inc(step, 1)
                    st.gate(dve, step, chain(i, 3 * h + 3))
                    st.gate(dve, placed, c * 2 + h + 1)
                st.gate(dve, stored, (c + 1) * 32)
            rounds(st, dve, bodies, body)
            dve.sem_inc(checked, 1)
            st.gate(dve, tested, n + 1)
            vx.tensor_scalar(flag[:, :], pr[:, 0:1], 1.0, None, ALU.min).then_inc(step, 1)
            st.gate(dve, step, chain(bodies, 1))
            vx.memset(some[:, :], 0.0).then_inc(step, 1)
            st.gate(dve, step, chain(bodies, 2))
        levels(dve, run)
        dve.sem_inc(placed_free, 1)

        def give(i):
            st.gate(dve, placed_free, i + 1)
            for h in (0, 1):
                g = (2 * i + h) * GROUP
                vx.tensor_copy(index[h][:, :], mi[:, LAST, bass.ds(g, GROUP)])
                ins = vx.tensor_copy(rows[h][:, :, :], acc[:, bass.ds(g, GROUP), :])
            ins.then_inc(sent, 1)
        rounds(st, dve, bodies, give)
    st.close()


def gnn(nc, x, src, dst, ea16, ea32, ew, w, factors, out):
    ctx = ExitStack()
    Stage.psum = ctx.enter_context(nc.psum_tensor("psum", [P, 8 * BANK], F32))
    dram = lambda name, shape: nc.dram_tensor(name, shape, F32, kind="Internal").ap()
    by_dst, half_d = dram("by_dst", [EP, REC]), dram("half_d", [EP, REC])
    by_src, half_s = dram("by_src", [EP, NARROW]), dram("half_s", [EP, NARROW])
    sort_edges(nc, "sort_dst", REC, DST, by_dst, half_d, inputs=(src, dst, ew, ea16, ea32))
    sort_edges(nc, "sort_src", NARROW, SRC, by_src, half_s, table=by_dst)
    p1, q1, p2, q2, agg1, agg2 = (dram(n, [N, 16]) for n in ("p1", "q1", "p2", "q2", "agg1", "agg2"))
    eaw1, eaw2, ea32t = dram("eaw1", [EP, 16]), dram("eaw2", [EP, 16]), dram("ea32t", [32, EP])
    meta_d, meta_s = dram("meta_d", [P, META, TILES]), dram("meta_s", [P, META, TILES])
    x1, h1, agg3 = dram("x1", [N, D]), dram("h1", [N, D]), dram("agg3", [N, D])
    aggc = dram("aggc", [N + EP, D])
    degree, info1 = dram("degree", [EP]), dram("info1", [N, 2])
    infos = [info1] + [dram(f"info{n}", [N, 2]) for n in (2, 3, 4)]
    metas = [dram(f"meta{n}", [P, META, TILES]) for n in (1, 2, 3, 4)]
    lists = [None] + [dram(f"list{n}", [EP, LIST]) for n in (2, 3, 4)]
    counts = [None] + [nc.dram_tensor(f"bodies{n}", [1, 1], I32, kind="Internal").ap() for n in (2, 3, 4)]
    level_sums = [dram(f"sums{n}", [EP + P, D]) for n in (1, 2, 3)]
    turns = [dram(f"turn{n}", [EP + P, D]) for n in (0, 1)]
    order_stage(nc, "order_dst", by_dst, DST, SRC, meta_d, [agg1, agg2, agg3])
    order_stage(nc, "order_src", by_src, SRC, DST, meta_s,
                [aggc, out[N:, :], level_sums[0][EP:, :]] + level_sums[1:] + turns, degree=degree)
    for n in range(4):
        link_stage(nc, f"link{n + 1}", lists[n] if n else meta_s, None if n else degree, infos[n], counts[n], metas[n],
                   lists[n + 1] if n < 3 else None, counts[n + 1] if n < 3 else None)
    edge_features_stage(nc, by_dst, w["L0_gnn_W_msg1"][D:D + 16, :], w["L0_gnn_W_msg2"][16:32, :],
                        w["L0_gnn_b_msg1"], w["L0_gnn_b_msg2"], eaw1, eaw2, ea32t)
    projection_stage(nc, "project1", {"x": ([x], D)}, p1, q1, w["L0_gnn_W_msg1"][0:D, :], w["L0_gnn_W_skip1"],
                     w["L0_gnn_b_skip1"], 2, True)
    conv_edges(nc, "conv1", meta_d, p1, eaw1, agg1)
    projection_stage(nc, "project2", {"agg": ([agg1], 16), "q": ([q1], 16)}, p2, q2, w["L0_gnn_W_msg2"][0:16, :],
                     w["L0_gnn_W_skip2"], w["L0_gnn_b_skip2"], 8, False)
    conv_edges(nc, "conv2", meta_d, p2, eaw2, agg2)
    lin3_stage(nc, x, agg2, q2, w["L0_gnn_W_lin3"], w["L0_gnn_b_lin3"], x1, h1)
    x2, h2, h3 = dram("x2", [N, D]), dram("h2", [N, D]), dram("h3", [N, D])
    taylor = dram("taylor", [w["L2_gnn_W"].shape[0] * D, D])
    message_edges(nc, meta_d, h1, ea32t, w["L1_gnn_W1"], w["L1_gnn_b1"], w["L1_gnn_W2"], w["L1_gnn_b2"], agg3)
    gru_stage(nc, x1, h1, agg3, w["L1_gnn_w_ih"], w["L1_gnn_w_hh"], w["L1_gnn_b_ih"], w["L1_gnn_b_hh"], x2, h2)
    cheb_weights_stage(nc, w["L2_gnn_W"], taylor)
    first_cheb_edges(nc, metas[0], h2, taylor, level_sums[0], aggc)
    for n in (1, 2, 3):
        tier_stage(nc, f"cheb_tier{n + 1}", metas[n], counts[n], level_sums[n - 1], level_sums[n:n + 1] if n < 3 else turns,
                   n + 1, 0 if n < 3 else (CHEB_K - 4) // 2, aggc, taylor=taylor)
    cheb_stage(nc, x2, h2, aggc, info1, taylor[0:D, :], w["L2_gnn_bias"], h3, out)
    first_expm_edges(nc, metas[0], h3, w["L3_gnn_t"], factors, level_sums[0], out)
    for n in (1, 2, 3):
        tier_stage(nc, f"expm_tier{n + 1}", metas[n], counts[n], level_sums[n - 1], level_sums[n:n + 1] if n < 3 else turns,
                   n + 1, 0 if n < 3 else (EXPM_K - 4) // 2, out, expm=(w["L3_gnn_t"], factors))
    ctx.close()


INS = ['x', 'src', 'dst', 'edge_attr_16', 'edge_attr_32', 'edge_weight']
WS = ['L0_gnn_W_msg1', 'L0_gnn_b_msg1', 'L0_gnn_W_skip1', 'L0_gnn_b_skip1', 'L0_gnn_W_msg2', 'L0_gnn_b_msg2', 'L0_gnn_W_skip2', 'L0_gnn_b_skip2', 'L0_gnn_W_lin3', 'L0_gnn_b_lin3', 'L1_gnn_W1', 'L1_gnn_b1', 'L1_gnn_W2', 'L1_gnn_b2', 'L1_gnn_w_ih', 'L1_gnn_w_hh', 'L1_gnn_b_ih', 'L1_gnn_b_hh', 'L2_gnn_W', 'L2_gnn_bias', 'L3_gnn_t']


TURNED = ['L1_gnn_W1', 'L1_gnn_W2', 'L1_gnn_w_ih', 'L1_gnn_w_hh']


def kernel(**inputs):
    import numpy as np
    import concourse.bacc as bacc
    from concourse import mybir as mb
    from concourse.bass_utils import run_bass_kernel_spmd as run

    nc = bacc.Bacc("TRN2", target_bir_lowering=False, num_devices=1)
    arrays, aps = {}, {}
    for name in INS + WS:
        a = np.asarray(inputs[name])
        a = np.ascontiguousarray(a.T if name in TURNED else a)
        arrays[f"in_{name}"] = a
        aps[name] = nc.dram_tensor(f"in_{name}", a.shape, mb.dt.from_np(a.dtype), kind="ExternalInput").ap()
    series = np.array([1.0 / factorial(j) for j in range(SERIES + 1)])
    power = np.ones(1)
    for _ in range(SUBSTEPS):
        power = np.convolve(power, series)
    factors = np.ones((2, EXPM_K + 1), np.float32)
    for k in range(1, EXPM_K + 1):
        factors[0, k] = 1.0 / k
        factors[1, k] = power[k] * float(factorial(k)) / float(SUBSTEPS) ** k
    arrays["in_factors"] = factors
    fac = nc.dram_tensor("in_factors", factors.shape, mb.dt.float32, kind="ExternalInput").ap()
    out = nc.dram_tensor("out_nodes", (N + EP, D), mb.dt.float32, kind="ExternalOutput").ap()
    gnn(nc, *[aps[n] for n in INS], {n: aps[n] for n in WS}, fac, out)
    r = run(nc, [arrays], core_ids=[0])
    return r.results[0]["out_nodes"][0:N]
```

```python
from contextlib import ExitStack, nullcontext
from math import comb, factorial

import concourse.bass as bass
from concourse import mybir

F32 = mybir.dt.float32
I32 = mybir.dt.int32
U32 = mybir.dt.uint32
ALU = mybir.AluOpType
ACT = mybir.ActivationFunctionType
AX = mybir.AxisListType

P = 128
N, D, E = 100000, 64, 25000
TILES = -(-E // P)
EP = TILES * P
PAD = (1 << 17) - 1
DIGITS = [(0, 6), (6, 6), (12, 5)]
GROUP = 7
GROUPS = TILES // GROUP
NO_ROW = 1 << 20
assert N < PAD and GROUPS * GROUP == TILES and GROUPS % 2 == 0

BANK = 512

NP, NC = 125, 16
CHUNKS = N // (NP * NC)
assert CHUNKS % 2 == 0 and CHUNKS * NP * NC == N


class Stage:

    def __init__(self, nc, name):
        self.nc, self.name, self.ctx = nc, name, ExitStack()
        self.sems, self.bank = [], 0
        self.passed = self.sem("wait_passed")

    def sb(self, name, shape, dt=F32):
        return self.ctx.enter_context(self.nc.sbuf_tensor(f"{self.name}_{name}", shape, dt))

    def ps(self, name, shape, dt=F32):
        at = self.bank * BANK
        self.bank += -(-shape[1] // BANK)
        assert self.bank <= 8
        return Stage.psum[0:shape[0], at:at + shape[1]]

    def sem(self, name):
        self.sems.append(self.nc.alloc_semaphore(f"{self.name}_{name}"))
        return self.sems[-1]

    def block(self):
        return self.ctx.enter_context(self.nc.Block())

    def close(self):
        self.ctx.close()
        self.nc.clear_and_free_semaphores(self.sems)
        self.nc.all_engine_barrier()

    def gate(self, eng, sem, value):
        eng.wait_ge(sem, value)
        if not isinstance(value, int):
            eng.sem_inc(self.passed, 1)


class Chain:

    def __init__(self, stage, eng, sem):
        self.stage, self.eng, self.sem, self.n, self.base = stage, eng, sem, 0, 0

    def link(self, ins):
        self.n += 1
        ins.then_inc(self.sem, 1)
        self.stage.gate(self.eng, self.sem, self.base + self.n)


def halves(eng, count, body):
    body(0, True, False)
    with eng.Fori(1, count - 1) as i:
        body(i, False, False)
    body(count - 1, False, True)


def identity(st, eng, tile, sem):
    eng.memset(tile[:, :], 0.0).then_inc(sem, 1)
    eng.wait_ge(sem, 1)
    eng.affine_select(out=tile[:, :], in_=tile[:, :], compare_op=ALU.not_equal, fill=1.0, base=0,
                      pattern=[[-1, P]], channel_multiplier=1).then_inc(sem, 1)


def zero_pieces(*tables):
    pieces = []
    for z in tables:
        flat = z.rearrange("n w -> (n w)")
        size, at = flat.shape[0], 0
        while at < size:
            part = min(size - at, P * 4096)
            lanes = P if part % P == 0 else 125
            assert part % lanes == 0
            pieces.append((flat[at:at + part].rearrange("(p n) -> p n", p=lanes), lanes, part // lanes))
            at += part
    return pieces


def scatter_rows(nc, index, rows, width, table, bound):
    def attach(st):
        slot_i = [st.sb(f"move_i{h}", [P, GROUP], U32) for h in (0, 1)]
        slot_r = [st.sb(f"move_r{h}", [P, GROUP, width]) for h in (0, 1)]
        filled, sent = st.sem("move_filled"), [st.sem(f"move_sent{h}") for h in (0, 1)]

        def run(pool):
            def body(i, first, last):
                for h in (0, 1):
                    if not first:
                        st.gate(pool, sent[h], i * (16 * GROUP))
                    g = (2 * i + h) * GROUP
                    pool.tensor_copy(slot_i[h][:, :], index[:, bass.ds(g, GROUP)])
                    pool.tensor_copy(slot_r[h][:, :, :], rows[:, bass.ds(g, GROUP), :]).then_inc(filled, 1)
                    st.gate(pool, filled, 2 * i + h + 1)
                    for j in range(GROUP):
                        pool.indirect_dma_start(
                            table, bass.IndirectOffsetOnAxis(ap=slot_i[h][:, j:j + 1], axis=0),
                            slot_r[h][:, j, :], None, bounds_check=bound, oob_is_err=False).then_inc(sent[h], 16)
            halves(pool, GROUPS // 2, body)
            for h in (0, 1):
                pool.wait_ge(sent[h], 16 * GROUP * (GROUPS // 2))
        return run
    return attach


def gather_rows(nc, index, found, width, table):
    def attach(st):
        slot_i = [st.sb(f"move_i{h}", [P, GROUP], U32) for h in (0, 1)]
        slot_r = [st.sb(f"move_r{h}", [P, GROUP, width]) for h in (0, 1)]
        filled, got = st.sem("move_filled"), [st.sem(f"move_got{h}") for h in (0, 1)]
        half = GROUPS // 2

        def run(pool):
            def take(i, h):
                st.gate(pool, got[h], (i + 1) * (16 * GROUP))
                pool.tensor_copy(found[:, bass.ds((2 * i + h) * GROUP, GROUP), :], slot_r[h][:, :, :])

            def body(i, first, last):
                for h in (0, 1):
                    if not first:
                        take(i - 1, h)
                    pool.tensor_copy(slot_i[h][:, :], index[:, bass.ds((2 * i + h) * GROUP, GROUP)]).then_inc(filled, 1)
                    st.gate(pool, filled, 2 * i + h + 1)
                    for j in range(GROUP):
                        pool.indirect_dma_start(slot_r[h][:, j, :], None, table,
                                                bass.IndirectOffsetOnAxis(ap=slot_i[h][:, j:j + 1], axis=0)).then_inc(got[h], 16)
            halves(pool, half, body)
            for h in (0, 1):
                take(half - 1, h)
        return run
    return attach


class NextEdge:

    def __init__(self, st, nc):
        self.nc = nc
        self.up, self.wrap = st.sb("shift_up", [P, P]), st.sb("shift_wrap", [P, P])
        self.moved, self.wrapped = st.ps("next_moved", [P, TILES]), st.ps("next_wrapped", [P, TILES])
        self.const, self.done = st.sem("shift_consts"), st.sem("next_done")

    def pool(self, pool):
        for tile in (self.up, self.wrap):
            pool.memset(tile[:, :], 0.0).then_inc(self.const, 1)
        pool.wait_ge(self.const, 2)
        for tile, base in ((self.up, -1), (self.wrap, P - 1)):
            pool.affine_select(out=tile[:, :], in_=tile[:, :], compare_op=ALU.not_equal, fill=1.0, base=base,
                               pattern=[[-1, P]], channel_multiplier=1).then_inc(self.const, 1)

    def tensor(self, pe, value):
        pe.wait_ge(self.const, 4)
        self.nc.tensor.matmul(self.moved[:, :], self.up[:, :], value, start=True, stop=True)
        self.nc.tensor.matmul(self.wrapped[:, :], self.wrap[:, :], value, start=True, stop=True).then_inc(self.done, 1)

    def vector(self, ch, out):
        ch.eng.wait_ge(self.done, 1)
        ch.link(self.nc.vector.tensor_copy(out[:, :], self.moved[:, :]))
        ch.link(self.nc.vector.tensor_tensor(out[:, 0:TILES - 1], out[:, 0:TILES - 1], self.wrapped[:, 1:], ALU.add))


SRC, DST, WGT, EA16, EA32, REC = 0, 1, 2, 3, 19, 52
NARROW = 4


class Sort:

    def __init__(self, nc, name, width, key, ping, pong, inputs):
        self.nc, self.name, self.width, self.key, self.inputs = nc, name, width, key, inputs
        self.ctx = ExitStack()
        self.rec = self.ctx.enter_context(nc.sbuf_tensor(f"{name}_records", [P, TILES, width], F32))
        self.rank_i = self.ctx.enter_context(nc.sbuf_tensor(f"{name}_rank", [P, TILES], U32))
        self.tables = [ping if (len(DIGITS) - 1 - n) % 2 == 0 else pong for n in range(len(DIGITS))]

    def scatter(self, n):
        return scatter_rows(self.nc, self.rank_i, self.rec, self.width, self.tables[n][:, :], EP - 1)

    def ranks(self, n, zeroes):
        nc, rec, rank_i, key = self.nc, self.rec, self.rank_i, self.key
        shift, bits = DIGITS[n]
        bins_n = 1 << bits
        st = Stage(nc, f"{self.name}_ranks{n}")
        onehot = st.sb("onehot", [P, bins_n, TILES])
        count = st.sb("count", [P, bins_n, TILES])
        bins = st.sb("bins", [P, bins_n])
        digit_i = st.sb("digit_i", [P, TILES], I32)
        digit, rank = st.sb("digit", [P, TILES]), st.sb("rank", [P, TILES])
        inbin, base, upto = (st.sb(x, [P, bins_n]) for x in ("inbin", "base", "upto"))
        below, ones = st.sb("below", [P, P]), st.sb("ones", [P, P])
        zero = st.sb("zero", [P, 4096])
        sums = st.ps("sums", [P, 2 * bins_n])
        loaded, blank, consts, step, counted, summed, zeroed, cleared = (
            st.sem(x) for x in ("loaded", "blank", "consts", "step", "counted", "summed", "zeroed", "cleared"))
        rec_key = rec[:, :, key].bitcast(I32)
        full, rest = E // TILES, E % TILES
        wide = self.width == REC
        if n == 0:
            src, dst, weight, ea16, ea32 = self.inputs
            column = st.sb("column", [P, 3, TILES])
        block = st.block()

        @block.sync
        def _(sync):
            if n:
                sync.dma_start(rec[:, :, :], self.tables[n - 1][0:EP, :].rearrange("(p t) w -> p t w", p=P)).then_inc(loaded, 16)
                return
            sync.wait_ge(blank, 3)
            for a, to in ((src.bitcast(F32), column[:, 0, :]), (dst.bitcast(F32), column[:, 1, :]),
                          (weight, column[:, 2, :])):
                sync.dma_start(to[0:full, :], a[0:full * TILES].rearrange("(p t) -> p t", p=full)).then_inc(loaded, 16)
                sync.dma_start(to[full:full + 1, 0:rest], a[full * TILES:E].rearrange("(p t) -> p t", p=1)).then_inc(loaded, 16)
            if wide:
                for a, to in ((ea16, rec[:, :, EA16:EA16 + 16]), (ea32, rec[:, :, EA32:EA32 + 32])):
                    sync.dma_start(to[0:full, :, :], a[0:full * TILES, :].rearrange("(p t) w -> p t w", p=full)).then_inc(loaded, 16)
                    sync.dma_start(to[full:full + 1, 0:rest, :], a[full * TILES:E, :].rearrange("(p t) w -> p t w", p=1)).then_inc(loaded, 16)
        n_loads = 1 if n else 10 if wide else 6

        @block.scalar
        def _(act):
            if zeroes:
                act.wait_ge(zeroed, 1)
                for to, lanes, words in zeroes:
                    act.dma_start(to, zero[0:lanes, 0:words]).then_inc(cleared, 16)
                act.wait_ge(cleared, 16 * len(zeroes))

        @block.gpsimd
        def _(pool):
            if n == 0:
                pool.memset(rec[:, :, :], 0.0).then_inc(blank, 1)
                pool.memset(column[:, 0:2, rest:].bitcast(I32), PAD).then_inc(blank, 1)
                pool.memset(column[:, 2, rest:], 0.0).then_inc(blank, 1)
            pool.iota(bins[:, :], pattern=[[1, bins_n]], base=0, channel_multiplier=0,
                      allow_small_or_imprecise_dtypes=True).then_inc(consts, 1)
            pool.memset(ones[:, :], 1.0).then_inc(consts, 1)
            pool.memset(below[:, :], 1.0).then_inc(consts, 1)
            pool.wait_ge(consts, 3)
            pool.affine_select(out=below[:, :], in_=below[:, :], compare_op=ALU.is_gt, fill=0.0, base=0,
                               pattern=[[1, P]], channel_multiplier=-1).then_inc(consts, 1)
            if zeroes:
                pool.memset(zero[:, :], 0.0).then_inc(zeroed, 1)

        @block.tensor
        def _(pe):
            pe.wait_ge(consts, 4)
            pe.wait_ge(counted, 1)
            nc.tensor.matmul(sums[:, 0:bins_n], below[:, :], inbin[:, :], start=True, stop=True)
            nc.tensor.matmul(sums[:, bins_n:], ones[:, :], inbin[:, :], start=True, stop=True).then_inc(summed, 1)

        @block.vector
        def _(dve):
            link = Chain(st, dve, step).link
            dve.wait_ge(consts, 4)
            dve.wait_ge(loaded, 16 * n_loads)
            if n == 0:
                if not wide:
                    dve.wait_ge(blank, 3)
                for at, c in ((SRC, 0), (DST, 1), (WGT, 2)):
                    link(nc.vector.tensor_copy(rec[:, :, at], column[:, c, :]))
            link(nc.vector.tensor_scalar(digit_i[:, :], rec_key, shift, (1 << bits) - 1,
                                         ALU.logical_shift_right, ALU.bitwise_and))
            link(nc.vector.tensor_copy(digit[:, :], digit_i[:, :]))
            link(nc.vector.tensor_tensor(onehot[:, :, :], digit[:, None, :].to_broadcast([P, bins_n, TILES]),
                                         bins[:, :, None].to_broadcast([P, bins_n, TILES]), ALU.is_equal))
            flat1 = onehot[:, :, :].rearrange("p b t -> p (b t)")
            flat2 = count[:, :, :].rearrange("p b t -> p (b t)")
            link(nc.vector.tensor_tensor_scan(flat2, flat1, flat1, 0.0, ALU.add, ALU.max))
            link(nc.vector.tensor_copy(upto[:, :], count[:, :, TILES - 1]))
            nc.vector.tensor_copy(inbin[:, 0:1], upto[:, 0:1])
            nc.vector.tensor_tensor(inbin[:, 1:], upto[:, 1:], upto[:, 0:bins_n - 1], ALU.subtract).then_inc(counted, 1)
            dve.wait_ge(summed, 1)
            link(nc.vector.tensor_tensor_scan(base[:, :], sums[:, bins_n:], bins[:, :], 0.0, ALU.add, ALU.bypass))
            link(nc.vector.tensor_tensor(base[:, :], base[:, :], sums[:, bins_n:], ALU.subtract))
            link(nc.vector.tensor_tensor(base[:, :], base[:, :], sums[:, 0:bins_n], ALU.add))
            link(nc.vector.tensor_tensor(base[:, 1:], base[:, 1:], upto[:, 0:bins_n - 1], ALU.subtract))
            link(nc.vector.tensor_tensor(count[:, :, :], count[:, :, :],
                                         base[:, :, None].to_broadcast([P, bins_n, TILES]), ALU.add))
            link(nc.vector.tensor_tensor(count[:, :, :], count[:, :, :], onehot[:, :, :], ALU.mult))
            link(nc.vector.tensor_reduce(rank[:, :], count[:, :, :].rearrange("p b t -> p t b"), AX.X, ALU.add))
            link(nc.vector.tensor_scalar(rank_i[:, :], rank[:, :], -1.0, None, ALU.add))
        st.close()

    def close(self):
        self.ctx.close()


def broadcast(vector, partitions):
    return vector.rearrange("(a n) -> a n", a=1).to_broadcast([partitions, vector.shape[0]])


def by_chunk(table):
    return table[0:N, :].rearrange("(p c j) w -> p c j w", p=NP, c=CHUNKS)


class Norm:

    def __init__(self, st, nc):
        self.st, self.nc = st, nc
        self.total = [st.sb(f"ln_total{h}", [NP, NC]) for h in (0, 1)]
        self.var = [st.sb(f"ln_var{h}", [NP, NC]) for h in (0, 1)]
        self.centred = [st.sb(f"ln_centred{h}", [NP, NC, D]) for h in (0, 1)]
        self.square = [st.sb(f"ln_square{h}", [NP, NC, D]) for h in (0, 1)]
        self.eps = st.sb("ln_eps", [NP, 1])
        self.is_centred, self.is_squared, self.is_var, self.is_std = (
            st.sem(f"ln_{x}") for x in ("centred", "squared", "var", "std"))

    def centre(self, ch, h, x):
        nc = self.nc
        ch.link(nc.vector.tensor_reduce(self.total[h][:, :], x, AX.X, ALU.add))
        ch.link(nc.vector.tensor_scalar(self.total[h][:, :], self.total[h][:, :], -1.0 / D, None, ALU.mult))
        return nc.vector.tensor_tensor(self.centred[h][:, :, :], x, per_node(self.total[h]), ALU.add).then_inc(self.is_centred, 1)

    def square_up(self, act, i, h):
        self.st.gate(act, self.is_centred, 2 * i + h + 1)
        self.nc.scalar.activation(self.square[h][:, :, :], self.centred[h][:, :, :], ACT.Square).then_inc(self.is_squared, 1)

    def variance(self, ch, i, h):
        self.st.gate(ch.eng, self.is_squared, 2 * i + h + 1)
        self.nc.vector.tensor_reduce(self.var[h][:, :], self.square[h][:, :, :], AX.X, ALU.add).then_inc(self.is_var, 1)

    def root(self, act, i, h):
        self.st.gate(act, self.is_var, 2 * i + h + 1)
        self.nc.scalar.activation(self.var[h][:, :], self.var[h][:, :], ACT.Sqrt, bias=self.eps[:, :],
                                  scale=1.0 / D).then_inc(self.is_std, 1)

    def finish(self, ch, i, h, out):
        nc = self.nc
        self.st.gate(ch.eng, self.is_std, 2 * i + h + 1)
        ch.link(nc.vector.reciprocal(self.var[h][:, :], self.var[h][:, :]))
        return nc.vector.scalar_tensor_tensor(out=out, in0=self.centred[h][:, :, :], scalar=0.0,
                                              in1=per_node(self.var[h]), op0=ALU.max, op1=ALU.mult)


def per_node(t):
    return t[:, :, None].to_broadcast([NP, NC, D])


def slots(eng, chunks, phases, pair=None):
    half = chunks // 2

    def two(i):
        if pair is not None:
            pair(i)
        for h in (0, 1):
            for lag, f in phases:
                chunk = 2 * i + h - lag if isinstance(i, int) else 0
                back = (h - lag) // 2
                if 0 <= chunk < chunks:
                    f(i - -back if back else i, (h - lag) % 2)
    two(0)
    two(1)
    with eng.Fori(2, half) as i:
        two(i)
    for i in range(half, half + -(-max(lag for lag, _ in phases) // 2)):
        two(i)


def parts_of_chunks(n):
    at = [2 * (k * (CHUNKS // 2) // n) for k in range(n + 1)]
    return [(a, b - a) for a, b in zip(at, at[1:])]


def node_stage(nc, name, part, beside, ins, outs, units, at_once, cols, weights, biases, setup):
    first_chunk, chunks = part
    st = Stage(nc, f"{name}_{first_chunk}")
    steps = units // at_once
    parts = [(k, n, table, w) for k, (tables, w) in ins.items() for n, table in enumerate(tables)]
    tin = {k: [st.sb(f"in_{k}{h}", [NP, NC, w * len(ts)]) for h in (0, 1)] for k, (ts, w) in ins.items()}
    tout = {k: [st.sb(f"out_{k}{h}", [NP, NC, w]) for h in (0, 1)] for k, (_, w) in outs.items()}
    wt = st.sb("weights", [P, cols])
    bias = {k: st.sb(f"bias_{k}", [P, v.shape[0]]) for k, v in biases.items()}
    ident = st.sb("ident", [P, P])
    turned = [st.sb(f"turned{b}", [P, at_once, NP]) for b in (0, 1)]
    pturn = [st.ps(f"turn{b}", [P, 512]) for b in (0, 1)]
    banks = -(-at_once * cols // 512)
    pout = [st.ps(f"product{b}", [P, banks * 512]) for b in (0, 1)]
    zeroed, const, loaded_w, step = (st.sem(x) for x in ("zeroed", "const", "loaded_w", "dve_step"))
    loaded = [st.sem(f"loaded{h}") for h in (0, 1)]
    stored = {k: [st.sem(f"stored_{k}{h}") for h in (0, 1)] for k in outs}
    ready, moved, copied, done, used = (
        st.sem(x) for x in ("source_ready", "transposed", "copied", "multiplied", "product_used"))

    def arrived(eng, i, h):
        st.gate(eng, loaded[h], (i + 1) * (16 * len(parts)))

    def writable(eng, k, i, h):
        if not (isinstance(i, int) and i == 0):
            st.gate(eng, stored[k][h], i * 16)

    def product(s, eng, i, h):
        st.gate(eng, done, (2 * i + h) * steps + (s + 1))
        return pout[(h * steps + s) % 2][0:NP, 0:at_once * cols]

    hook = setup(st, tin=tin, tout=tout, bias=bias, arrived=arrived, writable=writable, product=product, used=used, ready=ready)
    run_beside = beside(st) if beside else None
    block = st.block()
    half = chunks // 2
    src = hook["source"]

    @block.gpsimd
    def _(pool):
        pool.memset(wt[:, :], 0.0).then_inc(zeroed, 1)
        if hook["norm"]:
            pool.memset(hook["norm"].eps[:, :], 1e-5).then_inc(zeroed, 1)
        identity(st, pool, ident, const)
        if run_beside:
            run_beside(pool)

    blanks = 2 if hook["norm"] else 1

    @block.sync
    def _(sync):
        sync.wait_ge(zeroed, blanks)
        for r, c, a in weights:
            sync.dma_start(wt[r:r + a.shape[0], c:c + a.shape[1]], a).then_inc(loaded_w, 16)
        for k, v in biases.items():
            sync.dma_start(bias[k][:, :], broadcast(v, P)).then_inc(loaded_w, 16)

        def load(i, h):
            chunk = 2 * i + h
            if not (isinstance(i, int) and i == 0):
                st.gate(sync, hook["inputs_read"], chunk - 1)
                if hook["turns_inputs"]:
                    st.gate(sync, moved, chunk * steps - steps)
            for k, n, table, w in parts:
                sync.dma_start(tin[k][h][:, :, n * w:(n + 1) * w], by_chunk(table)[:, bass.ds(chunk + first_chunk, 1), :, :]
                               .rearrange("p c j w -> p (c j) w")).then_inc(loaded[h], 16)
        slots(sync, chunks, [(0, load)])

    @block.scalar
    def _(act):
        act.wait_ge(zeroed, blanks)

        def copy(s):
            def f(i, h):
                n = (2 * i + h) * steps + s
                b = (h * steps + s) % 2
                st.gate(act, moved, n + 1)
                if not (isinstance(n, int) and n < 2):
                    st.gate(act, done, n - 1)
                nc.scalar.activation(turned[b][:, :, :], pturn[b][:, 0:at_once * NP].rearrange("p (u n) -> p u n", n=NP),
                                     ACT.Copy).then_inc(copied, 1)
            return f

        def store(k):
            def f(i, h):
                st.gate(act, hook["written"][k][0], 2 * i + h + 1)
                act.dma_start(by_chunk(outs[k][0])[:, bass.ds(2 * i + h + first_chunk, 1), :, :].rearrange("p c j w -> p (c j) w"),
                              tout[k][h][:, :, :]).then_inc(stored[k][h], 16)
            return f
        slots(act, chunks, hook["scalar"](act, [copy(s) for s in range(steps)])
              + [(lag, store(k)) for k, (_, lag) in hook["written"].items()])
        for k in outs:
            for h in (0, 1):
                act.wait_ge(stored[k][h], 16 * half)

    @block.tensor
    def _(pe):
        pe.wait_ge(const, 2)
        pe.wait_ge(loaded_w, 16 * (len(weights) + len(biases)))

        def turn(i, h, s):
            n = (2 * i + h) * steps + s
            b = (h * steps + s) % 2
            if s == 0:
                if hook["turns_inputs"]:
                    arrived(pe, i, h)
                else:
                    st.gate(pe, ready, 2 * i + h + 1)
            if not (isinstance(n, int) and n < 2):
                st.gate(pe, copied, n - 1)
            for u in range(at_once):
                ins_ = nc.tensor.transpose(pturn[b][:, u * NP:(u + 1) * NP], src(h, s * at_once + u), ident[0:NP, 0:NP])
            ins_.then_inc(moved, 1)

        def multiply(i, h, s):
            n = (2 * i + h) * steps + s
            b = (h * steps + s) % 2
            st.gate(pe, copied, n + 1)
            if not (isinstance(n, int) and n < 2):
                st.gate(pe, used, n - 1)
            for u in range(at_once):
                ins_ = nc.tensor.matmul(pout[b][0:NP, u * cols:(u + 1) * cols], turned[b][:, u, :], wt[:, :],
                                        start=True, stop=True)
            ins_.then_inc(done, 1)

        def work(i, h):
            turn(i, h, 0)
            for s in range(steps):
                if s + 1 < steps:
                    turn(i, h, s + 1)
                multiply(i, h, s)
        slots(pe, chunks, [(0, work)])

    @block.vector
    def _(dve):
        ch = Chain(st, dve, step)
        dve.wait_ge(loaded_w, 16 * (len(weights) + len(biases)))
        if "vector_start" in hook:
            hook["vector_start"](dve)
        marks = []

        def pair(i):
            if isinstance(i, int) and i <= 2:
                marks.append(ch.n)
            elif not isinstance(i, int):
                per = ch.n - marks[1]
                ch.n, ch.base = 0, i * per + (marks[1] - per)
                marks[2:] = [per]
            else:
                if i == half:
                    ch.n, ch.base = marks[1] + marks[2] * (half - 1), 0
        slots(dve, chunks, hook["vector"](ch), pair)
    st.close()


def projection_stage(nc, name, part, beside, ins, p_table, q_table, w_msg, w_skip, b_skip, per_unit, normed):
    width = P // per_unit

    def setup(st, tin, tout, bias, arrived, writable, product, used, ready):
        hid = [st.sb(f"hidden{h}", [NP, NC, width]) for h in (0, 1)]
        flat = [t[:, :, :].rearrange("p j w -> p (j w)") for t in hid]
        steps, at_once = (2, 4) if normed else (1, 2)
        put = st.sem("outputs_made")
        ln = Norm(st, nc) if normed else None

        def vector(ch):
            def centre(i, h):
                arrived(ch.eng, i, h)
                ln.centre(ch, h, tin["x"][h][:, :, :])

            def finish(i, h):
                ln.finish(ch, i, h, hid[h][:, :, :]).then_inc(ready, 1)

            def hidden(i, h):
                arrived(ch.eng, i, h)
                ch.link(nc.vector.tensor_tensor(hid[h][:, :, :], tin["agg"][h][:, :, :], tin["q"][h][:, :, :], ALU.add))
                nc.vector.tensor_scalar(hid[h][:, :, :], hid[h][:, :, :], 0.0, None, ALU.max).then_inc(ready, 1)

            def take(i, h):
                m = at_once * per_unit
                for k in ("p", "q"):
                    writable(ch.eng, k, i, h)
                for s in range(steps):
                    o = product(s, ch.eng, i, h).rearrange("p (j w) -> p j w", w=32)
                    nc.vector.tensor_copy(tout["p"][h][:, s * m:(s + 1) * m, :], o[:, :, 0:16])
                    nc.vector.tensor_tensor(tout["q"][h][:, s * m:(s + 1) * m, :], o[:, :, 16:32],
                                            bias["skip"][0:NP, None, :].to_broadcast([NP, m, 16]), ALU.add).then_inc(used, 1)
                st.gate(ch.eng, used, (2 * i + h + 1) * steps)
                ch.eng.sem_inc(put, 1)
            return [(0, centre), (1, finish), (0, lambda i, h: ln.variance(ch, i, h)), (2, take)] if normed else [(0, hidden), (1, take)]

        def scalar(act, copies):
            if normed:
                return ([(0, lambda i, h: ln.square_up(act, i, h))] + [(1, f) for f in copies]
                        + [(0, lambda i, h: ln.root(act, i, h))])
            return [(0, f) for f in copies]
        last = 2 if normed else 1
        return {"source": lambda h, u: flat[h][:, u * P:(u + 1) * P], "norm": ln, "turns_inputs": False, "vector": vector,
                "scalar": scalar, "inputs_read": ln.is_centred if normed else ready, "written": {"p": (put, last), "q": (put, last)}}

    weights = [(k * width, k * 32 + c, a) for k in range(per_unit) for c, a in ((0, w_msg), (16, w_skip))]
    node_stage(nc, name, part, beside, ins, {"p": (p_table, 16), "q": (q_table, 16)}, NC // per_unit, 4 if normed else 2,
               32 * per_unit, weights, {"skip": b_skip}, setup)


def lin3_stage(nc, part, beside, x, agg, q, w_lin3, b_lin3, x1, h1):
    def setup(st, tin, tout, bias, arrived, writable, product, used, ready):
        ln = Norm(st, nc)
        hid = [st.sb(f"hidden{h}", [NP, NC, 16]) for h in (0, 1)]
        before = [st.sb(f"before{h}", [NP, NC, D]) for h in (0, 1)]
        flat = [t[:, :, :].rearrange("p j w -> p (j w)") for t in hid]
        added, ended = st.sem("x_and_bias"), st.sem("h1_made")

        def vector(ch):
            def prepare(i, h):
                arrived(ch.eng, i, h)
                nc.vector.tensor_tensor(hid[h][:, :, :], tin["agg"][h][:, :, :], tin["q"][h][:, :, :], ALU.add).then_inc(ready, 1)
                nc.vector.tensor_tensor(before[h][:, :, :], tin["x"][h][:, :, :],
                                        bias["lin3"][0:NP, None, :].to_broadcast([NP, NC, D]), ALU.add).then_inc(added, 1)

            def add_up(i, h):
                writable(ch.eng, "x1", i, h)
                prod = product(0, ch.eng, i, h)
                st.gate(ch.eng, added, 2 * i + h + 1)
                nc.vector.tensor_tensor(tout["x1"][h][:, :, :].rearrange("p j w -> p (j w)"),
                                        before[h][:, :, :].rearrange("p j w -> p (j w)"), prod, ALU.add).then_inc(used, 1)
                st.gate(ch.eng, used, 2 * i + h + 1)
                ln.centre(ch, h, tout["x1"][h][:, :, :])

            def finish(i, h):
                writable(ch.eng, "h1", i, h)
                ln.finish(ch, i, h, tout["h1"][h][:, :, :]).then_inc(ended, 1)
            return [(0, prepare), (1, add_up), (2, finish), (1, lambda i, h: ln.variance(ch, i, h))]

        return {"source": lambda h, u: flat[h][:, u * P:(u + 1) * P], "norm": ln, "turns_inputs": False, "vector": vector,
                "scalar": lambda act, copies: ([(0, f) for f in copies] + [(1, lambda i, h: ln.square_up(act, i, h)),
                                                                             (1, lambda i, h: ln.root(act, i, h))]),
                "inputs_read": added, "written": {"x1": (used, 1), "h1": (ended, 2)}}

    node_stage(nc, "lin3", part, beside, {"x": ([x], D), "agg": ([agg], 16), "q": ([q], 16)}, {"x1": (x1, D), "h1": (h1, D)}, 2, 2, 512,
               [(16 * k, D * k, w_lin3) for k in range(8)], {"lin3": b_lin3}, setup)


KEY, PREV, LAST, OWN, OTHER, WEIGHT, WEIGHT2, META = range(8)


def order_stage(nc, name, table, key, other, meta, degree=None):
    st = Stage(nc, name)
    words = st.sb("words", [P, TILES, NARROW])
    following = NextEdge(st, nc)
    m = st.sb("meta", [P, META, TILES])
    mi = m[:, :, :].bitcast(U32)
    nextf, same, bumped = (st.sb(n, [P, TILES]) for n in ("next_f", "same", "bumped"))
    lastp = st.sb("last_partition", [P, 1])
    zero = st.sb("zero", [P, P])
    loaded, zeroed, keyed, step, made, written = (
        st.sem(n) for n in ("loaded", "zeroed", "keyed", "step", "made", "written"))
    if degree is not None:
        words_a, key_a = st.sb("words_a", [P, TILES, NARROW]), st.sb("key_a", [P, TILES])
        after, deg, start, before = st.sb("after", [P, TILES]), st.sb("deg", [P, TILES]), st.sb("start", [P, 1]), st.sb("before", [1, P + 1])
        ident = st.sb("ident", [P, P])
        prow, pcol = st.ps("prow", [P, P]), st.ps("pcol", [P, P])
        const, ends, turned, counted, keyed_a = (st.sem(n) for n in ("const", "ends", "turned", "counted", "keyed_a"))
        pnext = st.ps("pnext", [P, 1])
    block = st.block()
    rows = table[0:EP, :].rearrange("(t p) w -> p t w", p=P)

    @block.gpsimd
    def _(pool):
        following.pool(pool)
        pool.memset(zero[:, :], 0.0).then_inc(zeroed, 1)
        pool.memset(lastp[:, :], 1.0).then_inc(zeroed, 1)
        pool.wait_ge(zeroed, 2)
        pool.affine_select(out=lastp[:, :], in_=lastp[:, :], compare_op=ALU.is_ge, fill=0.0, base=-(P - 1),
                           pattern=[[0, 1]], channel_multiplier=1).then_inc(zeroed, 1)
        if degree is not None:
            pool.iota(after[:, :], pattern=[[1, TILES]], base=1, channel_multiplier=TILES,
                      allow_small_or_imprecise_dtypes=True).then_inc(zeroed, 1)
            identity(st, pool, ident, const)

    @block.sync
    def _(sync):
        with nc.allow_non_contiguous_dma("a few words of each record"):
            sync.dma_start(words[:, :, :], rows[:, :, 0:NARROW]).then_inc(loaded, 16)
            if degree is not None:
                sync.dma_start(words_a[:, :, :], table[0:EP, 0:NARROW].rearrange("(p t) w -> p t w", p=P)).then_inc(loaded, 16)
        sync.wait_ge(made, 1)
        sync.dma_start(meta, m[:, :, :]).then_inc(written, 16)
        if degree is not None:
            sync.wait_ge(counted, 1)
            sync.dma_start(degree.rearrange("(p t) -> p t", p=P), deg[:, :]).then_inc(written, 16)
        sync.wait_ge(written, 16 if degree is None else 32)

    @block.tensor
    def _(pe):
        pe.wait_ge(keyed, 1)
        following.tensor(pe, m[:, KEY, :])
        if degree is None:
            return
        pe.wait_ge(const, 2)
        pe.wait_ge(keyed_a, 1)
        nc.tensor.matmul(pnext[:, 0:1], following.up[:, :], key_a[:, 0:1], start=True, stop=True).then_inc(turned, 1)
        pe.wait_ge(ends, 1)
        nc.tensor.transpose(prow[0:1, 0:P], deg[:, TILES - 1:TILES], ident[:, :]).then_inc(turned, 1)
        pe.wait_ge(ends, 2)
        nc.tensor.transpose(pcol[:, 0:1], before[0:1, 0:P], ident[0:1, 0:1]).then_inc(turned, 1)

    @block.vector
    def _(dve):
        ch = Chain(st, dve, step)
        dve.wait_ge(loaded, 16 if degree is None else 32)
        dve.wait_ge(zeroed, 3 if degree is None else 4)
        nc.vector.tensor_copy(m[:, KEY, :], words[:, :, key].bitcast(I32)).then_inc(keyed, 1)
        dve.wait_ge(keyed, 1)
        if degree is not None:
            nc.vector.tensor_copy(key_a[:, :], words_a[:, :, key].bitcast(I32)).then_inc(keyed_a, 1)
        following.vector(ch, nextf)
        ch.link(nc.vector.tensor_tensor(same[:, :], m[:, KEY, :], nextf[:, :], ALU.is_equal))
        ch.link(nc.vector.scalar_tensor_tensor(out=bumped[:, :], in0=same[:, :], scalar=float(NO_ROW),
                                               in1=m[:, KEY, :], op0=ALU.mult, op1=ALU.add))
        ch.link(nc.vector.tensor_copy(mi[:, LAST, :], bumped[:, :]))
        ch.link(nc.vector.tensor_scalar(mi[:, OWN, :], m[:, KEY, :], float(N - 1), None, ALU.min))
        ch.link(nc.vector.tensor_copy(m[:, WEIGHT, :], words[:, :, WGT]))
        ch.link(nc.vector.tensor_copy(nextf[:, :], words[:, :, other].bitcast(I32)))
        ch.link(nc.vector.tensor_scalar(mi[:, OTHER, :], nextf[:, :], float(N - 1), None, ALU.min))
        ch.link(nc.vector.tensor_scalar(same[:, :], m[:, KEY, :], 1.0, lastp[:, 0:1], ALU.add, ALU.mult))
        ch.link(nc.vector.memset(m[:, PREV, :], -1.0))
        ch.link(nc.vector.memset(m[:, WEIGHT2, :], 0.0))
        nc.vector.tensor_scalar(m[:, PREV, 1:], same[:, 0:TILES - 1], -1.0, None, ALU.add).then_inc(made, 1)
        if degree is None:
            return
        dve.wait_ge(turned, 1)
        dve.wait_ge(keyed_a, 1)
        ch.link(nc.vector.tensor_copy(nextf[:, TILES - 1:TILES], pnext[:, 0:1]))
        ch.link(nc.vector.tensor_copy(nextf[:, 0:TILES - 1], key_a[:, 1:]))
        ch.link(nc.vector.tensor_tensor(same[:, :], key_a[:, :], nextf[:, :], ALU.not_equal))
        ch.link(nc.vector.tensor_tensor(same[:, :], same[:, :], after[:, :], ALU.mult))
        nc.vector.tensor_tensor_scan(deg[:, :], same[:, :], same[:, :], 0.0, ALU.max, ALU.max).then_inc(ends, 1)
        dve.wait_ge(turned, 2)
        ch.link(nc.vector.memset(before[:, :], 0.0))
        nc.vector.tensor_tensor_scan(before[0:1, 1:], prow[0:1, 0:P], zero[0:1, 0:P], 0.0, ALU.max, ALU.max).then_inc(ends, 1)
        dve.wait_ge(turned, 3)
        ch.link(nc.vector.tensor_copy(start[:, :], pcol[:, 0:1]))
        ch.link(nc.vector.tensor_scalar(bumped[:, 1:], deg[:, 0:TILES - 1], start[:, 0:1], None, ALU.max))
        ch.link(nc.vector.tensor_copy(bumped[:, 0:1], start[:, :]))
        nc.vector.tensor_tensor(deg[:, :], after[:, :], bumped[:, :], ALU.subtract).then_inc(counted, 1)
    st.close()


def by_group(table, g, lo, hi, group=GROUP):
    return table[bass.ds(g * (group * P), group * P), lo:hi].rearrange("(j p) w -> p j w", p=P)


def edge_features_stage(nc, by_dst, w_e1, w_e2, b1, b2, eaw1, eaw2, ea32t):
    st = Stage(nc, "edge_features")
    attr = [st.sb(f"attr{h}", [P, GROUP, 48]) for h in (0, 1)]
    attr16 = [st.sb(f"attr16_{h}", [P, GROUP * 16]) for h in (0, 1)]
    t16 = [st.sb(f"t16_{h}", [GROUP * 16, P]) for h in (0, 1)]
    t32 = [st.sb(f"t32_{h}", [32, GROUP * P]) for h in (0, 1)]
    o1 = [st.sb(f"o1_{h}", [P, GROUP, 16]) for h in (0, 1)]
    o2 = [st.sb(f"o2_{h}", [P, GROUP, 16]) for h in (0, 1)]
    wt = st.sb("weights", [GROUP * 16, GROUP * 32])
    bias = st.sb("bias", [P, 32])
    ident = st.sb("ident", [P, P])
    p16 = st.ps("p16", [P, 512])
    p32 = st.ps("p32", [32, 1024])
    pout = st.ps("pout", [P, 512])
    zeroed, const, loaded_w, packed, turned, copied, multiplied, added = (
        st.sem(n) for n in ("zeroed", "const", "loaded_w", "packed", "turned", "copied", "multiplied", "added"))
    loaded = [st.sem(f"loaded{h}") for h in (0, 1)]
    stored = [st.sem(f"stored{h}") for h in (0, 1)]
    block = st.block()
    half = GROUPS // 2

    @block.gpsimd
    def _(pool):
        pool.memset(wt[:, :], 0.0).then_inc(zeroed, 1)
        identity(st, pool, ident, const)

    @block.sync
    def _(sync):
        sync.wait_ge(zeroed, 1)
        for j in range(GROUP):
            for c, a in ((0, w_e1), (16, w_e2)):
                sync.dma_start(wt[16 * j:16 * j + 16, 32 * j + c:32 * j + c + 16], a).then_inc(loaded_w, 16)
        sync.dma_start(bias[:, 0:16], broadcast(b1, P)).then_inc(loaded_w, 16)
        sync.dma_start(bias[:, 16:32], broadcast(b2, P)).then_inc(loaded_w, 16)

        def body(i, first, last):
            for h in (0, 1):
                if not first:
                    st.gate(sync, turned, 2 * i - 1 + h)
                sync.dma_start(attr[h][:, :, :], by_group(by_dst, 2 * i + h, EA16, EA16 + 48)).then_inc(loaded[h], 16)
        halves(sync, half, body)

    @block.tensor
    def _(pe):
        pe.wait_ge(const, 2)
        pe.wait_ge(loaded_w, 16 * (2 * GROUP + 2))

        def body(i, first, last):
            for h in (0, 1):
                g = 2 * i + h
                st.gate(pe, packed, g + 1)
                if not (first and h == 0):
                    st.gate(pe, copied, g)
                nc.tensor.transpose(p16[0:GROUP * 16, 0:P], attr16[h][:, :], ident[:, :])
                for j in range(GROUP):
                    ins = nc.tensor.transpose(p32[:, j * P:(j + 1) * P], attr[h][:, j, 16:48], ident[:, :])
                ins.then_inc(turned, 1)
                st.gate(pe, copied, g + 1)
                if not (first and h == 0):
                    st.gate(pe, added, g)
                nc.tensor.matmul(pout[:, 0:GROUP * 32], t16[h][:, :], wt[:, :], start=True, stop=True).then_inc(multiplied, 1)
        halves(pe, half, body)

    @block.scalar
    def _(act):
        def body(i, first, last):
            for h in (0, 1):
                g = 2 * i + h
                st.gate(act, turned, g + 1)
                if not first:
                    st.gate(act, multiplied, g - 1)
                    st.gate(act, stored[h], i * 48)
                nc.scalar.activation(t16[h][:, :], p16[0:GROUP * 16, 0:P], ACT.Copy)
                nc.scalar.activation(t32[h][:, :], p32[:, 0:GROUP * P], ACT.Copy).then_inc(copied, 1)
                st.gate(act, copied, g + 1)
                act.dma_start(ea32t[:, bass.ds(g * (GROUP * P), GROUP * P)], t32[h][:, :]).then_inc(stored[h], 16)
                st.gate(act, added, g + 1)
                act.dma_start(by_group(eaw1, g, 0, 16), o1[h][:, :, :]).then_inc(stored[h], 16)
                act.dma_start(by_group(eaw2, g, 0, 16), o2[h][:, :, :]).then_inc(stored[h], 16)
        halves(act, half, body)
        for h in (0, 1):
            act.wait_ge(stored[h], 48 * half)

    @block.vector
    def _(dve):
        dve.wait_ge(loaded_w, 16 * (2 * GROUP + 2))

        def body(i, first, last):
            for h in (0, 1):
                g = 2 * i + h
                st.gate(dve, loaded[h], (i + 1) * 16)
                if not first:
                    st.gate(dve, turned, g - 1)
                    st.gate(dve, stored[h], i * 48)
                nc.vector.tensor_copy(attr16[h][:, :].rearrange("p (j w) -> p j w", w=16), attr[h][:, :, 0:16]).then_inc(packed, 1)
                st.gate(dve, multiplied, g + 1)
                o = pout[:, 0:GROUP * 32].rearrange("p (j w) -> p j w", w=32)
                for c, t in ((0, o1), (16, o2)):
                    ins = nc.vector.tensor_tensor(t[h][:, :, :], o[:, :, c:c + 16],
                                                  bias[:, None, c:c + 16].to_broadcast([P, GROUP, 16]), ALU.add)
                ins.then_inc(added, 1)
        halves(dve, half, body)
    st.close()


def edge_stage(nc, name, meta, gathers, gathered, width, setup, scatter=None, add=False):
    st = Stage(nc, name)
    m = st.sb("meta", [P, META, TILES])
    mi = m[:, :, :].bitcast(U32)
    ident = st.sb("ident", [P, P])
    index = [st.sb(f"index{h}", [P, len(gathers), GROUP], U32) for h in (0, 1)]
    to = [st.sb(f"to{h}", [P, GROUP], U32) for h in (0, 1)]
    keyslot = [st.sb(f"keyslot{h}", [P, GROUP]) for h in (0, 1)]
    rows = [st.sb(f"rows{h}", [P, GROUP, gathered]) for h in (0, 1)]
    values = [st.sb(f"values{h}", [P, GROUP, width]) for h in (0, 1)]
    same = [st.sb(f"same{h}", [P, GROUP, P]) for h in (0, 1)]
    carry = [st.sb(f"carry{h}", [P, GROUP, P]) for h in (0, 1)]
    sums = [st.sb(f"sums{h}", [P, GROUP, width]) for h in (0, 1)]
    pkey = st.ps("pkey", [P, 1024])
    psum = [st.ps(f"psum{b}", [P, 512]) for b in (0, 1)]
    (const, loaded_m, idx_ready, to_ready, key_turned, same_made, values_ready, summed, copied, posted, cleared) = (
        st.sem(n) for n in ("const", "loaded_meta", "index_ready", "to_ready", "key_turned", "same_made",
                            "values_ready", "summed", "sum_copied", "posted", "cleared"))
    got = [st.sem(f"gathered{h}") for h in (0, 1)]
    put = [st.sem(f"scattered{h}") for h in (0, 1)]
    half = GROUPS // 2
    per = 16 * GROUP
    hook = setup(st, dict(m=m, rows=rows, values=values, sums=sums, got=got, values_ready=values_ready,
                          per=per * len(gathers), ident=ident, copied=copied, posted=posted, put=put, put_per=per, half=half))
    prep_loads = hook.get("sync_start")
    block = st.block()

    @block.sync
    def _(sync):
        sync.dma_start(m[:, :, :], meta).then_inc(loaded_m, 16)
        if prep_loads:
            prep_loads(sync)
        if "sync" in hook:
            halves(sync, half, lambda i, first, last: [hook["sync"](sync, i, h, first) for h in (0, 1)])
        if "sync_end" in hook:
            hook["sync_end"](sync)

    @block.gpsimd
    def _(pool):
        identity(st, pool, ident, const)
        pool.memset(sums[1][:, GROUP - 1, :], 0.0).then_inc(cleared, 1)
        if "pool_start" in hook:
            hook["pool_start"](pool)

        def gather(i, h, first):
            g = 2 * i + h
            st.gate(pool, idx_ready, g + 1)
            if not first:
                st.gate(pool, values_ready, g - 1)
            for n, (table, _, at, wd) in enumerate(gathers):
                for j in range(GROUP):
                    pool.indirect_dma_start(rows[h][:, j, at:at + wd], None, table,
                                            bass.IndirectOffsetOnAxis(ap=index[h][:, n, j:j + 1], axis=0)).then_inc(got[h], 16)

        def send(i, h):
            g = 2 * i + h
            st.gate(pool, to_ready, g + 1)
            if add:
                st.gate(pool, posted, g + 1)
            else:
                st.gate(pool, copied, (g + 1) * GROUP)
            for j in range(GROUP):
                at = bass.IndirectOffsetOnAxis(ap=to[h][:, j:j + 1], axis=0)
                if add:
                    pool.indirect_dma_start(scatter, at, hook["sent"][h][:, j, :], None, compute_op=ALU.add).then_inc(put[h], 16)
                else:
                    pool.indirect_dma_start(scatter, at, sums[h][:, j, :], None, bounds_check=N - 1,
                                            oob_is_err=False).then_inc(put[h], 16)

        def body(i, first, last):
            gather(i, 1, first)
            if scatter is not None:
                send(i, 0)
            if not last:
                gather(i + 1, 0, False)
            if scatter is not None:
                send(i, 1)
        gather(0, 0, True)
        halves(pool, half, body)
        if scatter is not None:
            for h in (0, 1):
                pool.wait_ge(put[h], per * half)

    @block.tensor
    def _(pe):
        pe.wait_ge(const, 2)
        pe.wait_ge(cleared, 1)
        if "pe_start" in hook:
            hook["pe_start"](pe)

        def turn_keys(i, h, first):
            g = 2 * i + h
            st.gate(pe, idx_ready, g + 1)
            if not (first and h == 0):
                st.gate(pe, same_made, g)
            for j in range(GROUP):
                ins = nc.tensor.transpose(pkey[:, j * P:(j + 1) * P], keyslot[h][:, j:j + 1].to_broadcast([P, P]), ident[:, :])
            ins.then_inc(key_turned, 1)

        def sum_up(i, h, first):
            g = 2 * i + h
            st.gate(pe, values_ready, g + 1)
            for j in range(GROUP):
                tile = g * GROUP + j
                b = (h * GROUP + j) % 2
                if not (first and h == 0 and j < 2):
                    st.gate(pe, copied, tile - 1)
                nc.tensor.matmul(psum[b][:, 0:width], same[h][:, j, :], values[h][:, j, :], start=True, stop=False)
                if not (first and h == 0 and j == 0):
                    st.gate(pe, copied, tile)
                before = sums[h][:, j - 1, :] if j else sums[1 - h][:, GROUP - 1, :]
                nc.tensor.matmul(psum[b][:, 0:width], carry[h][:, j, :], before, start=False, stop=True).then_inc(summed, 1)

        def body(i, first, last):
            for h in (0, 1):
                if h == 0:
                    turn_keys(i, 1, first)
                elif not last:
                    turn_keys(i + 1, 0, False)
                if "pe" in hook:
                    hook["pe"](pe, i, h, first)
                sum_up(i, h, first)
                if "pe_post" in hook:
                    hook["pe_post"](pe, i, h, first)
        turn_keys(0, 0, True)
        halves(pe, half, body)

    @block.scalar
    def _(act):
        if "act_start" in hook:
            hook["act_start"](act)
        def body(i, first, last):
            for h in (0, 1):
                g = 2 * i + h
                if "act" in hook:
                    hook["act"](act, i, h, first)
                if not first:
                    if scatter is not None and not add:
                        st.gate(act, put[h], i * per)
                    if "post" in hook:
                        st.gate(act, posted, g - 1)
                    if "act_reuse" in hook:
                        hook["act_reuse"](act, i, h)
                elif h == 1:
                    act.wait_ge(cleared, 1)
                for j in range(GROUP):
                    st.gate(act, summed, g * GROUP + j + 1)
                    nc.scalar.activation(sums[h][:, j, :], psum[(h * GROUP + j) % 2][:, 0:width], ACT.Copy).then_inc(copied, 1)
                if "act_post" in hook:
                    hook["act_post"](act, i, h, first)
        halves(act, half, body)

    @block.vector
    def _(dve):
        dve.wait_ge(loaded_m, 16)
        if "vector_start" in hook:
            hook["vector_start"](dve)

        def stage(i, h, first):
            g = 2 * i + h
            if not first:
                st.gate(dve, got[h], i * (per * len(gathers)))
                st.gate(dve, key_turned, g - 1)
            for n, (_, row, _, _) in enumerate(gathers):
                nc.vector.tensor_copy(index[h][:, n, :], mi[:, row, bass.ds(g * GROUP, GROUP)])
            nc.vector.tensor_copy(keyslot[h][:, :], m[:, KEY, bass.ds(g * GROUP, GROUP)]).then_inc(idx_ready, 1)

        def stage_to(i, h, first):
            if not first:
                st.gate(dve, put[h], i * per)
            nc.vector.tensor_copy(to[h][:, :], mi[:, LAST, bass.ds((2 * i + h) * GROUP, GROUP)]).then_inc(to_ready, 1)

        def compare(i, h, first):
            g = 2 * i + h
            st.gate(dve, key_turned, g + 1)
            if not first:
                st.gate(dve, summed, (g - 1) * GROUP)
            turned = pkey[:, 0:GROUP * P].rearrange("p (j e) -> p j e", e=P)
            for row, mat in ((KEY, same), (PREV, carry)):
                ins = nc.vector.tensor_tensor(mat[h][:, :, :], turned,
                                              m[:, row, bass.ds(g * GROUP, GROUP)].unsqueeze(2).to_broadcast([P, GROUP, P]),
                                              ALU.is_equal)
            ins.then_inc(same_made, 1)

        def body(i, first, last):
            for h in (0, 1):
                if h == 0:
                    stage(i, 1, first)
                elif not last:
                    stage(i + 1, 0, False)
                compare(i, h, first)
                hook["values"](dve, i, h, first).then_inc(values_ready, 1)
                if scatter is not None:
                    stage_to(i, h, first)
            if "post" in hook:
                for h in (0, 1):
                    hook["post"](dve, i, h, first).then_inc(posted, 1)
        stage(0, 0, True)
        halves(dve, half, body)
    st.close()


def conv_edges(nc, name, meta, p_table, eaw, agg):
    def setup(st, c):
        feat = [st.sb(f"feat{h}", [P, GROUP, 16]) for h in (0, 1)]
        arrived = [st.sem(f"feat_arrived{h}") for h in (0, 1)]

        def sync(eng, i, h, first):
            if not first:
                st.gate(eng, c["values_ready"], 2 * i - 1 + h)
            eng.dma_start(feat[h][:, :, :], by_group(eaw, 2 * i + h, 0, 16)).then_inc(arrived[h], 16)

        def values(dve, i, h, first):
            st.gate(dve, c["got"][h], (i + 1) * c["per"])
            st.gate(dve, arrived[h], (i + 1) * 16)
            return nc.vector.tensor_tensor(c["values"][h][:, :, :], c["rows"][h][:, :, :], feat[h][:, :, :], ALU.add)
        return {"sync": sync, "values": values}
    edge_stage(nc, name, meta, [(p_table, OTHER, 0, 16)], 16, 16, setup, scatter=agg)


def message_edges(nc, meta, h_table, ea32t, w1t, b1, w2t, b2, agg):
    def setup(st, c):
        w_nodes, w_edge, w_out = st.sb("w_nodes", [P, D]), st.sb("w_edge", [32, D]), st.sb("w_out", [D, D])
        bias1, bias2 = st.sb("bias1", [D, 1]), st.sb("bias2", [P, D])
        attr = [st.sb(f"attr{h}", [32, GROUP * P]) for h in (0, 1)]
        ht = st.sb("rows_t", [P, GROUP * P])
        zt = st.sb("hidden_turned", [D, GROUP * P])
        pt = st.ps("turn", [P, 1024])
        pm = st.ps("message", [P, 512])
        arrived = [st.sem(f"attr_arrived{h}") for h in (0, 1)]
        loaded_w, turned, moved, hidden, rectified, done = (
            st.sem(n) for n in ("loaded_w", "rows_turned", "rows_copied", "hidden_done", "rectified", "message_done"))
        cuts = ((0, 512), (512, GROUP * P))

        def sync_start(eng):
            eng.dma_start(w_nodes[:, :], w1t[0:P, :]).then_inc(loaded_w, 16)
            eng.dma_start(w_edge[:, :], w1t[P:P + 32, :]).then_inc(loaded_w, 16)
            eng.dma_start(w_out[:, :], w2t).then_inc(loaded_w, 16)
            eng.dma_start(bias1[:, :], b1.rearrange("(n a) -> n a", a=1)).then_inc(loaded_w, 16)
            eng.dma_start(bias2[:, :], broadcast(b2, P)).then_inc(loaded_w, 16)

        def sync(eng, i, h, first):
            if not first:
                st.gate(eng, hidden, 2 * i - 1 + h)
            eng.dma_start(attr[h][:, :], ea32t[:, bass.ds((2 * i + h) * (GROUP * P), GROUP * P)]).then_inc(arrived[h], 16)

        def pe(eng, i, h, first):
            g, start = 2 * i + h, first and h == 0
            st.gate(eng, c["got"][h], (i + 1) * c["per"])
            if not start:
                st.gate(eng, rectified, g)
            for j in range(GROUP):
                ins = nc.tensor.transpose(pt[:, j * P:(j + 1) * P], c["rows"][h][:, j, :], c["ident"][:, :])
            ins.then_inc(turned, 1)
            st.gate(eng, moved, g + 1)
            st.gate(eng, arrived[h], (i + 1) * 16)
            for a, b in cuts:
                nc.tensor.matmul(pt[0:D, a:b], w_nodes[:, :], ht[:, a:b], start=True, stop=False)
                ins = nc.tensor.matmul(pt[0:D, a:b], w_edge[:, :], attr[h][:, a:b], start=False, stop=True)
            ins.then_inc(hidden, 1)
            st.gate(eng, rectified, g + 1)
            if not start:
                st.gate(eng, c["values_ready"], g)
            for j in range(GROUP):
                ins = nc.tensor.matmul(pm[:, j * D:(j + 1) * D], zt[:, j * P:(j + 1) * P], w_out[:, :], start=True, stop=True)
            ins.then_inc(done, 1)

        def act(eng, i, h, first):
            g = 2 * i + h
            st.gate(eng, turned, g + 1)
            for a, b in cuts:
                ins = nc.scalar.activation(ht[:, a:b], pt[:, a:b], ACT.Copy)
            ins.then_inc(moved, 1)
            st.gate(eng, hidden, g + 1)
            if not (first and h == 0):
                st.gate(eng, done, g)
            for a, b in cuts:
                ins = nc.scalar.activation(zt[:, a:b], pt[0:D, a:b], ACT.Relu, bias=bias1[:, :])
            ins.then_inc(rectified, 1)

        def values(eng, i, h, first):
            st.gate(eng, done, 2 * i + h + 1)
            return nc.vector.tensor_tensor(c["values"][h][:, :, :], pm[:, 0:GROUP * D].rearrange("p (j w) -> p j w", w=D),
                                           bias2[:, None, :].to_broadcast([P, GROUP, D]), ALU.add)
        wait_w = lambda eng: eng.wait_ge(loaded_w, 16 * 5)
        return {"sync_start": sync_start, "sync": sync, "pe": pe, "pe_start": wait_w, "act_start": wait_w,
                "act": act, "vector_start": wait_w, "values": values}
    edge_stage(nc, "messages", meta, [(h_table, OTHER, 0, D), (h_table, OWN, D, D)], P, D, setup, scatter=agg)


def gru_stage(nc, part, beside, x1, h1, agg, w_iht, w_hht, b_ih, b_hh, x2, h2):
    def setup(st, tin, tout, bias, arrived, writable, product, used, ready):
        ln = Norm(st, nc)
        gates = [st.sb(f"gates{h}", [NP, NC, 4 * D]) for h in (0, 1)]
        new = [st.sb(f"new{h}", [NP, NC, D]) for h in (0, 1)]
        rest = [st.sb(f"rest{h}", [NP, NC, D]) for h in (0, 1)]
        kept = [st.sb(f"kept{h}", [NP, NC, D]) for h in (0, 1)]
        both = st.sb("bias_both", [NP, 4 * D])
        flipped, opened, pre, tanhed, bstep, read, mixed, ended = (st.sem(n) for n in (
            "z_flipped", "gates_open", "new_before", "new_done", "bias_step", "inputs_read", "x2_made", "h2_made"))

        def vector_start(dve):
            ch = Chain(st, dve, bstep)
            ch.link(nc.vector.tensor_tensor(both[:, 0:2 * D], bias["ih"][0:NP, 0:2 * D], bias["hh"][0:NP, 0:2 * D], ALU.add))
            ch.link(nc.vector.tensor_copy(both[:, 2 * D:3 * D], bias["ih"][0:NP, 2 * D:3 * D]))
            ch.link(nc.vector.tensor_copy(both[:, 3 * D:4 * D], bias["hh"][0:NP, 2 * D:3 * D]))

        def vector(ch):
            def gather_gates(steps):
                def f(i, h):
                    for s in steps:
                        nc.vector.tensor_tensor(gates[h][:, 4 * s:4 * s + 4, :],
                                                product(s, ch.eng, i, h).rearrange("p (u w) -> p u w", u=4),
                                                both[:, None, :].to_broadcast([NP, 4, 4 * D]), ALU.add).then_inc(used, 1)
                return f

            def open_gates(i, h):
                g, chunk = gates[h], 2 * i + h
                arrived(ch.eng, i, h)
                st.gate(ch.eng, opened, chunk + 1)
                ch.link(nc.vector.tensor_tensor(new[h][:, :, :], g[:, :, 0:D], g[:, :, 3 * D:4 * D], ALU.mult))
                nc.vector.tensor_tensor(new[h][:, :, :], new[h][:, :, :], g[:, :, 2 * D:3 * D], ALU.add).then_inc(pre, 1)
                ch.link(nc.vector.tensor_tensor(kept[h][:, :, :], tin["state"][h][:, :, 0:D], g[:, :, D:2 * D], ALU.mult))
                nc.vector.tensor_tensor(kept[h][:, :, :], kept[h][:, :, :], tin["x1"][h][:, :, :], ALU.add).then_inc(read, 1)

            def mix(i, h):
                chunk = 2 * i + h
                writable(ch.eng, "x2", i, h)
                st.gate(ch.eng, tanhed, chunk + 1)
                st.gate(ch.eng, read, chunk + 1)
                ch.link(nc.vector.tensor_tensor(new[h][:, :, :], new[h][:, :, :], rest[h][:, :, :], ALU.mult))
                nc.vector.tensor_tensor(tout["x2"][h][:, :, :], new[h][:, :, :], kept[h][:, :, :], ALU.add).then_inc(mixed, 1)
                st.gate(ch.eng, mixed, chunk + 1)
                ln.centre(ch, h, tout["x2"][h][:, :, :])

            def finish(i, h):
                writable(ch.eng, "h2", i, h)
                ln.finish(ch, i, h, tout["h2"][h][:, :, :]).then_inc(ended, 1)
            return [(1, gather_gates((0, 1))), (2, mix), (1, gather_gates((2, 3))), (2, lambda i, h: ln.variance(ch, i, h)),
                    (1, open_gates), (2, finish)]

        def scalar(act, copies):
            def open_gates(i, h):
                chunk = 2 * i + h
                st.gate(act, used, (chunk + 1) * len(copies))
                nc.scalar.activation(rest[h][:, :, :], gates[h][:, :, D:2 * D], ACT.Sigmoid, scale=-1.0).then_inc(flipped, 1)
                st.gate(act, flipped, chunk + 1)
                nc.scalar.activation(gates[h][:, :, 0:2 * D], gates[h][:, :, 0:2 * D], ACT.Sigmoid).then_inc(opened, 1)

            def tanh(i, h):
                st.gate(act, pre, 2 * i + h + 1)
                nc.scalar.activation(new[h][:, :, :], new[h][:, :, :], ACT.Tanh).then_inc(tanhed, 1)
            return [(1, copies[2]), (1, copies[3]), (2, lambda i, h: ln.square_up(act, i, h)), (1, open_gates),
                    (2, lambda i, h: ln.root(act, i, h)), (0, copies[0]), (0, copies[1]), (1, tanh)]
        return {"source": lambda h, u: tin["state"][h][:, u, :], "norm": ln, "turns_inputs": True, "vector_start": vector_start,
                "vector": vector, "scalar": scalar, "inputs_read": read, "written": {"x2": (mixed, 2), "h2": (ended, 2)}}
    node_stage(nc, "gru", part, beside, {"state": ([h1, agg], D), "x1": ([x1], D)}, {"x2": (x2, D), "h2": (h2, D)}, NC, 4, 4 * D,
               [(0, 0, w_hht[:, 0:2 * D]), (0, 3 * D, w_hht[:, 2 * D:3 * D]), (D, 0, w_iht)],
               {"ih": b_ih, "hh": b_hh}, setup)


def cheb_weights_stage(nc, w, taylor):
    st = Stage(nc, "cheb_weights")
    terms = w.shape[0]
    wk, v = st.sb("w", [D, terms, D]), st.sb("v", [D, terms, D])
    loaded, step, stored = st.sem("loaded"), st.sem("step"), st.sem("stored")
    block = st.block()

    @block.sync
    def _(sync):
        sync.dma_start(wk[:, :, :], w.rearrange("k i o -> i k o")).then_inc(loaded, 16)
        sync.wait_ge(step, terms * (terms + 1) // 2)
        sync.dma_start(taylor.rearrange("(k i) o -> i k o", i=D), v[:, :, :]).then_inc(stored, 16)
        sync.wait_ge(stored, 16)

    @block.vector
    def _(dve):
        ch = Chain(st, dve, step)
        dve.wait_ge(loaded, 16)
        for j in range(terms):
            for k in range(j, terms):
                c = (-1) ** (k - j) * comb(k, j) / factorial(k)
                if k == j:
                    ch.link(nc.vector.tensor_scalar(v[:, j, :], wk[:, k, :], c, None, ALU.mult))
                else:
                    ch.link(nc.vector.scalar_tensor_tensor(out=v[:, j, :], in0=wk[:, k, :], scalar=c, in1=v[:, j, :],
                                                           op0=ALU.mult, op1=ALU.add))
    st.close()


def cheb_stage(nc, x2, h2, agg, info, w0, bias_, h3, out):
    def setup(st, tin, tout, bias, arrived, writable, product, used, ready):
        ln = Norm(st, nc)
        flat = [t[:, :, :].rearrange("p j w -> p (j w)") for t in tin["h2"]]
        part = [st.sb(f"part{h}", [NP, NC, D]) for h in (0, 1)]
        x3 = [st.sb(f"x3_{h}", [NP, NC, D]) for h in (0, 1)]
        root = [st.sb(f"root{h}", [NP, NC]) for h in (0, 1)]
        clamped, rooted = st.sem("degree_clamped"), st.sem("degree_rooted")
        read, ended, made = st.sem("inputs_read"), st.sem("h3_made"), st.sem("out_made")
        steps = 2

        def vector(ch):
            def clamp(i, h):
                arrived(ch.eng, i, h)
                nc.vector.tensor_scalar(root[h][:, :], tin["info"][h][:, :, 1], 1.0, None, ALU.max).then_inc(clamped, 1)

            def prepare(i, h):
                st.gate(ch.eng, rooted, 2 * i + h + 1)
                ch.link(nc.vector.reciprocal(root[h][:, :], root[h][:, :]))
                ch.link(nc.vector.tensor_tensor(part[h][:, :, :], tin["agg"][h][:, :, :], per_node(root[h]), ALU.mult))
                ch.link(nc.vector.tensor_tensor(part[h][:, :, :], part[h][:, :, :], tin["x2"][h][:, :, :], ALU.add))
                nc.vector.tensor_tensor(part[h][:, :, :], part[h][:, :, :],
                                        bias["cheb"][0:NP, None, :].to_broadcast([NP, NC, D]), ALU.add).then_inc(read, 1)

            def add_up(i, h):
                st.gate(ch.eng, read, 2 * i + h + 1)
                if not (isinstance(i, int) and i == 0):
                    st.gate(ch.eng, made, 2 * i + h - 1)
                for s in range(steps):
                    cut = lambda t: t[h][:, 8 * s:8 * s + 8, :].rearrange("p j w -> p (j w)")
                    nc.vector.tensor_tensor(cut(x3), cut(part), product(s, ch.eng, i, h), ALU.add).then_inc(used, 1)
                st.gate(ch.eng, used, (2 * i + h + 1) * steps)
                ln.centre(ch, h, x3[h][:, :, :])

            def finish(i, h):
                writable(ch.eng, "h3", i, h)
                writable(ch.eng, "out", i, h)
                ln.finish(ch, i, h, tout["h3"][h][:, :, :]).then_inc(ended, 1)
                st.gate(ch.eng, ended, 2 * i + h + 1)
                nc.vector.tensor_tensor(tout["out"][h][:, :, :], x3[h][:, :, :], tout["h3"][h][:, :, :], ALU.add).then_inc(made, 1)
            return [(0, clamp), (1, add_up), (0, prepare), (2, finish), (1, lambda i, h: ln.variance(ch, i, h))]

        def root_degree(act, i, h):
            st.gate(act, clamped, 2 * i + h + 1)
            nc.scalar.activation(root[h][:, :], root[h][:, :], ACT.Sqrt).then_inc(rooted, 1)
        return {"source": lambda h, u: flat[h][:, u * P:(u + 1) * P], "norm": ln, "turns_inputs": True, "vector": vector,
                "scalar": lambda act, copies: ([(0, lambda i, h: root_degree(act, i, h))] + [(0, f) for f in copies] + [(1, lambda i, h: ln.square_up(act, i, h)),
                                                                             (1, lambda i, h: ln.root(act, i, h))]),
                "inputs_read": read, "written": {"h3": (ended, 2), "out": (made, 2)}}
    node_stage(nc, "cheb", (0, CHUNKS), None, {"h2": ([h2], D), "x2": ([x2], D), "agg": ([agg], D), "info": ([info], 2)}, {"h3": (h3, D), "out": (out, D)},
               NC // 2, 4, 2 * D, [(0, 0, w0), (D, D, w0)], {"cheb": bias_}, setup)


CHEB_K = 10
SUBSTEPS, SERIES = 4, 20
EXPM_K = SUBSTEPS * SERIES
assert CHEB_K % 2 == 0 and EXPM_K % 2 == 0

LIST = 8
BODY = 2 * GROUP * P
BODIES = EP // BODY
FEW = 2
FINE = 2 * FEW * P
FINES = EP // FINE
NEST = 7
assert FINES % NEST == 0 and FINES * FINE == EP
ZERO_ROW = EP


def rounds(st, eng, bodies, body):
    with eng.Fori(0, BODIES) as i:
        with nullcontext() if isinstance(bodies, int) else eng.If(i < bodies):
            body(i)


def fine_rounds(eng, fine, body):
    with eng.Fori(0, FINES // NEST) as i:
        with eng.If(i * NEST < fine):
            with eng.Fori(0, NEST) as j:
                with eng.If(i * NEST + j < fine):
                    body(i * NEST + j)


def link_stage(nc, name, source, info, bodies_in, meta, next_list, bodies_out):
    st = Stage(nc, name)
    m = st.sb("meta", [P, META, TILES])
    mi = m[:, :, :].bitcast(U32)
    nxt, dst, same, low, last, pos, flag, tmp, rank = (
        st.sb(n, [P, TILES]) for n in ("next", "dst", "same", "low", "last", "pos", "flag", "tmp", "rank"))
    pointer, deg, npos = (st.sb(n, [P, TILES]) for n in ("pointer", "deg", "npos"))
    at_node, at_dst, at_rank = (st.sb(n, [P, TILES], U32) for n in ("at_node", "at_dst", "at_rank"))
    pair, found = st.sb("pair", [P, TILES, 2]), st.sb("found", [P, TILES, 2])
    rec = st.sb("records", [P, TILES, LIST])
    blank = st.sb("blank", [P, TILES, LIST])
    blank_info = st.sb("blank_info", [NP, N // NP, 2])
    slot_i = [st.sb(f"slot_i{h}", [P, GROUP], U32) for h in (0, 1)]
    slot_r = [st.sb(f"slot_r{h}", [P, GROUP, LIST]) for h in (0, 1)]
    slot_2 = [st.sb(f"slot_2{h}", [P, GROUP, 2]) for h in (0, 1)]
    lastp = st.sb("last_partition", [P, 1])
    below, ones = st.sb("below", [P, P]), st.sb("ones", [P, P])
    starts, counted, total = st.sb("starts", [P, BODIES + FINES]), st.sb("counted", [P, BODIES + FINES]), st.sb("total", [P, 1])
    bodies_f, bodies_i, given = st.sb("bodies_f", [P, 2]), st.sb("bodies_i", [P, 2], I32), st.sb("given", [1, 2], I32)
    pranks, ptotals = st.ps("ranks", [P, TILES]), st.ps("totals", [P, TILES])
    loaded, const, step, staged, moved, moves, cleared, flagged, ranked, rooted, made, stored, keyed = (
        st.sem(n) for n in ("loaded", "const", "step", "staged", "moved", "moves", "cleared", "flagged", "ranked",
                            "rooted", "made", "stored", "keyed"))
    block = st.block()
    n_loads = 2
    given_rec = st.sb("given_records", [P, TILES, LIST])
    following = NextEdge(st, nc)

    def load(sync):
        rows = source[0:EP, :].rearrange("(t p) w -> p t w", p=P)
        sync.dma_start(given_rec[:, :, :], rows).then_inc(loaded, 16)
        sync.dma_start(given[:, :], bodies_in).then_inc(loaded, 16)

    def fill_and_store(sync):
        sync.dma_start(info.rearrange("(p n) w -> p n w", p=NP), blank_info[:, :, :]).then_inc(cleared, 16)
        if next_list is not None:
            sync.dma_start(next_list.rearrange("(t p) w -> p t w", p=P), blank[:, :, :]).then_inc(cleared, 16)
        sync.wait_ge(made, 1)
        sync.dma_start(meta, m[:, :, :]).then_inc(stored, 16)
        if next_list is not None:
            sync.wait_ge(made, 2)
            sync.dma_start(bodies_out, bodies_i[0:1, :]).then_inc(stored, 16)
        sync.wait_ge(stored, 16 if next_list is None else 32)

    @block.sync
    def _(sync):
        load(sync)
        sync.wait_ge(const, 9)
        fill_and_store(sync)

    passes = 2 if next_list is None else 3

    @block.gpsimd
    def _(pool):
        following.pool(pool)
        pool.memset(lastp[:, :], 1.0).then_inc(const, 1)
        pool.memset(ones[:, :], 1.0).then_inc(const, 1)
        pool.memset(below[:, :], 1.0).then_inc(const, 1)
        pool.memset(blank[:, :, :], 0.0).then_inc(const, 1)
        pool.memset(blank_info[:, :, :], 0.0).then_inc(const, 1)
        pool.iota(pos[:, :], pattern=[[P, TILES]], base=0, channel_multiplier=1,
                  allow_small_or_imprecise_dtypes=True).then_inc(const, 1)
        pool.iota(starts[:, 0:BODIES], pattern=[[BODY, BODIES]], base=0, channel_multiplier=0,
                  allow_small_or_imprecise_dtypes=True)
        pool.iota(starts[:, BODIES:], pattern=[[FINE, FINES]], base=0, channel_multiplier=0,
                  allow_small_or_imprecise_dtypes=True).then_inc(const, 1)
        pool.wait_ge(const, 7)
        pool.affine_select(out=below[:, :], in_=below[:, :], compare_op=ALU.is_gt, fill=0.0, base=0,
                           pattern=[[1, P]], channel_multiplier=-1).then_inc(rooted, 1)
        pool.affine_select(out=lastp[:, :], in_=lastp[:, :], compare_op=ALU.is_ge, fill=0.0, base=-(P - 1),
                           pattern=[[0, 1]], channel_multiplier=1).then_inc(rooted, 1)
        pool.memset(blank[:, :, 0:2], float(PAD)).then_inc(rooted, 1)
        pool.memset(blank[:, :, 4:5], float(ZERO_ROW)).then_inc(rooted, 1)
        pool.memset(blank_info[:, :, 0:1], float(ZERO_ROW)).then_inc(rooted, 1)
        pool.wait_ge(rooted, 5)
        pool.sem_inc(const, 2)
        pool.wait_ge(loaded, 16 * n_loads)
        bodies = pool.value_load(given[0:1, 0:1], min_val=1, max_val=BODIES)
        pool.wait_ge(cleared, 16 if next_list is None else 32)
        for n in range(passes):
            def move(i):
                c = i + bodies * n
                st.gate(pool, staged, c + 1)
                for h in (0, 1):
                    for j in range(GROUP):
                        at = bass.IndirectOffsetOnAxis(ap=slot_i[h][:, j:j + 1], axis=0)
                        if n == 0:
                            pool.indirect_dma_start(info, at, slot_2[h][:, j, :], None, bounds_check=N - 1,
                                                    oob_is_err=False).then_inc(moves, 16)
                        elif n == 1:
                            pool.indirect_dma_start(slot_2[h][:, j, :], None, info, at).then_inc(moves, 16)
                        else:
                            pool.indirect_dma_start(next_list, at, slot_r[h][:, j, :], None, bounds_check=EP - 1,
                                                    oob_is_err=False).then_inc(moves, 16)
                st.gate(pool, moves, (c + 1) * (32 * GROUP))
                pool.sem_inc(moved, 1)
            rounds(st, pool, bodies, move)

    @block.tensor
    def _(pe):
        pe.wait_ge(keyed, 1)
        following.tensor(pe, m[:, KEY, :])
        if next_list is None:
            return
        pe.wait_ge(rooted, 5)
        pe.wait_ge(flagged, 1)
        nc.tensor.matmul(pranks[:, :], below[:, :], flag[:, :], start=True, stop=True)
        nc.tensor.matmul(ptotals[:, :], ones[:, :], flag[:, :], start=True, stop=True).then_inc(ranked, 1)

    @block.vector
    def _(dve):
        ch = Chain(st, dve, step)
        link, v = ch.link, nc.vector
        dve.sem_inc(moved, 1)
        dve.wait_ge(loaded, 16 * n_loads)
        dve.wait_ge(rooted, 5)
        bodies = dve.value_load(given[0:1, 0:1], min_val=1, max_val=BODIES)
        v.tensor_copy(m[:, KEY, :], given_rec[:, :, 0]).then_inc(keyed, 1)
        for to, w in ((dst[:, :], 1), (m[:, WEIGHT, :], 2), (m[:, WEIGHT2, :], 3), (pointer[:, :], 4)):
            link(v.tensor_copy(to, given_rec[:, :, w]))
        following.vector(ch, nxt)
        dve.wait_ge(keyed, 1)
        link(v.tensor_tensor(last[:, :], m[:, KEY, :], nxt[:, :], ALU.not_equal))
        link(v.tensor_scalar(same[:, :], m[:, KEY, :], 1.0, lastp[:, 0:1], ALU.add, ALU.mult))
        link(v.memset(m[:, PREV, 0:1], -1.0))
        link(v.tensor_scalar(m[:, PREV, 1:], same[:, 0:TILES - 1], -1.0, None, ALU.add))
        link(v.memset(deg[:, :], 0.0))
        link(v.tensor_copy(mi[:, OTHER, :], pointer[:, :]))
        link(v.tensor_scalar(low[:, :], m[:, KEY, :], float(N), None, ALU.is_lt))
        link(v.tensor_tensor(last[:, :], last[:, :], low[:, :], ALU.mult))
        link(v.tensor_scalar(npos[:, :], pos[:, :], float(N), None, ALU.add))
        link(v.tensor_tensor(tmp[:, :], m[:, KEY, :], npos[:, :], ALU.subtract))
        link(v.tensor_tensor(tmp[:, :], tmp[:, :], last[:, :], ALU.mult))
        link(v.tensor_tensor(tmp[:, :], tmp[:, :], npos[:, :], ALU.add))
        link(v.tensor_copy(mi[:, LAST, :], tmp[:, :]))
        link(v.tensor_scalar(tmp[:, :], m[:, KEY, :], -float(NO_ROW), None, ALU.add))
        link(v.tensor_tensor(tmp[:, :], tmp[:, :], last[:, :], ALU.mult))
        link(v.tensor_scalar(at_node[:, :], tmp[:, :], float(NO_ROW), None, ALU.add))
        link(v.tensor_scalar(at_dst[:, :], dst[:, :], float(N - 1), None, ALU.min))
        link(v.tensor_copy(pair[:, :, 0], pos[:, :]))
        link(v.tensor_copy(pair[:, :, 1], deg[:, :]))

        def send(index, rows, slots, n):
            def body(i):
                c = i + bodies * n
                st.gate(dve, moved, c + 1)
                for h in (0, 1):
                    g = (2 * i + h) * GROUP
                    ins = v.tensor_copy(slot_i[h][:, :], index[:, bass.ds(g, GROUP)])
                    if rows is not None:
                        ins = v.tensor_copy(slots[h][:, :, :], rows[:, bass.ds(g, GROUP), :])
                ins.then_inc(staged, 1)
                if rows is None:
                    st.gate(dve, moved, c + 2)
                    for h in (0, 1):
                        ins = v.tensor_copy(found[:, bass.ds((2 * i + h) * GROUP, GROUP), :], slot_2[h][:, :, :])
                    ch.n, ch.base = 0, i + after_head
                    link(ins)
            rounds(st, dve, bodies, body)

        send(at_node, pair, slot_2, 0)
        after_head = ch.n
        link(v.memset(found[:, :, 1:2], 0.0))
        link(v.memset(found[:, :, 0:1], float(ZERO_ROW)))
        after_head = ch.n
        send(at_dst, None, None, 1)
        ch.n, ch.base = after_head, bodies
        link(v.tensor_copy(m[:, OWN, :].bitcast(U32), found[:, :, 0]))
        link(v.tensor_scalar(flag[:, :], found[:, :, 0], float(ZERO_ROW), None, ALU.is_lt))
        v.tensor_tensor(flag[:, :], flag[:, :], low[:, :], ALU.mult).then_inc(flagged, 1)
        if next_list is not None:
            link(v.tensor_copy(rec[:, :, 3], m[:, WEIGHT2, :]))
        dve.sem_inc(made, 1)
        if next_list is None:
            return
        link(v.memset(rec[:, :, 5:LIST], 0.0))
        for w, a in ((0, m[:, KEY, :]), (1, dst[:, :]), (2, m[:, WEIGHT, :]), (4, found[:, :, 0])):
            link(v.tensor_copy(rec[:, :, w], a))
        dve.wait_ge(ranked, 1)
        link(v.tensor_tensor_scan(rank[:, :], ptotals[:, :], pos[:, :], 0.0, ALU.add, ALU.bypass))
        link(v.tensor_copy(total[:, :], rank[:, TILES - 1:TILES]))
        link(v.tensor_tensor(rank[:, :], rank[:, :], ptotals[:, :], ALU.subtract))
        link(v.tensor_tensor(rank[:, :], rank[:, :], pranks[:, :], ALU.add))
        link(v.tensor_scalar(rank[:, :], rank[:, :], -float(NO_ROW), None, ALU.add))
        link(v.tensor_tensor(rank[:, :], rank[:, :], flag[:, :], ALU.mult))
        link(v.tensor_scalar(at_rank[:, :], rank[:, :], float(NO_ROW), None, ALU.add))
        link(v.tensor_scalar(counted[:, :], starts[:, :], total[:, 0:1], None, ALU.is_lt))
        link(v.tensor_reduce(bodies_f[:, 0:1], counted[:, 0:BODIES], AX.X, ALU.add))
        link(v.tensor_reduce(bodies_f[:, 1:2], counted[:, BODIES:], AX.X, ALU.add))
        link(v.tensor_scalar(bodies_i[:, :], bodies_f[:, :], 1.0, None, ALU.max))
        dve.sem_inc(made, 1)
        send(at_rank, rec, slot_r, 2)
    st.close()


class FirstLink:

    def __init__(self, nc, source, degree, info, meta, next_list, bodies_out):
        self.nc, self.source, self.degree, self.info, self.meta = nc, source, degree, info, meta
        self.next_list, self.bodies_out = next_list, bodies_out
        self.ctx = ExitStack()
        sb = lambda n, shape, dt=F32: self.ctx.enter_context(nc.sbuf_tensor(f"link1_{n}", shape, dt))
        self.m, self.rec, self.low = sb("meta", [P, META, TILES]), sb("records", [P, TILES, LIST]), sb("low", [P, TILES])
        self.pair, self.found = sb("pair", [P, TILES, 2]), sb("found", [P, TILES, 2])
        self.at_node, self.at_dst, self.at_rank = (sb(n, [P, TILES], U32) for n in ("at_node", "at_dst", "at_rank"))

    def announce(self):
        return scatter_rows(self.nc, self.at_node, self.pair, 2, self.info, N - 1)

    def find(self):
        return gather_rows(self.nc, self.at_dst, self.found, 2, self.info)

    def list_up(self):
        return scatter_rows(self.nc, self.at_rank, self.rec, LIST, self.next_list, EP - 1)

    def begin(self):
        nc, m, low = self.nc, self.m, self.low
        st = Stage(nc, "link1_begin")
        mi = m[:, :, :].bitcast(U32)
        tmp, last, pos, npos, deg = (st.sb(n, [P, TILES]) for n in ("tmp", "last", "pos", "npos", "deg"))
        blank, blank_info = st.sb("blank", [P, TILES, LIST]), st.sb("blank_info", [NP, N // NP, 2])
        loaded, const, filled, step, cleared = (st.sem(n) for n in ("loaded", "const", "filled", "step", "cleared"))
        block = st.block()

        @block.sync
        def _(sync):
            sync.dma_start(m[:, :, :], self.source).then_inc(loaded, 16)
            with nc.allow_non_contiguous_dma("one word of each record"):
                sync.dma_start(deg[:, :], self.degree.rearrange("(t p) -> p t", p=P)).then_inc(loaded, 16)
            sync.wait_ge(filled, 3)
            sync.dma_start(self.info.rearrange("(p n) w -> p n w", p=NP), blank_info[:, :, :]).then_inc(cleared, 16)
            sync.dma_start(self.next_list.rearrange("(t p) w -> p t w", p=P), blank[:, :, :]).then_inc(cleared, 16)
            sync.wait_ge(cleared, 32)

        @block.gpsimd
        def _(pool):
            pool.iota(pos[:, :], pattern=[[P, TILES]], base=0, channel_multiplier=1,
                      allow_small_or_imprecise_dtypes=True).then_inc(const, 1)
            pool.memset(blank[:, :, :], 0.0).then_inc(const, 1)
            pool.memset(blank_info[:, :, :], 0.0).then_inc(const, 1)
            pool.wait_ge(const, 3)
            pool.memset(blank[:, :, 0:2], float(PAD)).then_inc(filled, 1)
            pool.memset(blank[:, :, 4:5], float(ZERO_ROW)).then_inc(filled, 1)
            pool.memset(blank_info[:, :, 0:1], float(ZERO_ROW)).then_inc(filled, 1)

        @block.vector
        def _(dve):
            link, v = Chain(st, dve, step).link, nc.vector
            dve.wait_ge(loaded, 32)
            dve.wait_ge(const, 3)
            link(v.tensor_copy(tmp[:, :], mi[:, LAST, :]))
            link(v.tensor_scalar(last[:, :], tmp[:, :], float(NO_ROW), None, ALU.is_lt))
            link(v.tensor_scalar(low[:, :], m[:, KEY, :], float(N), None, ALU.is_lt))
            link(v.tensor_tensor(last[:, :], last[:, :], low[:, :], ALU.mult))
            link(v.tensor_scalar(npos[:, :], pos[:, :], float(N), None, ALU.add))
            link(v.tensor_tensor(tmp[:, :], m[:, KEY, :], npos[:, :], ALU.subtract))
            link(v.tensor_tensor(tmp[:, :], tmp[:, :], last[:, :], ALU.mult))
            link(v.tensor_tensor(tmp[:, :], tmp[:, :], npos[:, :], ALU.add))
            link(v.tensor_copy(mi[:, LAST, :], tmp[:, :]))
            link(v.tensor_scalar(tmp[:, :], m[:, KEY, :], -float(NO_ROW), None, ALU.add))
            link(v.tensor_tensor(tmp[:, :], tmp[:, :], last[:, :], ALU.mult))
            link(v.tensor_scalar(self.at_node[:, :], tmp[:, :], float(NO_ROW), None, ALU.add))
            link(v.tensor_copy(self.at_dst[:, :], mi[:, OTHER, :]))
            link(v.tensor_copy(self.pair[:, :, 0], pos[:, :]))
            link(v.tensor_copy(self.pair[:, :, 1], deg[:, :]))
        st.close()

    def middle(self):
        nc, m, found, rec = self.nc, self.m, self.found, self.rec
        st = Stage(nc, "link1_middle")
        tmp, std, flag, rank, spare = (st.sb(n, [P, TILES]) for n in ("tmp", "std", "flag", "rank", "spare"))
        below, ones = st.sb("below", [P, P]), st.sb("ones", [P, P])
        starts, counted, total = st.sb("starts", [P, BODIES + FINES]), st.sb("counted", [P, BODIES + FINES]), st.sb("total", [P, 1])
        bodies_f, bodies_i = st.sb("bodies_f", [P, 2]), st.sb("bodies_i", [P, 2], I32)
        pranks, ptotals = st.ps("ranks", [P, TILES]), st.ps("totals", [P, TILES])
        const, step, flagged, ranked, asked, rooted, made, stored = (
            st.sem(n) for n in ("const", "step", "flagged", "ranked", "asked", "rooted", "made", "stored"))
        block = st.block()

        @block.sync
        def _(sync):
            sync.wait_ge(made, 1)
            sync.dma_start(self.meta, m[:, :, :]).then_inc(stored, 16)
            sync.dma_start(self.bodies_out, bodies_i[0:1, :]).then_inc(stored, 16)
            sync.wait_ge(stored, 32)

        @block.gpsimd
        def _(pool):
            pool.memset(ones[:, :], 1.0).then_inc(const, 1)
            pool.memset(below[:, :], 1.0).then_inc(const, 1)
            pool.memset(spare[:, :], 0.0).then_inc(const, 1)
            pool.iota(starts[:, 0:BODIES], pattern=[[BODY, BODIES]], base=0, channel_multiplier=0,
                      allow_small_or_imprecise_dtypes=True)
            pool.iota(starts[:, BODIES:], pattern=[[FINE, FINES]], base=0, channel_multiplier=0,
                      allow_small_or_imprecise_dtypes=True).then_inc(const, 1)
            pool.wait_ge(const, 4)
            pool.affine_select(out=below[:, :], in_=below[:, :], compare_op=ALU.is_gt, fill=0.0, base=0,
                               pattern=[[1, P]], channel_multiplier=-1).then_inc(const, 1)

        @block.tensor
        def _(pe):
            pe.wait_ge(const, 5)
            pe.wait_ge(flagged, 1)
            nc.tensor.matmul(pranks[:, :], below[:, :], flag[:, :], start=True, stop=True)
            nc.tensor.matmul(ptotals[:, :], ones[:, :], flag[:, :], start=True, stop=True).then_inc(ranked, 1)

        @block.scalar
        def _(act):
            act.wait_ge(asked, 1)
            nc.scalar.activation(std[:, :], tmp[:, :], ACT.Sqrt).then_inc(rooted, 1)

        @block.vector
        def _(dve):
            link, v = Chain(st, dve, step).link, nc.vector
            dve.wait_ge(const, 5)
            link(v.tensor_copy(m[:, OWN, :].bitcast(U32), found[:, :, 0]))
            link(v.tensor_scalar(flag[:, :], found[:, :, 0], float(ZERO_ROW), None, ALU.is_lt))
            v.tensor_tensor(flag[:, :], flag[:, :], self.low[:, :], ALU.mult).then_inc(flagged, 1)
            v.tensor_scalar(tmp[:, :], found[:, :, 1], 1.0, None, ALU.max).then_inc(asked, 1)
            dve.wait_ge(rooted, 1)
            link(v.reciprocal(std[:, :], std[:, :]))
            link(v.tensor_scalar(tmp[:, :], found[:, :, 1], 0.0, None, ALU.is_gt))
            link(v.tensor_tensor(m[:, WEIGHT2, :], std[:, :], tmp[:, :], ALU.mult))
            link(v.tensor_tensor(rec[:, :, 3], m[:, WEIGHT2, :], m[:, WEIGHT2, :], ALU.mult))
            link(v.memset(rec[:, :, 5:LIST], 0.0))
            for w, a in ((0, m[:, KEY, :]), (1, self.at_dst[:, :]), (2, m[:, WEIGHT, :]), (4, found[:, :, 0])):
                link(v.tensor_copy(rec[:, :, w], a))
            dve.wait_ge(ranked, 1)
            link(v.tensor_tensor_scan(rank[:, :], ptotals[:, :], spare[:, :], 0.0, ALU.add, ALU.bypass))
            link(v.tensor_copy(total[:, :], rank[:, TILES - 1:TILES]))
            link(v.tensor_tensor(rank[:, :], rank[:, :], ptotals[:, :], ALU.subtract))
            link(v.tensor_tensor(rank[:, :], rank[:, :], pranks[:, :], ALU.add))
            link(v.tensor_scalar(rank[:, :], rank[:, :], -float(NO_ROW), None, ALU.add))
            link(v.tensor_tensor(rank[:, :], rank[:, :], flag[:, :], ALU.mult))
            link(v.tensor_scalar(self.at_rank[:, :], rank[:, :], float(NO_ROW), None, ALU.add))
            link(v.tensor_scalar(counted[:, :], starts[:, :], total[:, 0:1], None, ALU.is_lt))
            link(v.tensor_reduce(bodies_f[:, 0:1], counted[:, 0:BODIES], AX.X, ALU.add))
            link(v.tensor_reduce(bodies_f[:, 1:2], counted[:, BODIES:], AX.X, ALU.add))
            v.tensor_scalar(bodies_i[:, :], bodies_f[:, :], 1.0, None, ALU.max).then_inc(made, 1)
        st.close()

    def close(self):
        self.ctx.close()


def first_cheb_edges(nc, meta, h_table, taylor, sums_table, target):
    def setup(st, c):
        w1 = st.sb("taylor1", [D, D])
        turned = st.sb("sums_t", [D, GROUP * P])
        sent = [st.sb(f"sent{h}", [P, GROUP, D]) for h in (0, 1)]
        pt, pr = st.ps("turn", [P, 1024]), st.ps("product", [P, 512])
        loaded_w, moved, tcopied, done = (st.sem(n) for n in ("loaded_w", "sums_turned", "turned_copied", "product_done"))
        stored = [st.sem(f"stored{h}") for h in (0, 1)]

        def sync(eng, i, h, first):
            st.gate(eng, c["copied"], (2 * i + h + 1) * GROUP)
            eng.dma_start(by_group(sums_table, 2 * i + h, 0, D), c["sums"][h][:, :, :]).then_inc(stored[h], 16)

        def pe_post(eng, i, h, first):
            g, start = 2 * i + h, first and h == 0
            st.gate(eng, c["copied"], (g + 1) * GROUP)
            if not start:
                st.gate(eng, tcopied, g)
            for j in range(GROUP):
                ins = nc.tensor.transpose(pt[0:D, j * P:(j + 1) * P], c["sums"][h][:, j, :], c["ident"][:, :])
            ins.then_inc(moved, 1)
            st.gate(eng, tcopied, g + 1)
            if not start:
                st.gate(eng, c["posted"], g)
            for j in range(GROUP):
                ins = nc.tensor.matmul(pr[:, j * D:(j + 1) * D], turned[:, j * P:(j + 1) * P], w1[:, :], start=True, stop=True)
            ins.then_inc(done, 1)

        def act_post(eng, i, h, first):
            g = 2 * i + h
            st.gate(eng, moved, g + 1)
            if not (first and h == 0):
                st.gate(eng, done, g)
            nc.scalar.activation(turned[:, :], pt[0:D, 0:GROUP * P], ACT.Copy).then_inc(tcopied, 1)

        def values(eng, i, h, first):
            st.gate(eng, c["got"][h], (i + 1) * c["per"])
            w = c["m"][:, WEIGHT2, bass.ds((2 * i + h) * GROUP, GROUP)].unsqueeze(2).to_broadcast([P, GROUP, D])
            return nc.vector.tensor_tensor(c["values"][h][:, :, :], c["rows"][h][:, :, :], w, ALU.mult)

        def post(eng, i, h, first):
            st.gate(eng, done, 2 * i + h + 1)
            if not first:
                st.gate(eng, c["put"][h], i * c["put_per"])
            return nc.vector.tensor_copy(sent[h][:, :, :], pr[:, 0:GROUP * D].rearrange("p (j w) -> p j w", w=D))

        def sync_end(eng):
            for h in (0, 1):
                eng.wait_ge(stored[h], 16 * c["half"])
        return {"sync_start": lambda eng: eng.dma_start(w1[:, :], taylor[D:2 * D, :]).then_inc(loaded_w, 16),
                "sync": sync, "sync_end": sync_end, "pe_start": lambda eng: eng.wait_ge(loaded_w, 16),
                "pe_post": pe_post, "act_post": act_post,
                "act_reuse": lambda eng, i, h: st.gate(eng, stored[h], i * 16),
                "values": values, "post": post, "sent": sent}
    edge_stage(nc, "cheb_first", meta, [(h_table, OTHER, 0, D)], D, D, setup, scatter=target, add=True)


def rate(nc, dve, st, sem, t_tile, out, inverse, coef):
    ch = Chain(st, dve, sem)
    ch.link(nc.vector.tensor_scalar(out[:, :], t_tile[:, :], 1e-8, -1.0, ALU.max, ALU.mult))
    ch.link(nc.vector.tensor_scalar(coef[:, :], inverse, out[:, 0:1], None, ALU.mult))


def first_expm_edges(nc, meta, h_table, t, factors, terms_table, target):
    def setup(st, c):
        K1 = factors.shape[1]
        sent = [st.sb(f"sent{h}", [P, GROUP, D]) for h in (0, 1)]
        fac, tt, mt, coef = st.sb("factors", [P, K1]), st.sb("t", [P, 1]), st.sb("minus_t", [P, 1]), st.sb("coef", [P, K1])
        loaded_w, cstep = st.sem("loaded_w"), st.sem("coef_step")
        stored = [st.sem(f"stored{h}") for h in (0, 1)]

        def sync_start(eng):
            eng.dma_start(fac[:, :], broadcast(factors[0, :], P)).then_inc(loaded_w, 16)
            eng.dma_start(tt[:, :], broadcast(t, P)).then_inc(loaded_w, 16)

        def vector_start(eng):
            eng.wait_ge(loaded_w, 32)
            rate(nc, eng, st, cstep, tt, mt, fac[:, :], coef)

        def sync(eng, i, h, first):
            st.gate(eng, c["posted"], 2 * i + h + 1)
            eng.dma_start(by_group(terms_table, 2 * i + h, 0, D), sent[h][:, :, :]).then_inc(stored[h], 16)

        def values(eng, i, h, first):
            st.gate(eng, c["got"][h], (i + 1) * c["per"])
            w = c["m"][:, WEIGHT, bass.ds((2 * i + h) * GROUP, GROUP)].unsqueeze(2).to_broadcast([P, GROUP, D])
            return nc.vector.tensor_tensor(c["values"][h][:, :, :], c["rows"][h][:, :, :], w, ALU.mult)

        def post(eng, i, h, first):
            st.gate(eng, c["copied"], (2 * i + h + 1) * GROUP)
            if not first:
                st.gate(eng, c["put"][h], i * c["put_per"])
                st.gate(eng, stored[h], i * 16)
            return nc.vector.tensor_scalar(sent[h][:, :, :], c["sums"][h][:, :, :], coef[:, 1:2], None, ALU.mult)

        def sync_end(eng):
            for h in (0, 1):
                eng.wait_ge(stored[h], 16 * c["half"])
        return {"sync_start": sync_start, "vector_start": vector_start, "sync": sync, "sync_end": sync_end,
                "values": values, "post": post, "sent": sent}
    edge_stage(nc, "expm_first", meta, [(h_table, OTHER, 0, D)], D, D, setup, scatter=target, add=True)


def tier_stage(nc, name, meta, bodies_in, before, tables, level, pairs, target, group=GROUP, taylor=None, expm=None):
    st = Stage(nc, name)
    m = st.sb("meta", [P, META, TILES])
    mi = m[:, :, :].bitcast(U32)
    acc = st.sb("acc", [P, TILES, D])
    ident, ones = st.sb("ident", [P, P]), st.sb("ones", [P, P])
    two = lambda n, shape, dt=F32: [st.sb(f"{n}{h}", shape, dt) for h in (0, 1)]
    index, keyslot, rows, values = two("index", [P, group], U32), two("keyslot", [P, group]), two("rows", [P, group, D]), two("values", [P, group, D])
    same, carry, sums = two("same", [P, group, P]), two("carry", [P, group, P]), two("sums", [P, group, D])
    nonzero = st.sb("nonzero", [P, group, D])
    some, any_, flag = st.sb("some", [P, 1]), st.sb("any", [P, 1]), st.sb("flag", [P, 1], I32)
    given = st.sb("given", [1, 2], I32)
    pkey = st.ps("pkey", [P, 1024])
    psum = [st.ps(f"psum{b}", [P, 512]) for b in (0, 1)]
    (const, loaded, staged, got, key_turned, same_made, values_ready, summed, copied, stored, step, cleared, scaled,
     turned_s, tcopied, product, checked, tested, level_ready, sent, put, placed, cstep) = (st.sem(n) for n in (
         "const", "loaded", "staged", "gathered", "key_turned", "same_made", "values_ready", "summed", "sum_copied",
         "stored", "step", "cleared", "scaled", "sums_turned", "turned_copied", "product", "checked", "tested",
         "level_ready", "sent", "put", "placed", "coef_step"))
    placed_free = st.sem("added")
    if taylor is not None:
        v = st.sb("taylor", [D, taylor.shape[0] // D, D])
        turned = st.sb("turned", [D, group * P])
        pt = st.ps("turn", [P, 1024])
        kept = sums
        n_loads = 3
    else:
        t, factors = expm
        K1 = factors.shape[1]
        fac, tt, mt, coef = st.sb("factors", [P, 2 * K1]), st.sb("t", [P, 1]), st.sb("minus_t", [P, 1]), st.sb("coef", [P, K1])
        kept = two("term", [P, group, D])
        n_loads = 5
    pr = st.ps("product", [P, 512])
    weight = WEIGHT2 if taylor is not None else WEIGHT
    block = st.block()
    per = 2 * group * 16

    def levels(eng, run):
        run(0, level, before, tables[0], OTHER)
        if eng is vec[0]:
            eng.sem_inc(level_ready, 1)
        if not pairs:
            return
        at_once = 4 if pairs % 2 == 0 else 2
        with eng.Fori(0, 2 * pairs // at_once) as q:
            st.gate(eng, level_ready, at_once * q + 1)
            any_due = eng.value_load(flag[0:1, 0:1], min_val=0, max_val=1)
            with eng.If(any_due > 0):
                for k in range(at_once):
                    n = at_once * q + (1 + k)
                    if k:
                        st.gate(eng, level_ready, n)
                        due = eng.value_load(flag[0:1, 0:1], min_val=0, max_val=1)
                    with eng.If(due > 0) if k else nullcontext():
                        run(n, n + level, tables[k % 2], tables[1 - k % 2], OWN)
                    if eng is vec[0]:
                        eng.sem_inc(level_ready, 1)
            if eng is vec[0]:
                with eng.If(any_due < 1):
                    eng.sem_inc(level_ready, at_once)
    vec = [None]

    def count(eng):
        eng.wait_ge(loaded, 16 * n_loads)
        if group == GROUP:
            bodies = eng.value_load(given[0:1, 0:1], min_val=1, max_val=BODIES)
            return bodies, lambda body: rounds(st, eng, bodies, body)
        fine = eng.value_load(given[0:1, 1:2], min_val=1, max_val=FINES)
        return fine, lambda body: fine_rounds(eng, fine, body)

    @block.sync
    def _(sync):
        sync.dma_start(m[:, :, :], meta).then_inc(loaded, 16)
        sync.dma_start(given[:, :], bodies_in).then_inc(loaded, 16)
        if taylor is not None:
            sync.dma_start(v[:, :, :], taylor.rearrange("(k i) o -> i k o", i=D)).then_inc(loaded, 16)
        else:
            for n in (0, 1):
                sync.dma_start(fac[:, n * K1:(n + 1) * K1], broadcast(factors[n, :], P)).then_inc(loaded, 16)
            sync.dma_start(tt[:, :], broadcast(t, P)).then_inc(loaded, 16)
        bodies, over_list = count(sync)

        def run(n, k, source, into, row):
            def body(i):
                c = n * bodies + i
                for h in (0, 1):
                    if taylor is not None:
                        st.gate(sync, copied, c * (2 * group) + (h + 1) * group)
                    else:
                        st.gate(sync, scaled, c * 2 + (h + 1))
                    sync.dma_start(by_group(into, 2 * i + h, 0, D, group), kept[h][:, :, :]).then_inc(stored, 16)
            over_list(body)
        levels(sync, run)
        st.gate(sync, stored, bodies * 32)

    @block.gpsimd
    def _(pool):
        pool.memset(sums[1][:, :, :], 0.0).then_inc(cleared, 1)
        pool.memset(ones[:, :], 1.0).then_inc(cleared, 1)
        pool.memset(acc[:, :, :], 0.0).then_inc(cleared, 1)
        pool.memset(some[:, :], 0.0).then_inc(cleared, 1)
        identity(st, pool, ident, const)
        bodies, over_list = count(pool)

        def run(n, k, source, into, row):
            def body(i):
                c = n * bodies + i
                st.gate(pool, staged, c + 1)
                for h in (0, 1):
                    for j in range(group):
                        pool.indirect_dma_start(rows[h][:, j, :], None, source,
                                                bass.IndirectOffsetOnAxis(ap=index[h][:, j:j + 1], axis=0)).then_inc(got, 16)
            over_list(body)
        levels(pool, run)

        def add(i):
            st.gate(pool, sent, i + 1)
            for h in (0, 1):
                for j in range(group):
                    pool.indirect_dma_start(target, bass.IndirectOffsetOnAxis(ap=index[h][:, j:j + 1], axis=0),
                                            rows[h][:, j, :], None, compute_op=ALU.add).then_inc(put, 16)
            st.gate(pool, put, (i + 1) * per)
            pool.sem_inc(placed_free, 1)
        over_list(add)

    @block.tensor
    def _(pe):
        pe.wait_ge(const, 2)
        pe.wait_ge(cleared, 4)
        bodies, over_list = count(pe)

        def run(n, k, source, into, row):
            def body(i):
                c = n * bodies + i
                st.gate(pe, staged, c + 1)
                for h in (0, 1):
                    if h:
                        st.gate(pe, same_made, c * 2 + 1)
                    for j in range(group):
                        ins = nc.tensor.transpose(pkey[:, j * P:(j + 1) * P], keyslot[h][:, j:j + 1].to_broadcast([P, P]), ident[:, :])
                    ins.then_inc(key_turned, 1)
                for h in (0, 1):
                    st.gate(pe, values_ready, c * 2 + h + 1)
                    for j in range(group):
                        tile = h * group + j
                        if tile >= 2:
                            st.gate(pe, copied, c * (2 * group) + (tile - 1))
                        nc.tensor.matmul(psum[tile % 2][:, 0:D], same[h][:, j, :], values[h][:, j, :], start=True, stop=False)
                        if tile:
                            st.gate(pe, copied, c * (2 * group) + tile)
                        prior = sums[h][:, j - 1, :] if j else sums[1 - h][:, group - 1, :]
                        nc.tensor.matmul(psum[tile % 2][:, 0:D], carry[h][:, j, :], prior, start=False, stop=True).then_inc(summed, 1)
                if taylor is None:
                    return
                for h in (0, 1):
                    st.gate(pe, copied, c * (2 * group) + (h + 1) * group)
                    if h:
                        st.gate(pe, tcopied, c * 2 + 1)
                    for j in range(group):
                        ins = nc.tensor.transpose(pt[0:D, j * P:(j + 1) * P], sums[h][:, j, :], ident[:, :])
                    ins.then_inc(turned_s, 1)
                    st.gate(pe, tcopied, c * 2 + h + 1)
                    if h:
                        st.gate(pe, placed, c * 2 + 1)
                    for j in range(group):
                        ins = nc.tensor.matmul(pr[:, j * D:(j + 1) * D], turned[:, j * P:(j + 1) * P],
                                               v[:, bass.ds(k, 1), :].rearrange("i k o -> i (k o)"), start=True, stop=True)
                    ins.then_inc(product, 1)
            over_list(body)
            st.gate(pe, checked, n + 1)
            nc.tensor.matmul(pr[:, 0:1], ones[:, :], some[:, :], start=True, stop=True).then_inc(tested, 1)
        levels(pe, run)

    @block.scalar
    def _(act):
        act.wait_ge(cleared, 4)
        bodies, over_list = count(act)

        def run(n, k, source, into, row):
            def body(i):
                c = n * bodies + i
                for h in (0, 1):
                    for j in range(group):
                        st.gate(act, summed, c * (2 * group) + (h * group + j + 1))
                        nc.scalar.activation(sums[h][:, j, :], psum[(h * group + j) % 2][:, 0:D], ACT.Copy).then_inc(copied, 1)
                if taylor is None:
                    return
                for h in (0, 1):
                    st.gate(act, turned_s, c * 2 + h + 1)
                    if h:
                        st.gate(act, product, c * 2 + 1)
                    nc.scalar.activation(turned[:, :], pt[0:D, 0:group * P], ACT.Copy).then_inc(tcopied, 1)
            over_list(body)
        levels(act, run)

    @block.vector
    def _(dve):
        vec[0] = dve
        vx = nc.vector
        dve.wait_ge(cleared, 4)
        bodies, over_list = count(dve)
        if taylor is None:
            rate(nc, dve, st, cstep, tt, mt, fac[:, 0:K1], coef)
        steps_body, steps_level = 6, 2

        def run(n, k, source, into, row):
            def chain(i, at):
                return (n * bodies + i) * steps_body + n * steps_level + at

            def body(i):
                c = n * bodies + i
                for h in (0, 1):
                    g = (2 * i + h) * group
                    vx.tensor_copy(index[h][:, :], mi[:, row, bass.ds(g, group)])
                    ins = vx.tensor_copy(keyslot[h][:, :], m[:, KEY, bass.ds(g, group)])
                ins.then_inc(staged, 1)
                for h in (0, 1):
                    st.gate(dve, key_turned, c * 2 + h + 1)
                    turned_k = pkey[:, 0:group * P].rearrange("p (j e) -> p j e", e=P)
                    for r, mat in ((KEY, same), (PREV, carry)):
                        ins = vx.tensor_tensor(mat[h][:, :, :], turned_k,
                                               m[:, r, bass.ds((2 * i + h) * group, group)].unsqueeze(2).to_broadcast([P, group, P]), ALU.is_equal)
                    ins.then_inc(same_made, 1)
                st.gate(dve, got, (c + 1) * per)
                for h in (0, 1):
                    w = m[:, weight, bass.ds((2 * i + h) * group, group)].unsqueeze(2).to_broadcast([P, group, D])
                    vx.tensor_tensor(values[h][:, :, :], rows[h][:, :, :], w, ALU.mult).then_inc(values_ready, 1)
                for h in (0, 1):
                    part = acc[:, bass.ds((2 * i + h) * group, group), :]
                    if taylor is not None:
                        st.gate(dve, product, c * 2 + h + 1)
                        vx.tensor_tensor(part, part, pr[:, 0:group * D].rearrange("p (j w) -> p j w", w=D), ALU.add).then_inc(placed, 1)
                    else:
                        st.gate(dve, copied, c * (2 * group) + (h + 1) * group)
                        vx.tensor_scalar(kept[h][:, :, :], sums[h][:, :, :], coef[:, bass.ds(k, 1)], None, ALU.mult).then_inc(scaled, 1)
                        st.gate(dve, scaled, c * 2 + h + 1)
                        vx.scalar_tensor_tensor(out=part, in0=kept[h][:, :, :], scalar=fac[:, bass.ds(k + K1, 1)], in1=part,
                                                op0=ALU.mult, op1=ALU.add).then_inc(placed, 1)
                    vx.tensor_scalar(nonzero[:, :, :], kept[h][:, :, :], 0.0, None, ALU.not_equal).then_inc(step, 1)
                    st.gate(dve, step, chain(i, 3 * h + 1))
                    vx.tensor_reduce(any_[:, :], nonzero[:, :, :].rearrange("p j w -> p (j w)"), AX.X, ALU.max).then_inc(step, 1)
                    st.gate(dve, step, chain(i, 3 * h + 2))
                    vx.tensor_tensor(some[:, :], some[:, :], any_[:, :], ALU.max).then_inc(step, 1)
                    st.gate(dve, step, chain(i, 3 * h + 3))
                    st.gate(dve, placed, c * 2 + h + 1)
                st.gate(dve, stored, (c + 1) * 32)
            over_list(body)
            dve.sem_inc(checked, 1)
            st.gate(dve, tested, n + 1)
            vx.tensor_scalar(flag[:, :], pr[:, 0:1], 1.0, None, ALU.min).then_inc(step, 1)
            st.gate(dve, step, chain(bodies, 1))
            vx.memset(some[:, :], 0.0).then_inc(step, 1)
            st.gate(dve, step, chain(bodies, 2))
        levels(dve, run)
        dve.sem_inc(placed_free, 1)

        def give(i):
            st.gate(dve, placed_free, i + 1)
            for h in (0, 1):
                g = (2 * i + h) * group
                vx.tensor_copy(index[h][:, :], mi[:, LAST, bass.ds(g, group)])
                ins = vx.tensor_copy(rows[h][:, :, :], acc[:, bass.ds(g, group), :])
            ins.then_inc(sent, 1)
        over_list(give)
    st.close()


def gnn(nc, x, src, dst, ea16, ea32, ew, w, factors, out):
    ctx = ExitStack()
    Stage.psum = ctx.enter_context(nc.psum_tensor("psum", [P, 8 * BANK], F32))
    dram = lambda name, shape: nc.dram_tensor(name, shape, F32, kind="Internal").ap()
    by_dst, half_d = dram("by_dst", [EP, REC]), dram("half_d", [EP, REC])
    by_src, half_s = dram("by_src", [EP, NARROW]), dram("half_s", [EP, NARROW])
    p1, q1, p2, q2, agg1, agg2 = (dram(n, [N, 16]) for n in ("p1", "q1", "p2", "q2", "agg1", "agg2"))
    eaw1, eaw2, ea32t = dram("eaw1", [EP, 16]), dram("eaw2", [EP, 16]), dram("ea32t", [32, EP])
    meta_d, meta_s = dram("meta_d", [P, META, TILES]), dram("meta_s", [P, META, TILES])
    x1, h1, agg3 = dram("x1", [N, D]), dram("h1", [N, D]), dram("agg3", [N, D])
    x2, h2, h3 = dram("x2", [N, D]), dram("h2", [N, D]), dram("h3", [N, D])
    aggc = dram("aggc", [N + EP, D])
    degree, info1 = dram("degree", [EP]), dram("info1", [N, 2])
    infos = [info1] + [dram(f"info{n}", [N, 2]) for n in (2, 3, 4)]
    metas = [dram(f"meta{n}", [P, META, TILES]) for n in (1, 2, 3, 4)]
    lists = [None] + [dram(f"list{n}", [EP, LIST]) for n in (2, 3, 4)]
    counts = [None] + [nc.dram_tensor(f"bodies{n}", [1, 2], I32, kind="Internal").ap() for n in (2, 3, 4)]
    level_sums = [dram(f"sums{n}", [EP + P, D]) for n in (1, 2, 3)]
    turns = [dram(f"turn{n}", [EP + P, D]) for n in (0, 1)]
    zeroes = zero_pieces(agg1, agg2, agg3, aggc, out[N:, :], level_sums[0][EP:, :], *level_sums[1:], *turns)
    share = -(-len(zeroes) // (2 * len(DIGITS)))

    inputs = (src, dst, ew, ea16, ea32)
    sort = Sort(nc, "sort_dst", REC, DST, by_dst, half_d, inputs)
    for n, part in enumerate(parts_of_chunks(len(DIGITS))):
        sort.ranks(n, zeroes[n * share:(n + 1) * share])
        projection_stage(nc, "project1", part, sort.scatter(n), {"x": ([x], D)}, p1, q1, w["L0_gnn_W_msg1"][0:D, :],
                         w["L0_gnn_W_skip1"], w["L0_gnn_b_skip1"], 2, True)
    sort.close()
    order_stage(nc, "order_dst", by_dst, DST, SRC, meta_d)
    edge_features_stage(nc, by_dst, w["L0_gnn_W_msg1"][D:D + 16, :], w["L0_gnn_W_msg2"][16:32, :],
                        w["L0_gnn_b_msg1"], w["L0_gnn_b_msg2"], eaw1, eaw2, ea32t)
    conv_edges(nc, "conv1", meta_d, p1, eaw1, agg1)
    sort = Sort(nc, "sort_src", NARROW, SRC, by_src, half_s, inputs)
    sort.ranks(0, zeroes[3 * share:4 * share])
    projection_stage(nc, "project2", (0, CHUNKS), sort.scatter(0), {"agg": ([agg1], 16), "q": ([q1], 16)}, p2, q2,
                     w["L0_gnn_W_msg2"][0:16, :], w["L0_gnn_W_skip2"], w["L0_gnn_b_skip2"], 8, False)
    conv_edges(nc, "conv2", meta_d, p2, eaw2, agg2)
    for n, part in enumerate(parts_of_chunks(len(DIGITS) - 1), 1):
        sort.ranks(n, zeroes[(3 + n) * share:(4 + n) * share])
        lin3_stage(nc, part, sort.scatter(n), x, agg2, q2, w["L0_gnn_W_lin3"], w["L0_gnn_b_lin3"], x1, h1)
    sort.close()
    order_stage(nc, "order_src", by_src, SRC, DST, meta_s, degree=degree)
    message_edges(nc, meta_d, h1, ea32t, w["L1_gnn_W1"], w["L1_gnn_b1"], w["L1_gnn_W2"], w["L1_gnn_b2"], agg3)
    link = FirstLink(nc, meta_s, degree, infos[0], metas[0], lists[1], counts[1])
    link.begin()
    for part, moves in zip(parts_of_chunks(3), (link.announce, link.find, link.list_up)):
        if moves == link.list_up:
            link.middle()
        gru_stage(nc, part, moves(), x1, h1, agg3, w["L1_gnn_w_ih"], w["L1_gnn_w_hh"], w["L1_gnn_b_ih"], w["L1_gnn_b_hh"], x2, h2)
    link.close()
    for n in (1, 2, 3):
        link_stage(nc, f"link{n + 1}", lists[n], infos[n], counts[n], metas[n],
                   lists[n + 1] if n < 3 else None, counts[n + 1] if n < 3 else None)
    taylor = dram("taylor", [w["L2_gnn_W"].shape[0] * D, D])
    cheb_weights_stage(nc, w["L2_gnn_W"], taylor)
    first_cheb_edges(nc, metas[0], h2, taylor, level_sums[0], aggc)
    for n in (1, 2, 3):
        tier_stage(nc, f"cheb_tier{n + 1}", metas[n], counts[n], level_sums[n - 1], level_sums[n:n + 1] if n < 3 else turns,
                   n + 1, 0 if n < 3 else (CHEB_K - 4) // 2, aggc, GROUP if n < 3 else FEW, taylor=taylor)
    cheb_stage(nc, x2, h2, aggc, info1, taylor[0:D, :], w["L2_gnn_bias"], h3, out)
    first_expm_edges(nc, metas[0], h3, w["L3_gnn_t"], factors, level_sums[0], out)
    for n in (1, 2, 3):
        tier_stage(nc, f"expm_tier{n + 1}", metas[n], counts[n], level_sums[n - 1], level_sums[n:n + 1] if n < 3 else turns,
                   n + 1, 0 if n < 3 else (EXPM_K - 4) // 2, out, GROUP if n < 3 else FEW, expm=(w["L3_gnn_t"], factors))
    ctx.close()


INS = ['x', 'src', 'dst', 'edge_attr_16', 'edge_attr_32', 'edge_weight']
WS = ['L0_gnn_W_msg1', 'L0_gnn_b_msg1', 'L0_gnn_W_skip1', 'L0_gnn_b_skip1', 'L0_gnn_W_msg2', 'L0_gnn_b_msg2', 'L0_gnn_W_skip2', 'L0_gnn_b_skip2', 'L0_gnn_W_lin3', 'L0_gnn_b_lin3', 'L1_gnn_W1', 'L1_gnn_b1', 'L1_gnn_W2', 'L1_gnn_b2', 'L1_gnn_w_ih', 'L1_gnn_w_hh', 'L1_gnn_b_ih', 'L1_gnn_b_hh', 'L2_gnn_W', 'L2_gnn_bias', 'L3_gnn_t']


TURNED = ['L1_gnn_W1', 'L1_gnn_W2', 'L1_gnn_w_ih', 'L1_gnn_w_hh']


def kernel(**inputs):
    import numpy as np
    import concourse.bacc as bacc
    from concourse import mybir as mb
    from concourse.bass_utils import run_bass_kernel_spmd as run

    nc = bacc.Bacc("TRN2", target_bir_lowering=False, num_devices=1)
    arrays, aps = {}, {}
    for name in INS + WS:
        a = np.asarray(inputs[name])
        a = np.ascontiguousarray(a.T if name in TURNED else a)
        arrays[f"in_{name}"] = a
        aps[name] = nc.dram_tensor(f"in_{name}", a.shape, mb.dt.from_np(a.dtype), kind="ExternalInput").ap()
    series = np.array([1.0 / factorial(j) for j in range(SERIES + 1)])
    power = np.ones(1)
    for _ in range(SUBSTEPS):
        power = np.convolve(power, series)
    factors = np.ones((2, EXPM_K + 1), np.float32)
    for k in range(1, EXPM_K + 1):
        factors[0, k] = 1.0 / k
        factors[1, k] = power[k] * float(factorial(k)) / float(SUBSTEPS) ** k
    arrays["in_factors"] = factors
    fac = nc.dram_tensor("in_factors", factors.shape, mb.dt.float32, kind="ExternalInput").ap()
    out = nc.dram_tensor("out_nodes", (N + EP, D), mb.dt.float32, kind="ExternalOutput").ap()
    gnn(nc, *[aps[n] for n in INS], {n: aps[n] for n in WS}, fac, out)
    r = run(nc, [arrays], core_ids=[0])
    return r.results[0]["out_nodes"][0:N]
```

```python
from contextlib import ExitStack, nullcontext
from math import comb, factorial

import concourse.bass as bass
from concourse import mybir

F32 = mybir.dt.float32
I32 = mybir.dt.int32
U32 = mybir.dt.uint32
ALU = mybir.AluOpType
ACT = mybir.ActivationFunctionType
AX = mybir.AxisListType

P = 128
N, D, E = 100000, 64, 25000
TILES = -(-E // P)
EP = TILES * P
PAD = (1 << 17) - 1
DIGITS = [(0, 6), (6, 6), (12, 5)]
GROUP = 7
GROUPS = TILES // GROUP
NO_ROW = 1 << 20
assert N < PAD and GROUPS * GROUP == TILES and GROUPS % 2 == 0

BANK = 512

NP, NC = 125, 16
CHUNKS = N // (NP * NC)
assert CHUNKS % 2 == 0 and CHUNKS * NP * NC == N


class Stage:

    def __init__(self, nc, name):
        self.nc, self.name, self.ctx = nc, name, ExitStack()
        self.sems, self.bank = [], 0
        self.passed = self.sem("wait_passed")

    def sb(self, name, shape, dt=F32):
        return self.ctx.enter_context(self.nc.sbuf_tensor(f"{self.name}_{name}", shape, dt))

    def ps(self, name, shape, dt=F32):
        at = self.bank * BANK
        self.bank += -(-shape[1] // BANK)
        assert self.bank <= 8
        return Stage.psum[0:shape[0], at:at + shape[1]]

    def sem(self, name):
        self.sems.append(self.nc.alloc_semaphore(f"{self.name}_{name}"))
        return self.sems[-1]

    def block(self):
        return self.ctx.enter_context(self.nc.Block())

    def close(self):
        self.ctx.close()
        self.nc.clear_and_free_semaphores(self.sems)
        self.nc.all_engine_barrier()

    def gate(self, eng, sem, value):
        eng.wait_ge(sem, value)
        if not isinstance(value, int):
            eng.sem_inc(self.passed, 1)


class Chain:

    def __init__(self, stage, eng, sem):
        self.stage, self.eng, self.sem, self.n, self.base = stage, eng, sem, 0, 0

    def link(self, ins):
        self.n += 1
        ins.then_inc(self.sem, 1)
        self.stage.gate(self.eng, self.sem, self.base + self.n)


def halves(eng, count, body):
    body(0, True, False)
    with eng.Fori(1, count - 1) as i:
        body(i, False, False)
    body(count - 1, False, True)


def identity(st, eng, tile, sem):
    eng.memset(tile[:, :], 0.0).then_inc(sem, 1)
    eng.wait_ge(sem, 1)
    eng.affine_select(out=tile[:, :], in_=tile[:, :], compare_op=ALU.not_equal, fill=1.0, base=0,
                      pattern=[[-1, P]], channel_multiplier=1).then_inc(sem, 1)


def zero_pieces(*tables):
    pieces = []
    for z in tables:
        flat = z.rearrange("n w -> (n w)")
        size, at = flat.shape[0], 0
        while at < size:
            part = min(size - at, P * 4096)
            lanes = P if part % P == 0 else 125
            assert part % lanes == 0
            pieces.append((flat[at:at + part].rearrange("(p n) -> p n", p=lanes), lanes, part // lanes))
            at += part
    return pieces


def scatter_rows(nc, index, rows, width, table, bound):
    def attach(st):
        slot_i = [st.sb(f"move_i{h}", [P, GROUP], U32) for h in (0, 1)]
        slot_r = [st.sb(f"move_r{h}", [P, GROUP, width]) for h in (0, 1)]
        filled, sent = st.sem("move_filled"), [st.sem(f"move_sent{h}") for h in (0, 1)]

        def run(pool):
            def body(i, first, last):
                for h in (0, 1):
                    if not first:
                        st.gate(pool, sent[h], i * (16 * GROUP))
                    g = (2 * i + h) * GROUP
                    pool.tensor_copy(slot_i[h][:, :], index[:, bass.ds(g, GROUP)])
                    pool.tensor_copy(slot_r[h][:, :, :], rows[:, bass.ds(g, GROUP), :]).then_inc(filled, 1)
                    st.gate(pool, filled, 2 * i + h + 1)
                    for j in range(GROUP):
                        pool.indirect_dma_start(
                            table, bass.IndirectOffsetOnAxis(ap=slot_i[h][:, j:j + 1], axis=0),
                            slot_r[h][:, j, :], None, bounds_check=bound, oob_is_err=False).then_inc(sent[h], 16)
            halves(pool, GROUPS // 2, body)
            for h in (0, 1):
                pool.wait_ge(sent[h], 16 * GROUP * (GROUPS // 2))
        return run
    return attach


def scatter_wide_rows(nc, index, rows, table, bound):
    def attach(st):
        sent = [st.sem(f"move_sent{h}") for h in (0, 1)]

        def run(pool):
            for t in range(TILES):
                i, h = t // (2 * GROUP), t // GROUP % 2
                if i and t % GROUP == 0:
                    pool.wait_ge(sent[h], i * (16 * GROUP))
                pool.indirect_dma_start(table, bass.IndirectOffsetOnAxis(ap=index[:, t:t + 1], axis=0),
                                        rows[:, t, :], None, bounds_check=bound, oob_is_err=False).then_inc(sent[h], 16)
            for h in (0, 1):
                pool.wait_ge(sent[h], 16 * GROUP * (GROUPS // 2))
        return run
    return attach


def gather_rows(nc, index, found, width, table):
    def attach(st):
        slot_i = [st.sb(f"find_i{h}", [P, GROUP], U32) for h in (0, 1)]
        slot_r = [st.sb(f"find_r{h}", [P, GROUP, width]) for h in (0, 1)]
        filled, got = st.sem("find_filled"), [st.sem(f"find_got{h}") for h in (0, 1)]
        half = GROUPS // 2

        def run(pool):
            def take(i, h):
                st.gate(pool, got[h], (i + 1) * (16 * GROUP))
                pool.tensor_copy(found[:, bass.ds((2 * i + h) * GROUP, GROUP), :], slot_r[h][:, :, :])

            def body(i, first, last):
                for h in (0, 1):
                    if not first:
                        take(i - 1, h)
                    pool.tensor_copy(slot_i[h][:, :], index[:, bass.ds((2 * i + h) * GROUP, GROUP)]).then_inc(filled, 1)
                    st.gate(pool, filled, 2 * i + h + 1)
                    for j in range(GROUP):
                        pool.indirect_dma_start(slot_r[h][:, j, :], None, table,
                                                bass.IndirectOffsetOnAxis(ap=slot_i[h][:, j:j + 1], axis=0)).then_inc(got[h], 16)
            halves(pool, half, body)
            for h in (0, 1):
                take(half - 1, h)
        return run
    return attach


def one_after_the_other(first, second):
    def attach(st):
        runs = first(st), second(st)

        def run(pool):
            for r in runs:
                r(pool)
        return run
    return attach


class NextEdge:

    def __init__(self, st, nc):
        self.nc = nc
        self.up, self.wrap = st.sb("shift_up", [P, P]), st.sb("shift_wrap", [P, P])
        self.moved, self.wrapped = st.ps("next_moved", [P, TILES]), st.ps("next_wrapped", [P, TILES])
        self.const, self.done = st.sem("shift_consts"), st.sem("next_done")

    def pool(self, pool):
        for tile in (self.up, self.wrap):
            pool.memset(tile[:, :], 0.0).then_inc(self.const, 1)
        pool.wait_ge(self.const, 2)
        for tile, base in ((self.up, -1), (self.wrap, P - 1)):
            pool.affine_select(out=tile[:, :], in_=tile[:, :], compare_op=ALU.not_equal, fill=1.0, base=base,
                               pattern=[[-1, P]], channel_multiplier=1).then_inc(self.const, 1)

    def tensor(self, pe, value):
        pe.wait_ge(self.const, 4)
        self.nc.tensor.matmul(self.moved[:, :], self.up[:, :], value, start=True, stop=True)
        self.nc.tensor.matmul(self.wrapped[:, :], self.wrap[:, :], value, start=True, stop=True).then_inc(self.done, 1)

    def vector(self, ch, out):
        ch.eng.wait_ge(self.done, 1)
        ch.link(self.nc.vector.tensor_copy(out[:, :], self.moved[:, :]))
        ch.link(self.nc.vector.tensor_tensor(out[:, 0:TILES - 1], out[:, 0:TILES - 1], self.wrapped[:, 1:], ALU.add))


SRC, DST, WGT, EA16, EA32, REC = 0, 1, 2, 3, 19, 52
NARROW = 4


class Work:

    def __init__(self, sync, vector, scalar=lambda eng: None, pool=lambda eng: None, tensor=lambda eng: None):
        self.sync, self.scalar, self.pool, self.tensor, self.vector = sync, scalar, pool, tensor, vector


class Sort:

    def __init__(self, nc, name, width, key, ping, pong, inputs):
        self.nc, self.name, self.width, self.key, self.inputs = nc, name, width, key, inputs
        self.ctx = ExitStack()
        self.rec = self.ctx.enter_context(nc.sbuf_tensor(f"{name}_records", [P, TILES, width], F32))
        self.rank_i = self.ctx.enter_context(nc.sbuf_tensor(f"{name}_rank", [P, TILES], U32))
        self.tables = [ping if (len(DIGITS) - 1 - n) % 2 == 0 else pong for n in range(len(DIGITS))]

    def scatter(self, n):
        if self.width == REC:
            return scatter_wide_rows(self.nc, self.rank_i, self.rec, self.tables[n][:, :], EP - 1)
        return scatter_rows(self.nc, self.rank_i, self.rec, self.width, self.tables[n][:, :], EP - 1)

    def ranks(self, n, zeroes):
        st = Stage(self.nc, f"{self.name}_ranks{n}")
        work = self.rank_work(n, zeroes)(st)
        block = st.block()
        block.sync(work.sync)
        block.gpsimd(work.pool)
        block.tensor(work.tensor)
        block.vector(work.vector)
        if zeroes:
            block.scalar(work.scalar)
        st.close()

    def rank_work(self, n, zeroes=()):
        return lambda st: self.attach_ranks(st, n, zeroes)

    def attach_ranks(self, st, n, zeroes):
        nc, rec, rank_i, key = self.nc, self.rec, self.rank_i, self.key
        shift, bits = DIGITS[n]
        bins_n = 1 << bits
        onehot = st.sb("rank_onehot", [P, bins_n, TILES])
        count = st.sb("rank_count", [P, bins_n, TILES])
        bins = st.sb("rank_bins", [P, bins_n])
        digit_i = st.sb("rank_digit_i", [P, TILES], I32)
        digit, rank = st.sb("rank_digit", [P, TILES]), st.sb("rank_rank", [P, TILES])
        inbin, base, upto = (st.sb(f"rank_{x}", [P, bins_n]) for x in ("inbin", "base", "upto"))
        below, ones = st.sb("rank_below", [P, P]), st.sb("rank_ones", [P, P])
        zero = st.sb("zero", [P, 4096]) if zeroes else None
        sums = st.ps("rank_sums", [P, 2 * bins_n])
        loaded, attributed, blank, consts, step, counted, summed, zeroed, cleared = (
            st.sem(f"rank_{x}") for x in ("loaded", "attributes", "blank", "consts", "step", "counted", "summed", "zeroed", "cleared"))
        rec_key = rec[:, :, key].bitcast(I32)
        full, rest = E // TILES, E % TILES
        wide = self.width == REC
        if n == 0:
            src, dst, weight, ea16, ea32 = self.inputs
            column = st.sb("rank_column", [P, 3, TILES])

        def sync_(sync):
            if n:
                sync.dma_start(rec[:, :, :], self.tables[n - 1][0:EP, :].rearrange("(p t) w -> p t w", p=P)).then_inc(loaded, 16)
                return
            sync.wait_ge(blank, 4)
            for a, to in ((src.bitcast(F32), column[:, 0, :]), (dst.bitcast(F32), column[:, 1, :]),
                          (weight, column[:, 2, :])):
                sync.dma_start(to[0:full, :], a[0:full * TILES].rearrange("(p t) -> p t", p=full)).then_inc(loaded, 16)
                sync.dma_start(to[full:full + 1, 0:rest], a[full * TILES:E].rearrange("(p t) -> p t", p=1)).then_inc(loaded, 16)
            if wide:
                for a, to in ((ea16, rec[:, :, EA16:EA16 + 16]), (ea32, rec[:, :, EA32:EA32 + 32])):
                    sync.dma_start(to[0:full, :, :], a[0:full * TILES, :].rearrange("(p t) w -> p t w", p=full)).then_inc(attributed, 16)
                    sync.dma_start(to[full:full + 1, 0:rest, :], a[full * TILES:E, :].rearrange("(p t) w -> p t w", p=1)).then_inc(attributed, 16)
                sync.wait_ge(attributed, 16 * 4)
        n_loads = 1 if n else 6

        def scalar(act):
            act.wait_ge(zeroed, 1)
            act.wait_ge(loaded, 16 * n_loads)
            if wide and n == 0:
                act.wait_ge(attributed, 16 * 4)
            for to, lanes, words in zeroes:
                act.dma_start(to, zero[0:lanes, 0:words]).then_inc(cleared, 16)
            act.wait_ge(cleared, 16 * len(zeroes))

        def pool_(pool):
            if n == 0:
                if wide:
                    pool.memset(rec[:, rest:, :], 0.0).then_inc(blank, 1)
                    pool.memset(rec[:, 0:rest, EA32 + 32:], 0.0).then_inc(blank, 1)
                else:
                    pool.memset(rec[:, :, :], 0.0).then_inc(blank, 2)
                pool.memset(column[:, 0:2, rest:].bitcast(I32), PAD).then_inc(blank, 1)
                pool.memset(column[:, 2, rest:], 0.0).then_inc(blank, 1)
            pool.iota(bins[:, :], pattern=[[1, bins_n]], base=0, channel_multiplier=0,
                      allow_small_or_imprecise_dtypes=True).then_inc(consts, 1)
            pool.memset(ones[:, :], 1.0).then_inc(consts, 1)
            pool.memset(below[:, :], 1.0).then_inc(consts, 1)
            pool.wait_ge(consts, 3)
            pool.affine_select(out=below[:, :], in_=below[:, :], compare_op=ALU.is_gt, fill=0.0, base=0,
                               pattern=[[1, P]], channel_multiplier=-1).then_inc(consts, 1)
            if zeroes:
                pool.memset(zero[:, :], 0.0).then_inc(zeroed, 1)

        def tensor(pe):
            pe.wait_ge(consts, 4)
            pe.wait_ge(counted, 1)
            nc.tensor.matmul(sums[:, 0:bins_n], below[:, :], inbin[:, :], start=True, stop=True)
            nc.tensor.matmul(sums[:, bins_n:], ones[:, :], inbin[:, :], start=True, stop=True).then_inc(summed, 1)

        def vector(dve):
            link = Chain(st, dve, step).link
            dve.wait_ge(consts, 4)
            dve.wait_ge(loaded, 16 * n_loads)
            if n == 0:
                if not wide:
                    dve.wait_ge(blank, 4)
                for at, c in ((SRC, 0), (DST, 1), (WGT, 2)):
                    link(nc.vector.tensor_copy(rec[:, :, at], column[:, c, :]))
            link(nc.vector.tensor_scalar(digit_i[:, :], rec_key, shift, (1 << bits) - 1,
                                         ALU.logical_shift_right, ALU.bitwise_and))
            link(nc.vector.tensor_copy(digit[:, :], digit_i[:, :]))
            link(nc.vector.tensor_tensor(onehot[:, :, :], digit[:, None, :].to_broadcast([P, bins_n, TILES]),
                                         bins[:, :, None].to_broadcast([P, bins_n, TILES]), ALU.is_equal))
            flat1 = onehot[:, :, :].rearrange("p b t -> p (b t)")
            flat2 = count[:, :, :].rearrange("p b t -> p (b t)")
            link(nc.vector.tensor_tensor_scan(flat2, flat1, flat1, 0.0, ALU.add, ALU.max))
            link(nc.vector.tensor_copy(upto[:, :], count[:, :, TILES - 1]))
            nc.vector.tensor_copy(inbin[:, 0:1], upto[:, 0:1])
            nc.vector.tensor_tensor(inbin[:, 1:], upto[:, 1:], upto[:, 0:bins_n - 1], ALU.subtract).then_inc(counted, 1)
            dve.wait_ge(summed, 1)
            link(nc.vector.tensor_tensor_scan(base[:, :], sums[:, bins_n:], bins[:, :], 0.0, ALU.add, ALU.bypass))
            link(nc.vector.tensor_tensor(base[:, :], base[:, :], sums[:, bins_n:], ALU.subtract))
            link(nc.vector.tensor_tensor(base[:, :], base[:, :], sums[:, 0:bins_n], ALU.add))
            link(nc.vector.tensor_tensor(base[:, 1:], base[:, 1:], upto[:, 0:bins_n - 1], ALU.subtract))
            link(nc.vector.tensor_tensor(count[:, :, :], count[:, :, :],
                                         base[:, :, None].to_broadcast([P, bins_n, TILES]), ALU.add))
            link(nc.vector.tensor_tensor(count[:, :, :], count[:, :, :], onehot[:, :, :], ALU.mult))
            link(nc.vector.tensor_reduce(rank[:, :], count[:, :, :].rearrange("p b t -> p t b"), AX.X, ALU.add))
            link(nc.vector.tensor_scalar(rank_i[:, :], rank[:, :], -1.0, None, ALU.add))
        return Work(sync=sync_, scalar=scalar, pool=pool_, tensor=tensor, vector=vector)

    def close(self):
        self.ctx.close()


def broadcast(vector, partitions):
    return vector.rearrange("(a n) -> a n", a=1).to_broadcast([partitions, vector.shape[0]])


def by_chunk(table):
    return table[0:N, :].rearrange("(p c j) w -> p c j w", p=NP, c=CHUNKS)


class Norm:

    def __init__(self, st, nc):
        self.st, self.nc = st, nc
        self.total = [st.sb(f"ln_total{h}", [NP, NC]) for h in (0, 1)]
        self.var = [st.sb(f"ln_var{h}", [NP, NC]) for h in (0, 1)]
        self.centred = [st.sb(f"ln_centred{h}", [NP, NC, D]) for h in (0, 1)]
        self.square = [st.sb(f"ln_square{h}", [NP, NC, D]) for h in (0, 1)]
        self.eps = st.sb("ln_eps", [NP, 1])
        self.is_centred, self.is_squared, self.is_var, self.is_std = (
            st.sem(f"ln_{x}") for x in ("centred", "squared", "var", "std"))

    def centre(self, ch, h, x):
        nc = self.nc
        ch.link(nc.vector.tensor_reduce(self.total[h][:, :], x, AX.X, ALU.add))
        ch.link(nc.vector.tensor_scalar(self.total[h][:, :], self.total[h][:, :], -1.0 / D, None, ALU.mult))
        return nc.vector.tensor_tensor(self.centred[h][:, :, :], x, per_node(self.total[h]), ALU.add).then_inc(self.is_centred, 1)

    def square_up(self, act, i, h):
        self.st.gate(act, self.is_centred, 2 * i + h + 1)
        self.nc.scalar.activation(self.square[h][:, :, :], self.centred[h][:, :, :], ACT.Square).then_inc(self.is_squared, 1)

    def variance(self, ch, i, h):
        self.st.gate(ch.eng, self.is_squared, 2 * i + h + 1)
        self.nc.vector.tensor_reduce(self.var[h][:, :], self.square[h][:, :, :], AX.X, ALU.add).then_inc(self.is_var, 1)

    def root(self, act, i, h):
        self.st.gate(act, self.is_var, 2 * i + h + 1)
        self.nc.scalar.activation(self.var[h][:, :], self.var[h][:, :], ACT.Sqrt, bias=self.eps[:, :],
                                  scale=1.0 / D).then_inc(self.is_std, 1)

    def finish(self, ch, i, h, out):
        nc = self.nc
        self.st.gate(ch.eng, self.is_std, 2 * i + h + 1)
        ch.link(nc.vector.reciprocal(self.var[h][:, :], self.var[h][:, :]))
        return nc.vector.scalar_tensor_tensor(out=out, in0=self.centred[h][:, :, :], scalar=0.0,
                                              in1=per_node(self.var[h]), op0=ALU.max, op1=ALU.mult)


def per_node(t):
    return t[:, :, None].to_broadcast([NP, NC, D])


def slots(eng, chunks, phases, pair=None):
    half = chunks // 2

    def two(i):
        if pair is not None:
            pair(i)
        for h in (0, 1):
            for lag, f in phases:
                chunk = 2 * i + h - lag if isinstance(i, int) else 0
                back = (h - lag) // 2
                if 0 <= chunk < chunks:
                    f(i - -back if back else i, (h - lag) % 2)
    two(0)
    two(1)
    with eng.Fori(2, half) as i:
        two(i)
    for i in range(half, half + -(-max(lag for lag, _ in phases) // 2)):
        two(i)


def pair_counter(ch, chunks):
    half, marks = chunks // 2, []

    def pair(i):
        if isinstance(i, int) and i < 2:
            marks.append(ch.n)
        elif not isinstance(i, int):
            per = ch.n - marks[1]
            ch.n, ch.base = 0, i * per + (marks[1] - per)
            marks[2:] = [per]
        elif i == half:
            ch.n, ch.base = marks[1] + marks[2] * (half - 1), 0
    return pair


def parts_of_chunks(n):
    at = [2 * (k * (CHUNKS // 2) // n) for k in range(n + 1)]
    return [(a, b - a) for a, b in zip(at, at[1:])]


def node_stage(nc, name, part, beside, ins, outs, units, at_once, cols, weights, biases, setup, after=None):
    first_chunk, chunks = part
    st = Stage(nc, f"{name}_{first_chunk}")
    steps = units // at_once
    parts = [(k, n, table, w) for k, (tables, w) in ins.items() for n, table in enumerate(tables)]
    tin = {k: [st.sb(f"in_{k}{h}", [NP, NC, w * len(ts)]) for h in (0, 1)] for k, (ts, w) in ins.items()}
    tout = {k: [st.sb(f"out_{k}{h}", [NP, NC, w]) for h in (0, 1)] for k, (_, w) in outs.items()}
    wt = st.sb("weights", [P, cols])
    bias = {k: st.sb(f"bias_{k}", [P, v.shape[0]]) for k, v in biases.items()}
    ident = st.sb("ident", [P, P])
    turned = [st.sb(f"turned{b}", [P, at_once, NP]) for b in (0, 1)]
    pturn = [st.ps(f"turn{b}", [P, 512]) for b in (0, 1)]
    banks = -(-at_once * cols // 512)
    pout = [st.ps(f"product{b}", [P, banks * 512]) for b in (0, 1)]
    zeroed, const, loaded_w, step = (st.sem(x) for x in ("zeroed", "const", "loaded_w", "dve_step"))
    loaded = [st.sem(f"loaded{h}") for h in (0, 1)]
    stored = {k: [st.sem(f"stored_{k}{h}") for h in (0, 1)] for k in outs}
    ready, moved, copied, done, used = (
        st.sem(x) for x in ("source_ready", "transposed", "copied", "multiplied", "product_used"))

    def arrived(eng, i, h):
        st.gate(eng, loaded[h], (i + 1) * (16 * len(parts)))

    def writable(eng, k, i, h):
        if not (isinstance(i, int) and i == 0):
            st.gate(eng, stored[k][h], i * 16)

    def product(s, eng, i, h):
        st.gate(eng, done, (2 * i + h) * steps + (s + 1))
        return pout[(h * steps + s) % 2][0:NP, 0:at_once * cols]

    hook = setup(st, tin=tin, tout=tout, bias=bias, arrived=arrived, writable=writable, product=product, used=used, ready=ready)
    run_beside = beside(st) if beside else None
    work_after = after(st) if after else None
    n_weights = len(weights) + len(biases)
    block = st.block()
    half = chunks // 2
    src = hook["source"]

    @block.gpsimd
    def _(pool):
        pool.memset(wt[:, :], 0.0).then_inc(zeroed, 1)
        if hook["norm"]:
            pool.memset(hook["norm"].eps[:, :], 1e-5).then_inc(zeroed, 1)
        identity(st, pool, ident, const)
        if work_after:
            work_after.pool(pool)
        if run_beside:
            run_beside(pool)
        if "pool" in hook:
            pool.wait_ge(loaded_w, 16 * n_weights)
            ch = Chain(st, pool, hook["pool_step"])
            slots(pool, chunks, hook["pool"](ch), pair_counter(ch, chunks))

    blanks = 2 if hook["norm"] else 1

    @block.sync
    def _(sync):
        sync.wait_ge(zeroed, blanks)
        for r, c, a in weights:
            sync.dma_start(wt[r:r + a.shape[0], c:c + a.shape[1]], a).then_inc(loaded_w, 16)
        for k, v in biases.items():
            sync.dma_start(bias[k][:, :], broadcast(v, P)).then_inc(loaded_w, 16)

        if "sync_start" in hook:
            hook["sync_start"](sync)

        def load(i, h):
            chunk = 2 * i + h
            if not (isinstance(i, int) and i == 0):
                st.gate(sync, hook["inputs_read"], chunk - 1)
                if hook["turns_inputs"]:
                    st.gate(sync, moved, chunk * steps - steps)
            for k, n, table, w in parts:
                sync.dma_start(tin[k][h][:, :, n * w:(n + 1) * w], by_chunk(table)[:, bass.ds(chunk + first_chunk, 1), :, :]
                               .rearrange("p c j w -> p (c j) w")).then_inc(loaded[h], 16)
        slots(sync, chunks, [(0, load)])
        if work_after:
            work_after.sync(sync)

    @block.scalar
    def _(act):
        act.wait_ge(zeroed, blanks)
        if "scalar_start" in hook:
            hook["scalar_start"](act)

        def copy(s):
            def f(i, h):
                n = (2 * i + h) * steps + s
                b = (h * steps + s) % 2
                st.gate(act, moved, n + 1)
                if not (isinstance(n, int) and n < 2):
                    st.gate(act, done, n - 1)
                nc.scalar.activation(turned[b][:, :, :], pturn[b][:, 0:at_once * NP].rearrange("p (u n) -> p u n", n=NP),
                                     ACT.Copy).then_inc(copied, 1)
            return f

        def store(k):
            def f(i, h):
                st.gate(act, hook["written"][k][0], 2 * i + h + 1)
                act.dma_start(by_chunk(outs[k][0])[:, bass.ds(2 * i + h + first_chunk, 1), :, :].rearrange("p c j w -> p (c j) w"),
                              tout[k][h][:, :, :]).then_inc(stored[k][h], 16)
            return f
        slots(act, chunks, hook["scalar"](act, [copy(s) for s in range(steps)])
              + [(lag, store(k)) for k, (_, lag) in hook["written"].items()])
        for k in outs:
            for h in (0, 1):
                act.wait_ge(stored[k][h], 16 * half)

    @block.tensor
    def _(pe):
        pe.wait_ge(const, 2)
        pe.wait_ge(loaded_w, 16 * n_weights)

        def turn(i, h, s):
            n = (2 * i + h) * steps + s
            b = (h * steps + s) % 2
            if s == 0:
                if hook["turns_inputs"]:
                    arrived(pe, i, h)
                else:
                    st.gate(pe, ready, 2 * i + h + 1)
            if not (isinstance(n, int) and n < 2):
                st.gate(pe, copied, n - 1)
            for u in range(at_once):
                ins_ = nc.tensor.transpose(pturn[b][:, u * NP:(u + 1) * NP], src(h, s * at_once + u), ident[0:NP, 0:NP])
            ins_.then_inc(moved, 1)

        def multiply(i, h, s):
            n = (2 * i + h) * steps + s
            b = (h * steps + s) % 2
            st.gate(pe, copied, n + 1)
            if not (isinstance(n, int) and n < 2):
                st.gate(pe, used, n - 1)
            for u in range(at_once):
                ins_ = nc.tensor.matmul(pout[b][0:NP, u * cols:(u + 1) * cols], turned[b][:, u, :], wt[:, :],
                                        start=True, stop=True)
            ins_.then_inc(done, 1)

        def work(i, h):
            turn(i, h, 0)
            for s in range(steps):
                if s + 1 < steps:
                    turn(i, h, s + 1)
                multiply(i, h, s)
        slots(pe, chunks, [(0, work)])
        if work_after:
            work_after.tensor(pe)

    @block.vector
    def _(dve):
        ch = Chain(st, dve, step)
        dve.wait_ge(loaded_w, 16 * n_weights)
        if "vector_start" in hook:
            hook["vector_start"](dve)
        slots(dve, chunks, hook["vector"](ch), pair_counter(ch, chunks))
        if work_after:
            work_after.vector(dve)
    st.close()


def projection_stage(nc, name, part, beside, ins, p_table, q_table, w_msg, w_skip, b_skip, per_unit, normed, after=None):
    width = P // per_unit

    def setup(st, tin, tout, bias, arrived, writable, product, used, ready):
        hid = [st.sb(f"hidden{h}", [NP, NC, width]) for h in (0, 1)]
        flat = [t[:, :, :].rearrange("p j w -> p (j w)") for t in hid]
        steps, at_once = (2, 4) if normed else (1, 2)
        put = st.sem("outputs_made")
        ln = Norm(st, nc) if normed else None

        def vector(ch):
            def centre(i, h):
                arrived(ch.eng, i, h)
                ln.centre(ch, h, tin["x"][h][:, :, :])

            def finish(i, h):
                ln.finish(ch, i, h, hid[h][:, :, :]).then_inc(ready, 1)

            def hidden(i, h):
                arrived(ch.eng, i, h)
                ch.link(nc.vector.tensor_tensor(hid[h][:, :, :], tin["agg"][h][:, :, :], tin["q"][h][:, :, :], ALU.add))
                nc.vector.tensor_scalar(hid[h][:, :, :], hid[h][:, :, :], 0.0, None, ALU.max).then_inc(ready, 1)

            def take(i, h):
                m = at_once * per_unit
                for k in ("p", "q"):
                    writable(ch.eng, k, i, h)
                for s in range(steps):
                    o = product(s, ch.eng, i, h).rearrange("p (j w) -> p j w", w=32)
                    nc.vector.tensor_copy(tout["p"][h][:, s * m:(s + 1) * m, :], o[:, :, 0:16])
                    nc.vector.tensor_tensor(tout["q"][h][:, s * m:(s + 1) * m, :], o[:, :, 16:32],
                                            bias["skip"][0:NP, None, :].to_broadcast([NP, m, 16]), ALU.add).then_inc(used, 1)
                st.gate(ch.eng, used, (2 * i + h + 1) * steps)
                ch.eng.sem_inc(put, 1)
            return [(0, centre), (1, finish), (0, lambda i, h: ln.variance(ch, i, h)), (2, take)] if normed else [(0, hidden), (1, take)]

        def scalar(act, copies):
            if normed:
                return ([(0, lambda i, h: ln.square_up(act, i, h))] + [(1, f) for f in copies]
                        + [(0, lambda i, h: ln.root(act, i, h))])
            return [(0, f) for f in copies]
        last = 2 if normed else 1
        return {"source": lambda h, u: flat[h][:, u * P:(u + 1) * P], "norm": ln, "turns_inputs": False, "vector": vector,
                "scalar": scalar, "inputs_read": ln.is_centred if normed else ready, "written": {"p": (put, last), "q": (put, last)}}

    weights = [(k * width, k * 32 + c, a) for k in range(per_unit) for c, a in ((0, w_msg), (16, w_skip))]
    node_stage(nc, name, part, beside, ins, {"p": (p_table, 16), "q": (q_table, 16)}, NC // per_unit, 4 if normed else 2,
               32 * per_unit, weights, {"skip": b_skip}, setup, after)


def lin3_stage(nc, part, beside, x, agg, q, w_lin3, b_lin3, x1, h1):
    def setup(st, tin, tout, bias, arrived, writable, product, used, ready):
        ln = Norm(st, nc)
        hid = [st.sb(f"hidden{h}", [NP, NC, 16]) for h in (0, 1)]
        before = [st.sb(f"before{h}", [NP, NC, D]) for h in (0, 1)]
        flat = [t[:, :, :].rearrange("p j w -> p (j w)") for t in hid]
        added, ended = st.sem("x_and_bias"), st.sem("h1_made")

        def vector(ch):
            def prepare(i, h):
                arrived(ch.eng, i, h)
                nc.vector.tensor_tensor(hid[h][:, :, :], tin["agg"][h][:, :, :], tin["q"][h][:, :, :], ALU.add).then_inc(ready, 1)
                nc.vector.tensor_tensor(before[h][:, :, :], tin["x"][h][:, :, :],
                                        bias["lin3"][0:NP, None, :].to_broadcast([NP, NC, D]), ALU.add).then_inc(added, 1)

            def add_up(i, h):
                writable(ch.eng, "x1", i, h)
                prod = product(0, ch.eng, i, h)
                st.gate(ch.eng, added, 2 * i + h + 1)
                nc.vector.tensor_tensor(tout["x1"][h][:, :, :].rearrange("p j w -> p (j w)"),
                                        before[h][:, :, :].rearrange("p j w -> p (j w)"), prod, ALU.add).then_inc(used, 1)
                st.gate(ch.eng, used, 2 * i + h + 1)
                ln.centre(ch, h, tout["x1"][h][:, :, :])

            def finish(i, h):
                writable(ch.eng, "h1", i, h)
                ln.finish(ch, i, h, tout["h1"][h][:, :, :]).then_inc(ended, 1)
            return [(0, prepare), (1, add_up), (2, finish), (1, lambda i, h: ln.variance(ch, i, h))]

        return {"source": lambda h, u: flat[h][:, u * P:(u + 1) * P], "norm": ln, "turns_inputs": False, "vector": vector,
                "scalar": lambda act, copies: ([(0, f) for f in copies] + [(1, lambda i, h: ln.square_up(act, i, h)),
                                                                             (1, lambda i, h: ln.root(act, i, h))]),
                "inputs_read": added, "written": {"x1": (used, 1), "h1": (ended, 2)}}

    node_stage(nc, "lin3", part, beside, {"x": ([x], D), "agg": ([agg], 16), "q": ([q], 16)}, {"x1": (x1, D), "h1": (h1, D)}, 2, 2, 512,
               [(16 * k, D * k, w_lin3) for k in range(8)], {"lin3": b_lin3}, setup)


KEY, PREV, LAST, OWN, OTHER, WEIGHT, WEIGHT2, META = range(8)


def order_stage(nc, name, table, key, other, meta, degree=None):
    st = Stage(nc, name)
    words = st.sb("words", [P, TILES, NARROW])
    following = NextEdge(st, nc)
    m = st.sb("meta", [P, META, TILES])
    mi = m[:, :, :].bitcast(U32)
    nextf, same, bumped = (st.sb(n, [P, TILES]) for n in ("next_f", "same", "bumped"))
    lastp = st.sb("last_partition", [P, 1])
    zero = st.sb("zero", [P, P])
    loaded, zeroed, keyed, step, made, written = (
        st.sem(n) for n in ("loaded", "zeroed", "keyed", "step", "made", "written"))
    if degree is not None:
        words_a, key_a = st.sb("words_a", [P, TILES, NARROW]), st.sb("key_a", [P, TILES])
        after, deg, start, before = st.sb("after", [P, TILES]), st.sb("deg", [P, TILES]), st.sb("start", [P, 1]), st.sb("before", [1, P + 1])
        ident = st.sb("ident", [P, P])
        prow, pcol = st.ps("prow", [P, P]), st.ps("pcol", [P, P])
        const, ends, turned, counted, keyed_a = (st.sem(n) for n in ("const", "ends", "turned", "counted", "keyed_a"))
        pnext = st.ps("pnext", [P, 1])
    block = st.block()
    rows = table[0:EP, :].rearrange("(t p) w -> p t w", p=P)

    @block.gpsimd
    def _(pool):
        following.pool(pool)
        pool.memset(zero[:, :], 0.0).then_inc(zeroed, 1)
        pool.memset(lastp[:, :], 1.0).then_inc(zeroed, 1)
        pool.wait_ge(zeroed, 2)
        pool.affine_select(out=lastp[:, :], in_=lastp[:, :], compare_op=ALU.is_ge, fill=0.0, base=-(P - 1),
                           pattern=[[0, 1]], channel_multiplier=1).then_inc(zeroed, 1)
        if degree is not None:
            pool.iota(after[:, :], pattern=[[1, TILES]], base=1, channel_multiplier=TILES,
                      allow_small_or_imprecise_dtypes=True).then_inc(zeroed, 1)
            identity(st, pool, ident, const)

    @block.sync
    def _(sync):
        with nc.allow_non_contiguous_dma("a few words of each record"):
            sync.dma_start(words[:, :, :], rows[:, :, 0:NARROW]).then_inc(loaded, 16)
            if degree is not None:
                sync.dma_start(words_a[:, :, :], table[0:EP, 0:NARROW].rearrange("(p t) w -> p t w", p=P)).then_inc(loaded, 16)
        sync.wait_ge(made, 1)
        sync.dma_start(meta, m[:, :, :]).then_inc(written, 16)
        if degree is not None:
            sync.wait_ge(counted, 1)
            sync.dma_start(degree.rearrange("(p t) -> p t", p=P), deg[:, :]).then_inc(written, 16)
        sync.wait_ge(written, 16 if degree is None else 32)

    @block.tensor
    def _(pe):
        pe.wait_ge(keyed, 1)
        following.tensor(pe, m[:, KEY, :])
        if degree is None:
            return
        pe.wait_ge(const, 2)
        pe.wait_ge(keyed_a, 1)
        nc.tensor.matmul(pnext[:, 0:1], following.up[:, :], key_a[:, 0:1], start=True, stop=True).then_inc(turned, 1)
        pe.wait_ge(ends, 1)
        nc.tensor.transpose(prow[0:1, 0:P], deg[:, TILES - 1:TILES], ident[:, :]).then_inc(turned, 1)
        pe.wait_ge(ends, 2)
        nc.tensor.transpose(pcol[:, 0:1], before[0:1, 0:P], ident[0:1, 0:1]).then_inc(turned, 1)

    @block.vector
    def _(dve):
        ch = Chain(st, dve, step)
        dve.wait_ge(loaded, 16 if degree is None else 32)
        dve.wait_ge(zeroed, 3 if degree is None else 4)
        nc.vector.tensor_copy(m[:, KEY, :], words[:, :, key].bitcast(I32)).then_inc(keyed, 1)
        dve.wait_ge(keyed, 1)
        if degree is not None:
            nc.vector.tensor_copy(key_a[:, :], words_a[:, :, key].bitcast(I32)).then_inc(keyed_a, 1)
        following.vector(ch, nextf)
        ch.link(nc.vector.tensor_tensor(same[:, :], m[:, KEY, :], nextf[:, :], ALU.is_equal))
        ch.link(nc.vector.scalar_tensor_tensor(out=bumped[:, :], in0=same[:, :], scalar=float(NO_ROW),
                                               in1=m[:, KEY, :], op0=ALU.mult, op1=ALU.add))
        ch.link(nc.vector.tensor_copy(mi[:, LAST, :], bumped[:, :]))
        ch.link(nc.vector.tensor_scalar(mi[:, OWN, :], m[:, KEY, :], float(N - 1), None, ALU.min))
        ch.link(nc.vector.tensor_copy(m[:, WEIGHT, :], words[:, :, WGT]))
        ch.link(nc.vector.tensor_copy(nextf[:, :], words[:, :, other].bitcast(I32)))
        ch.link(nc.vector.tensor_scalar(mi[:, OTHER, :], nextf[:, :], float(N - 1), None, ALU.min))
        ch.link(nc.vector.tensor_scalar(same[:, :], m[:, KEY, :], 1.0, lastp[:, 0:1], ALU.add, ALU.mult))
        ch.link(nc.vector.memset(m[:, PREV, :], -1.0))
        ch.link(nc.vector.memset(m[:, WEIGHT2, :], 0.0))
        nc.vector.tensor_scalar(m[:, PREV, 1:], same[:, 0:TILES - 1], -1.0, None, ALU.add).then_inc(made, 1)
        if degree is None:
            return
        dve.wait_ge(turned, 1)
        dve.wait_ge(keyed_a, 1)
        ch.link(nc.vector.tensor_copy(nextf[:, TILES - 1:TILES], pnext[:, 0:1]))
        ch.link(nc.vector.tensor_copy(nextf[:, 0:TILES - 1], key_a[:, 1:]))
        ch.link(nc.vector.tensor_tensor(same[:, :], key_a[:, :], nextf[:, :], ALU.not_equal))
        ch.link(nc.vector.tensor_tensor(same[:, :], same[:, :], after[:, :], ALU.mult))
        nc.vector.tensor_tensor_scan(deg[:, :], same[:, :], same[:, :], 0.0, ALU.max, ALU.max).then_inc(ends, 1)
        dve.wait_ge(turned, 2)
        ch.link(nc.vector.memset(before[:, :], 0.0))
        nc.vector.tensor_tensor_scan(before[0:1, 1:], prow[0:1, 0:P], zero[0:1, 0:P], 0.0, ALU.max, ALU.max).then_inc(ends, 1)
        dve.wait_ge(turned, 3)
        ch.link(nc.vector.tensor_copy(start[:, :], pcol[:, 0:1]))
        ch.link(nc.vector.tensor_scalar(bumped[:, 1:], deg[:, 0:TILES - 1], start[:, 0:1], None, ALU.max))
        ch.link(nc.vector.tensor_copy(bumped[:, 0:1], start[:, :]))
        nc.vector.tensor_tensor(deg[:, :], after[:, :], bumped[:, :], ALU.subtract).then_inc(counted, 1)
    st.close()


def by_group(table, g, lo, hi, group=GROUP):
    return table[bass.ds(g * (group * P), group * P), lo:hi].rearrange("(j p) w -> p j w", p=P)


def edge_features_stage(nc, by_dst, w_e1, w_e2, b1, b2, eaw1, eaw2, ea32t, zeroes):
    st = Stage(nc, "edge_features")
    attr = [st.sb(f"attr{h}", [P, GROUP, 48]) for h in (0, 1)]
    attr16 = [st.sb(f"attr16_{h}", [P, GROUP * 16]) for h in (0, 1)]
    t16 = [st.sb(f"t16_{h}", [GROUP * 16, P]) for h in (0, 1)]
    t32 = [st.sb(f"t32_{h}", [32, GROUP * P]) for h in (0, 1)]
    o1 = [st.sb(f"o1_{h}", [P, GROUP, 16]) for h in (0, 1)]
    o2 = [st.sb(f"o2_{h}", [P, GROUP, 16]) for h in (0, 1)]
    wt = st.sb("weights", [GROUP * 16, GROUP * 32])
    bias = st.sb("bias", [P, 32])
    ident = st.sb("ident", [P, P])
    p16, p32, pout = ([st.ps(f"{n}_{h}", shape) for h in (0, 1)]
                      for n, shape in (("p16", [P, 512]), ("p32", [32, 1024]), ("pout", [P, 512])))
    zeroed, const, loaded_w, packed, turned, copied, multiplied, added = (
        st.sem(n) for n in ("zeroed", "const", "loaded_w", "packed", "turned", "copied", "multiplied", "added"))
    loaded, stored16, stored32 = ([st.sem(f"{n}{h}") for h in (0, 1)] for n in ("loaded", "stored16_", "stored32_"))
    zero, blank, cleared = st.sb("zero", [P, 4096]), st.sem("zero_tile"), st.sem("cleared")
    block = st.block()

    def unless_first(eng, i, sem, value):
        if not (isinstance(i, int) and i == 0):
            st.gate(eng, sem, value)

    @block.gpsimd
    def _(pool):
        pool.memset(wt[:, :], 0.0).then_inc(zeroed, 1)
        identity(st, pool, ident, const)
        pool.memset(zero[:, :], 0.0).then_inc(blank, 1)
        pool.wait_ge(blank, 1)
        for to, lanes, words in zeroes:
            pool.dma_start(to, zero[0:lanes, 0:words]).then_inc(cleared, 16)
        pool.wait_ge(cleared, 16 * len(zeroes))

    @block.sync
    def _(sync):
        sync.wait_ge(zeroed, 1)
        for j in range(GROUP):
            for c, a in ((0, w_e1), (16, w_e2)):
                sync.dma_start(wt[16 * j:16 * j + 16, 32 * j + c:32 * j + c + 16], a).then_inc(loaded_w, 16)
        sync.dma_start(bias[:, 0:16], broadcast(b1, P)).then_inc(loaded_w, 16)
        sync.dma_start(bias[:, 16:32], broadcast(b2, P)).then_inc(loaded_w, 16)

        def load(i, h):
            unless_first(sync, i, turned, 2 * i + h - 1)
            sync.dma_start(attr[h][:, :, :], by_group(by_dst, 2 * i + h, EA16, EA16 + 48)).then_inc(loaded[h], 16)
        slots(sync, GROUPS, [(0, load)])

    @block.tensor
    def _(pe):
        pe.wait_ge(const, 2)
        pe.wait_ge(loaded_w, 16 * (2 * GROUP + 2))

        def turn(i, h):
            g = 2 * i + h
            st.gate(pe, packed, g + 1)
            unless_first(pe, i, copied, g - 1)
            nc.tensor.transpose(p16[h][0:GROUP * 16, 0:P], attr16[h][:, :], ident[:, :])
            for j in range(GROUP):
                ins = nc.tensor.transpose(p32[h][:, j * P:(j + 1) * P], attr[h][:, j, 16:48], ident[:, :])
            ins.then_inc(turned, 1)

        def multiply(i, h):
            g = 2 * i + h
            st.gate(pe, copied, g + 1)
            unless_first(pe, i, added, g - 1)
            nc.tensor.matmul(pout[h][:, 0:GROUP * 32], t16[h][:, :], wt[:, :], start=True, stop=True).then_inc(multiplied, 1)
        slots(pe, GROUPS, [(0, turn), (1, multiply)])

    @block.scalar
    def _(act):
        def copy(i, h):
            g = 2 * i + h
            st.gate(act, turned, g + 1)
            unless_first(act, i, multiplied, g - 1)
            unless_first(act, i, stored32[h], i * 16)
            nc.scalar.activation(t16[h][:, :], p16[h][0:GROUP * 16, 0:P], ACT.Copy)
            nc.scalar.activation(t32[h][:, :], p32[h][:, 0:GROUP * P], ACT.Copy).then_inc(copied, 1)
            st.gate(act, copied, g + 1)
            act.dma_start(ea32t[:, bass.ds(g * (GROUP * P), GROUP * P)], t32[h][:, :]).then_inc(stored32[h], 16)

        def store(i, h):
            g = 2 * i + h
            st.gate(act, added, g + 1)
            act.dma_start(by_group(eaw1, g, 0, 16), o1[h][:, :, :]).then_inc(stored16[h], 16)
            act.dma_start(by_group(eaw2, g, 0, 16), o2[h][:, :, :]).then_inc(stored16[h], 16)
        slots(act, GROUPS, [(0, copy), (2, store)])
        for h in (0, 1):
            act.wait_ge(stored32[h], 16 * (GROUPS // 2))
            act.wait_ge(stored16[h], 32 * (GROUPS // 2))

    @block.vector
    def _(dve):
        dve.wait_ge(loaded_w, 16 * (2 * GROUP + 2))

        def pack(i, h):
            st.gate(dve, loaded[h], (i + 1) * 16)
            unless_first(dve, i, turned, 2 * i + h - 1)
            nc.vector.tensor_copy(attr16[h][:, :].rearrange("p (j w) -> p j w", w=16), attr[h][:, :, 0:16]).then_inc(packed, 1)

        def add_bias(i, h):
            st.gate(dve, multiplied, 2 * i + h + 1)
            unless_first(dve, i, stored16[h], i * 32)
            o = pout[h][:, 0:GROUP * 32].rearrange("p (j w) -> p j w", w=32)
            for c, t in ((0, o1), (16, o2)):
                ins = nc.vector.tensor_tensor(t[h][:, :, :], o[:, :, c:c + 16],
                                              bias[:, None, c:c + 16].to_broadcast([P, GROUP, 16]), ALU.add)
            ins.then_inc(added, 1)
        slots(dve, GROUPS, [(0, pack), (2, add_bias)])
    st.close()


def edge_stage(nc, name, meta, gathers, gathered, width, setup, scatter=None, add=False):
    st = Stage(nc, name)
    m = st.sb("meta", [P, META, TILES])
    mi = m[:, :, :].bitcast(U32)
    ident = st.sb("ident", [P, P])
    index = [st.sb(f"index{h}", [P, len(gathers), GROUP], U32) for h in (0, 1)]
    to = [st.sb(f"to{h}", [P, GROUP], U32) for h in (0, 1)]
    keyslot = [st.sb(f"keyslot{h}", [P, GROUP]) for h in (0, 1)]
    rows = [st.sb(f"rows{h}", [P, GROUP, gathered]) for h in (0, 1)]
    values = [st.sb(f"values{h}", [P, GROUP, width]) for h in (0, 1)]
    same = [st.sb(f"same{h}", [P, GROUP, P]) for h in (0, 1)]
    carry = [st.sb(f"carry{h}", [P, GROUP, P]) for h in (0, 1)]
    sums = [st.sb(f"sums{h}", [P, GROUP, width]) for h in (0, 1)]
    pkey = st.ps("pkey", [P, 1024])
    psum = [st.ps(f"psum{b}", [P, 512]) for b in (0, 1)]
    (const, loaded_m, idx_ready, to_ready, key_turned, same_made, values_ready, summed, copied, posted, cleared) = (
        st.sem(n) for n in ("const", "loaded_meta", "index_ready", "to_ready", "key_turned", "same_made",
                            "values_ready", "summed", "sum_copied", "posted", "cleared"))
    got = [st.sem(f"gathered{h}") for h in (0, 1)]
    put = [st.sem(f"scattered{h}") for h in (0, 1)]
    half = GROUPS // 2
    per = 16 * GROUP
    hook = setup(st, dict(m=m, rows=rows, values=values, sums=sums, got=got, values_ready=values_ready,
                          per=per * len(gathers), ident=ident, copied=copied, posted=posted, put=put, put_per=per, half=half))
    prep_loads = hook.get("sync_start")
    block = st.block()

    @block.sync
    def _(sync):
        sync.dma_start(m[:, :, :], meta).then_inc(loaded_m, 16)
        if prep_loads:
            prep_loads(sync)
        if "sync" in hook:
            halves(sync, half, lambda i, first, last: [hook["sync"](sync, i, h, first) for h in (0, 1)])
        if "sync_end" in hook:
            hook["sync_end"](sync)

    @block.gpsimd
    def _(pool):
        identity(st, pool, ident, const)
        pool.memset(sums[1][:, GROUP - 1, :], 0.0).then_inc(cleared, 1)
        if "pool_start" in hook:
            hook["pool_start"](pool)

        def gather(i, h, first):
            g = 2 * i + h
            st.gate(pool, idx_ready, g + 1)
            if not first:
                st.gate(pool, values_ready, g - 1)
            for n, (table, _, at, wd) in enumerate(gathers):
                for j in range(GROUP):
                    pool.indirect_dma_start(rows[h][:, j, at:at + wd], None, table,
                                            bass.IndirectOffsetOnAxis(ap=index[h][:, n, j:j + 1], axis=0)).then_inc(got[h], 16)

        def send(i, h):
            g = 2 * i + h
            st.gate(pool, to_ready, g + 1)
            if add:
                st.gate(pool, posted, g + 1)
            else:
                st.gate(pool, copied, (g + 1) * GROUP)
            for j in range(GROUP):
                at = bass.IndirectOffsetOnAxis(ap=to[h][:, j:j + 1], axis=0)
                if add:
                    pool.indirect_dma_start(scatter, at, hook["sent"][h][:, j, :], None, compute_op=ALU.add).then_inc(put[h], 16)
                else:
                    pool.indirect_dma_start(scatter, at, sums[h][:, j, :], None, bounds_check=N - 1,
                                            oob_is_err=False).then_inc(put[h], 16)

        def body(i, first, last):
            for h in (0, 1):
                if not last:
                    gather(i + 1, h, False)
                if scatter is not None:
                    send(i, h)
        for h in (0, 1):
            gather(0, h, True)
        halves(pool, half, body)
        if scatter is not None:
            for h in (0, 1):
                pool.wait_ge(put[h], per * half)

    @block.tensor
    def _(pe):
        pe.wait_ge(const, 2)
        pe.wait_ge(cleared, 1)
        if "pe_start" in hook:
            hook["pe_start"](pe)

        def turn_keys(i, h, first):
            g = 2 * i + h
            st.gate(pe, idx_ready, g + 1)
            if not (first and h == 0):
                st.gate(pe, same_made, g)
            for j in range(GROUP):
                ins = nc.tensor.transpose(pkey[:, j * P:(j + 1) * P], keyslot[h][:, j:j + 1].to_broadcast([P, P]), ident[:, :])
            ins.then_inc(key_turned, 1)

        def sum_up(i, h, first):
            g = 2 * i + h
            st.gate(pe, values_ready, g + 1)
            for j in range(GROUP):
                tile = g * GROUP + j
                b = (h * GROUP + j) % 2
                if not (first and h == 0 and j < 2):
                    st.gate(pe, copied, tile - 1)
                nc.tensor.matmul(psum[b][:, 0:width], same[h][:, j, :], values[h][:, j, :], start=True, stop=False)
                if not (first and h == 0 and j == 0):
                    st.gate(pe, copied, tile)
                before = sums[h][:, j - 1, :] if j else sums[1 - h][:, GROUP - 1, :]
                nc.tensor.matmul(psum[b][:, 0:width], carry[h][:, j, :], before, start=False, stop=True).then_inc(summed, 1)

        def body(i, first, last):
            for h in (0, 1):
                if h == 0:
                    turn_keys(i, 1, first)
                elif not last:
                    turn_keys(i + 1, 0, False)
                if "pe" in hook:
                    hook["pe"](pe, i, h, first)
                if "pe_turn" in hook and not (first and h == 0):
                    hook["pe_turn"](pe, i if h else i - 1, 1 - h, first and h == 1)
                sum_up(i, h, first)
                if "pe_multiply" in hook and not (first and h == 0):
                    hook["pe_multiply"](pe, i if h else i - 1, 1 - h, first and h == 1)
        turn_keys(0, 0, True)
        halves(pe, half, body)
        if "pe_turn" in hook:
            hook["pe_turn"](pe, half - 1, 1, False)
            hook["pe_multiply"](pe, half - 1, 1, False)

    @block.scalar
    def _(act):
        if "act_start" in hook:
            hook["act_start"](act)
        def body(i, first, last):
            for h in (0, 1):
                g = 2 * i + h
                if "act" in hook:
                    hook["act"](act, i, h, first)
                if "act_post" in hook and not (first and h == 0):
                    hook["act_post"](act, i if h else i - 1, 1 - h, first and h == 1)
                if not first:
                    if scatter is not None and not add:
                        st.gate(act, put[h], i * per)
                    if "post" in hook:
                        st.gate(act, posted, g - 1)
                    if "act_reuse" in hook:
                        hook["act_reuse"](act, i, h)
                elif h == 1:
                    act.wait_ge(cleared, 1)
                for j in range(GROUP):
                    st.gate(act, summed, g * GROUP + j + 1)
                    nc.scalar.activation(sums[h][:, j, :], psum[(h * GROUP + j) % 2][:, 0:width], ACT.Copy).then_inc(copied, 1)
        halves(act, half, body)
        if "act_post" in hook:
            hook["act_post"](act, half - 1, 1, False)

    @block.vector
    def _(dve):
        dve.wait_ge(loaded_m, 16)
        if "vector_start" in hook:
            hook["vector_start"](dve)

        def stage(i, h, first):
            g = 2 * i + h
            if not first:
                st.gate(dve, got[h], i * (per * len(gathers)))
                st.gate(dve, key_turned, g - 1)
            for n, (_, row, _, _) in enumerate(gathers):
                nc.vector.tensor_copy(index[h][:, n, :], mi[:, row, bass.ds(g * GROUP, GROUP)])
            nc.vector.tensor_copy(keyslot[h][:, :], m[:, KEY, bass.ds(g * GROUP, GROUP)]).then_inc(idx_ready, 1)

        def stage_to(i, h, first):
            if not first:
                st.gate(dve, put[h], i * per)
            nc.vector.tensor_copy(to[h][:, :], mi[:, LAST, bass.ds((2 * i + h) * GROUP, GROUP)]).then_inc(to_ready, 1)

        def compare(i, h, first):
            g = 2 * i + h
            st.gate(dve, key_turned, g + 1)
            if not first:
                st.gate(dve, summed, (g - 1) * GROUP)
            turned = pkey[:, 0:GROUP * P].rearrange("p (j e) -> p j e", e=P)
            for row, mat in ((KEY, same), (PREV, carry)):
                ins = nc.vector.tensor_tensor(mat[h][:, :, :], turned,
                                              m[:, row, bass.ds(g * GROUP, GROUP)].unsqueeze(2).to_broadcast([P, GROUP, P]),
                                              ALU.is_equal)
            ins.then_inc(same_made, 1)

        def body(i, first, last):
            for h in (0, 1):
                compare(i, h, first)
                if "post" in hook and not first:
                    hook["post"](dve, i - 1, h, isinstance(i, int) and i == 1).then_inc(posted, 1)
                hook["values"](dve, i, h, first).then_inc(values_ready, 1)
                if not last:
                    stage(i + 1, h, False)
                if scatter is not None:
                    stage_to(i, h, first)
        for h in (0, 1):
            stage(0, h, True)
        if "post" in hook:
            body(0, True, False)
            body(1, False, False)
            with dve.Fori(2, half - 1) as i:
                body(i, False, False)
            body(half - 1, False, True)
            for h in (0, 1):
                hook["post"](dve, half - 1, h, False).then_inc(posted, 1)
        else:
            halves(dve, half, body)
    st.close()


def conv_edges(nc, name, meta, p_table, eaw, agg):
    def setup(st, c):
        feat = [st.sb(f"feat{h}", [P, GROUP, 16]) for h in (0, 1)]
        arrived = [st.sem(f"feat_arrived{h}") for h in (0, 1)]

        def sync(eng, i, h, first):
            if not first:
                st.gate(eng, c["values_ready"], 2 * i - 1 + h)
            eng.dma_start(feat[h][:, :, :], by_group(eaw, 2 * i + h, 0, 16)).then_inc(arrived[h], 16)

        def values(dve, i, h, first):
            st.gate(dve, c["got"][h], (i + 1) * c["per"])
            st.gate(dve, arrived[h], (i + 1) * 16)
            return nc.vector.tensor_tensor(c["values"][h][:, :, :], c["rows"][h][:, :, :], feat[h][:, :, :], ALU.add)
        return {"sync": sync, "values": values}
    edge_stage(nc, name, meta, [(p_table, OTHER, 0, 16)], 16, 16, setup, scatter=agg)


def message_edges(nc, meta, h_table, ea32t, w1t, b1, w2t, b2, agg):
    def setup(st, c):
        w_nodes, w_edge, w_out = st.sb("w_nodes", [P, D]), st.sb("w_edge", [32, D]), st.sb("w_out", [D, D])
        bias1, bias2 = st.sb("bias1", [D, 1]), st.sb("bias2", [P, D])
        attr = [st.sb(f"attr{h}", [32, GROUP * P]) for h in (0, 1)]
        ht = st.sb("rows_t", [P, GROUP * P])
        zt = st.sb("hidden_turned", [D, GROUP * P])
        pt = st.ps("turn", [P, 1024])
        pm = st.ps("message", [P, 512])
        arrived = [st.sem(f"attr_arrived{h}") for h in (0, 1)]
        loaded_w, turned, moved, hidden, rectified, done = (
            st.sem(n) for n in ("loaded_w", "rows_turned", "rows_copied", "hidden_done", "rectified", "message_done"))
        cuts = ((0, 512), (512, GROUP * P))

        def sync_start(eng):
            eng.dma_start(w_nodes[:, :], w1t[0:P, :]).then_inc(loaded_w, 16)
            eng.dma_start(w_edge[:, :], w1t[P:P + 32, :]).then_inc(loaded_w, 16)
            eng.dma_start(w_out[:, :], w2t).then_inc(loaded_w, 16)
            eng.dma_start(bias1[:, :], b1.rearrange("(n a) -> n a", a=1)).then_inc(loaded_w, 16)
            eng.dma_start(bias2[:, :], broadcast(b2, P)).then_inc(loaded_w, 16)

        def sync(eng, i, h, first):
            if not first:
                st.gate(eng, hidden, 2 * i - 1 + h)
            eng.dma_start(attr[h][:, :], ea32t[:, bass.ds((2 * i + h) * (GROUP * P), GROUP * P)]).then_inc(arrived[h], 16)

        def pe(eng, i, h, first):
            g, start = 2 * i + h, first and h == 0
            st.gate(eng, c["got"][h], (i + 1) * c["per"])
            if not start:
                st.gate(eng, rectified, g)
            for j in range(GROUP):
                ins = nc.tensor.transpose(pt[:, j * P:(j + 1) * P], c["rows"][h][:, j, :], c["ident"][:, :])
            ins.then_inc(turned, 1)
            st.gate(eng, moved, g + 1)
            st.gate(eng, arrived[h], (i + 1) * 16)
            for a, b in cuts:
                nc.tensor.matmul(pt[0:D, a:b], w_nodes[:, :], ht[:, a:b], start=True, stop=False)
                ins = nc.tensor.matmul(pt[0:D, a:b], w_edge[:, :], attr[h][:, a:b], start=False, stop=True)
            ins.then_inc(hidden, 1)
            st.gate(eng, rectified, g + 1)
            if not start:
                st.gate(eng, c["values_ready"], g)
            for j in range(GROUP):
                ins = nc.tensor.matmul(pm[:, j * D:(j + 1) * D], zt[:, j * P:(j + 1) * P], w_out[:, :], start=True, stop=True)
            ins.then_inc(done, 1)

        def act(eng, i, h, first):
            g = 2 * i + h
            st.gate(eng, turned, g + 1)
            for a, b in cuts:
                ins = nc.scalar.activation(ht[:, a:b], pt[:, a:b], ACT.Copy)
            ins.then_inc(moved, 1)
            st.gate(eng, hidden, g + 1)
            if not (first and h == 0):
                st.gate(eng, done, g)
            for a, b in cuts:
                ins = nc.scalar.activation(zt[:, a:b], pt[0:D, a:b], ACT.Relu, bias=bias1[:, :])
            ins.then_inc(rectified, 1)

        def values(eng, i, h, first):
            st.gate(eng, done, 2 * i + h + 1)
            return nc.vector.tensor_tensor(c["values"][h][:, :, :], pm[:, 0:GROUP * D].rearrange("p (j w) -> p j w", w=D),
                                           bias2[:, None, :].to_broadcast([P, GROUP, D]), ALU.add)
        wait_w = lambda eng: eng.wait_ge(loaded_w, 16 * 5)
        return {"sync_start": sync_start, "sync": sync, "pe": pe, "pe_start": wait_w, "act_start": wait_w,
                "act": act, "vector_start": wait_w, "values": values}
    edge_stage(nc, "messages", meta, [(h_table, OTHER, 0, D), (h_table, OWN, D, D)], P, D, setup, scatter=agg)


def gru_stage(nc, part, beside, x1, h1, agg, w_iht, w_hht, b_ih, b_hh, x2, h2):
    def setup(st, tin, tout, bias, arrived, writable, product, used, ready):
        ln = Norm(st, nc)
        gates = [st.sb(f"gates{h}", [NP, NC, 4 * D]) for h in (0, 1)]
        new = [st.sb(f"new{h}", [NP, NC, D]) for h in (0, 1)]
        rest = [st.sb(f"rest{h}", [NP, NC, D]) for h in (0, 1)]
        kept = [st.sb(f"kept{h}", [NP, NC, D]) for h in (0, 1)]
        both = st.sb("bias_both", [NP, 4 * D])
        flipped, opened, z_open, pre, tanhed, bstep, read, mixed, ended = (st.sem(n) for n in (
            "z_flipped", "r_open", "z_open", "new_before", "new_done", "bias_step", "inputs_read", "x2_made", "h2_made"))

        def vector_start(dve):
            ch = Chain(st, dve, bstep)
            ch.link(nc.vector.tensor_tensor(both[:, 0:2 * D], bias["ih"][0:NP, 0:2 * D], bias["hh"][0:NP, 0:2 * D], ALU.add))
            ch.link(nc.vector.tensor_copy(both[:, 2 * D:3 * D], bias["ih"][0:NP, 2 * D:3 * D]))
            ch.link(nc.vector.tensor_copy(both[:, 3 * D:4 * D], bias["hh"][0:NP, 2 * D:3 * D]))

        def vector(ch):
            def gather_gates(steps):
                def f(i, h):
                    for s in steps:
                        nc.vector.tensor_tensor(gates[h][:, 4 * s:4 * s + 4, :],
                                                product(s, ch.eng, i, h).rearrange("p (u w) -> p u w", u=4),
                                                both[:, None, :].to_broadcast([NP, 4, 4 * D]), ALU.add).then_inc(used, 1)
                return f

            def open_gates(i, h):
                g, chunk = gates[h], 2 * i + h
                arrived(ch.eng, i, h)
                st.gate(ch.eng, opened, chunk + 1)
                ch.link(nc.vector.tensor_tensor(new[h][:, :, :], g[:, :, 0:D], g[:, :, 3 * D:4 * D], ALU.mult))
                nc.vector.tensor_tensor(new[h][:, :, :], new[h][:, :, :], g[:, :, 2 * D:3 * D], ALU.add).then_inc(pre, 1)
                st.gate(ch.eng, z_open, chunk + 1)
                ch.link(nc.vector.tensor_tensor(kept[h][:, :, :], tin["state"][h][:, :, 0:D], g[:, :, D:2 * D], ALU.mult))
                nc.vector.tensor_tensor(kept[h][:, :, :], kept[h][:, :, :], tin["x1"][h][:, :, :], ALU.add).then_inc(read, 1)

            def mix(i, h):
                chunk = 2 * i + h
                writable(ch.eng, "x2", i, h)
                st.gate(ch.eng, tanhed, chunk + 1)
                st.gate(ch.eng, read, chunk + 1)
                ch.link(nc.vector.tensor_tensor(new[h][:, :, :], new[h][:, :, :], rest[h][:, :, :], ALU.mult))
                nc.vector.tensor_tensor(tout["x2"][h][:, :, :], new[h][:, :, :], kept[h][:, :, :], ALU.add).then_inc(mixed, 1)
                st.gate(ch.eng, mixed, chunk + 1)
                ln.centre(ch, h, tout["x2"][h][:, :, :])

            def finish(i, h):
                writable(ch.eng, "h2", i, h)
                ln.finish(ch, i, h, tout["h2"][h][:, :, :]).then_inc(ended, 1)
            return [(1, gather_gates((0, 1))), (2, mix), (1, gather_gates((2, 3))), (2, lambda i, h: ln.variance(ch, i, h)),
                    (1, open_gates), (2, finish)]

        def scalar(act, copies):
            def open_gates(i, h):
                chunk = 2 * i + h
                st.gate(act, used, (chunk + 1) * len(copies))
                nc.scalar.activation(gates[h][:, :, 0:D], gates[h][:, :, 0:D], ACT.Sigmoid).then_inc(opened, 1)
                nc.scalar.activation(rest[h][:, :, :], gates[h][:, :, D:2 * D], ACT.Sigmoid, scale=-1.0).then_inc(flipped, 1)
                st.gate(act, flipped, chunk + 1)
                nc.scalar.activation(gates[h][:, :, D:2 * D], gates[h][:, :, D:2 * D], ACT.Sigmoid).then_inc(z_open, 1)

            def tanh(i, h):
                st.gate(act, pre, 2 * i + h + 1)
                nc.scalar.activation(new[h][:, :, :], new[h][:, :, :], ACT.Tanh).then_inc(tanhed, 1)
            return [(1, copies[2]), (1, copies[3]), (2, lambda i, h: ln.square_up(act, i, h)), (0, copies[0]), (0, copies[1]),
                    (1, open_gates), (2, lambda i, h: ln.root(act, i, h)), (1, tanh)]
        return {"source": lambda h, u: tin["state"][h][:, u, :], "norm": ln, "turns_inputs": True, "vector_start": vector_start,
                "vector": vector, "scalar": scalar, "inputs_read": read, "written": {"x2": (mixed, 2), "h2": (ended, 2)}}
    node_stage(nc, "gru", part, beside, {"state": ([h1, agg], D), "x1": ([x1], D)}, {"x2": (x2, D), "h2": (h2, D)}, NC, 4, 4 * D,
               [(0, 0, w_hht[:, 0:2 * D]), (0, 3 * D, w_hht[:, 2 * D:3 * D]), (D, 0, w_iht)],
               {"ih": b_ih, "hh": b_hh}, setup)


def cheb_weights_work(nc, w, taylor):
    def attach(st):
        terms = w.shape[0]
        wk, v = st.sb("cheb_w", [D, terms, D]), st.sb("cheb_taylor", [D, terms, D])
        loaded, step, stored = st.sem("cheb_loaded"), st.sem("cheb_step"), st.sem("cheb_stored")

        def sync(sync):
            sync.dma_start(wk[:, :, :], w.rearrange("k i o -> i k o")).then_inc(loaded, 16)
            sync.wait_ge(step, terms * (terms + 1) // 2)
            sync.dma_start(taylor.rearrange("(k i) o -> i k o", i=D), v[:, :, :]).then_inc(stored, 16)
            sync.wait_ge(stored, 16)

        def vector(dve):
            ch = Chain(st, dve, step)
            dve.wait_ge(loaded, 16)
            for j in range(terms):
                for k in range(j, terms):
                    c = (-1) ** (k - j) * comb(k, j) / factorial(k)
                    if k == j:
                        ch.link(nc.vector.tensor_scalar(v[:, j, :], wk[:, k, :], c, None, ALU.mult))
                    else:
                        ch.link(nc.vector.scalar_tensor_tensor(out=v[:, j, :], in0=wk[:, k, :], scalar=c, in1=v[:, j, :],
                                                               op0=ALU.mult, op1=ALU.add))
        return Work(sync=sync, vector=vector)
    return attach


def cheb_stage(nc, x2, h2, agg, info, w0, bias_, h3, out):
    def setup(st, tin, tout, bias, arrived, writable, product, used, ready):
        ln = Norm(st, nc)
        flat = [t[:, :, :].rearrange("p j w -> p (j w)") for t in tin["h2"]]
        part = [st.sb(f"part{h}", [NP, NC, D]) for h in (0, 1)]
        x3 = [st.sb(f"x3_{h}", [NP, NC, D]) for h in (0, 1)]
        degrees, rate = st.sb("degrees", [NP, N // NP, 2]), st.sb("rate", [NP, N // NP])
        given, clamped, rooted, rate_ready = (st.sem(n) for n in ("degrees_given", "degree_clamped", "degree_rooted", "rate_ready"))
        scaled, read, ended, made, pool_step = (
            st.sem(n) for n in ("agg_scaled", "inputs_read", "h3_made", "out_made", "pool_step"))
        steps = 2

        def pool(ch):
            def prepare(i, h):
                arrived(ch.eng, i, h)
                if not (isinstance(i, int) and i == 0):
                    st.gate(ch.eng, used, (2 * i + h) * steps - steps)
                ch.eng.wait_ge(rate_ready, 1)
                rates = rate[:, bass.ds((2 * i + h) * NC, NC)].unsqueeze(2).to_broadcast([NP, NC, D])
                ch.link(ch.eng.tensor_tensor(part[h][:, :, :], tin["agg"][h][:, :, :], rates, ALU.mult))
                ch.eng.tensor_tensor(part[h][:, :, :], part[h][:, :, :],
                                     bias["cheb"][0:NP, None, :].to_broadcast([NP, NC, D]), ALU.add).then_inc(scaled, 1)

            def total(i, h):
                writable(ch.eng, "out", i, h)
                st.gate(ch.eng, ended, 2 * i + h + 1)
                ch.eng.tensor_tensor(tout["out"][h][:, :, :], x3[h][:, :, :], tout["h3"][h][:, :, :], ALU.add).then_inc(made, 1)
            return [(0, prepare), (2, total)]

        def vector(ch):
            def add_up(i, h):
                st.gate(ch.eng, scaled, 2 * i + h + 1)
                nc.vector.tensor_tensor(part[h][:, :, :], part[h][:, :, :], tin["x2"][h][:, :, :], ALU.add).then_inc(read, 1)
                st.gate(ch.eng, read, 2 * i + h + 1)
                if not (isinstance(i, int) and i == 0):
                    st.gate(ch.eng, made, 2 * i + h - 1)
                for s in range(steps):
                    cut = lambda t: t[h][:, 8 * s:8 * s + 8, :].rearrange("p j w -> p (j w)")
                    nc.vector.tensor_tensor(cut(x3), cut(part), product(s, ch.eng, i, h), ALU.add).then_inc(used, 1)
                st.gate(ch.eng, used, (2 * i + h + 1) * steps)
                ln.centre(ch, h, x3[h][:, :, :])

            def finish(i, h):
                writable(ch.eng, "h3", i, h)
                if not (isinstance(i, int) and i == 0):
                    st.gate(ch.eng, made, 2 * i + h - 1)
                ln.finish(ch, i, h, tout["h3"][h][:, :, :]).then_inc(ended, 1)
            return [(1, add_up), (2, finish), (1, lambda i, h: ln.variance(ch, i, h))]

        def sync_start(sync):
            sync.dma_start(degrees[:, :, :], info.rearrange("(p n) w -> p n w", p=NP)).then_inc(given, 16)

        def vector_start(dve):
            dve.wait_ge(given, 16)
            nc.vector.tensor_scalar(rate[:, :], degrees[:, :, 1], 1.0, None, ALU.max).then_inc(clamped, 1)
            dve.wait_ge(rooted, 1)
            nc.vector.reciprocal(rate[:, :], rate[:, :]).then_inc(rate_ready, 1)

        def scalar_start(act):
            act.wait_ge(clamped, 1)
            nc.scalar.activation(rate[:, :], rate[:, :], ACT.Sqrt).then_inc(rooted, 1)
        return {"source": lambda h, u: flat[h][:, u * P:(u + 1) * P], "norm": ln, "turns_inputs": True, "vector": vector,
                "pool": pool, "pool_step": pool_step, "sync_start": sync_start, "vector_start": vector_start, "scalar_start": scalar_start,
                "scalar": lambda act, copies: ([(0, f) for f in copies] + [(1, lambda i, h: ln.square_up(act, i, h)),
                                                                             (1, lambda i, h: ln.root(act, i, h))]),
                "inputs_read": read, "written": {"h3": (ended, 2), "out": (made, 2)}}
    node_stage(nc, "cheb", (0, CHUNKS), None, {"h2": ([h2], D), "x2": ([x2], D), "agg": ([agg], D)}, {"h3": (h3, D), "out": (out, D)},
               NC // 2, 4, 2 * D, [(0, 0, w0), (D, D, w0)], {"cheb": bias_}, setup)


CHEB_K = 10
SUBSTEPS, SERIES = 4, 20
EXPM_K = SUBSTEPS * SERIES
assert CHEB_K % 2 == 0 and EXPM_K % 2 == 0

LIST = 8
BODY = 2 * GROUP * P
BODIES = EP // BODY
FEW = 2
FINE = 2 * FEW * P
FINES = EP // FINE
NEST = 7
assert FINES % NEST == 0 and FINES * FINE == EP
ZERO_ROW = EP


def rounds(st, eng, bodies, body):
    with eng.Fori(0, BODIES) as i:
        with nullcontext() if isinstance(bodies, int) else eng.If(i < bodies):
            body(i)


def fine_rounds(eng, fine, body):
    with eng.Fori(0, FINES // NEST) as i:
        with eng.If(i * NEST < fine):
            with eng.Fori(0, NEST) as j:
                with eng.If(i * NEST + j < fine):
                    body(i * NEST + j)


def link_stage(nc, name, source, info, bodies_in, meta, next_list, bodies_out):
    st = Stage(nc, name)
    m = st.sb("meta", [P, META, TILES])
    mi = m[:, :, :].bitcast(U32)
    nxt, dst, same, low, last, pos, flag, tmp, rank = (
        st.sb(n, [P, TILES]) for n in ("next", "dst", "same", "low", "last", "pos", "flag", "tmp", "rank"))
    pointer, deg, npos = (st.sb(n, [P, TILES]) for n in ("pointer", "deg", "npos"))
    at_node, at_dst, at_rank = (st.sb(n, [P, TILES], U32) for n in ("at_node", "at_dst", "at_rank"))
    pair, found = st.sb("pair", [P, TILES, 2]), st.sb("found", [P, TILES, 2])
    rec = st.sb("records", [P, TILES, LIST])
    blank = st.sb("blank", [P, TILES, LIST])
    blank_info = st.sb("blank_info", [NP, N // NP, 2])
    slot_i = [st.sb(f"slot_i{h}", [P, GROUP], U32) for h in (0, 1)]
    slot_r = [st.sb(f"slot_r{h}", [P, GROUP, LIST]) for h in (0, 1)]
    slot_2 = [st.sb(f"slot_2{h}", [P, GROUP, 2]) for h in (0, 1)]
    lastp = st.sb("last_partition", [P, 1])
    below, ones = st.sb("below", [P, P]), st.sb("ones", [P, P])
    starts, counted, total = st.sb("starts", [P, BODIES + FINES]), st.sb("counted", [P, BODIES + FINES]), st.sb("total", [P, 1])
    bodies_f, bodies_i, given = st.sb("bodies_f", [P, 2]), st.sb("bodies_i", [P, 2], I32), st.sb("given", [1, 2], I32)
    pranks, ptotals = st.ps("ranks", [P, TILES]), st.ps("totals", [P, TILES])
    staged, moves = ([st.sem(f"{n}{h}") for h in (0, 1)] for n in ("staged", "moves"))
    loaded, const, step, cleared, flagged, ranked, rooted, made, stored, keyed = (
        st.sem(n) for n in ("loaded", "const", "step", "cleared", "flagged", "ranked",
                            "rooted", "made", "stored", "keyed"))
    block = st.block()
    n_loads = 2
    given_rec = st.sb("given_records", [P, TILES, LIST])
    following = NextEdge(st, nc)

    def load(sync):
        rows = source[0:EP, :].rearrange("(t p) w -> p t w", p=P)
        sync.dma_start(given_rec[:, :, :], rows).then_inc(loaded, 16)
        sync.dma_start(given[:, :], bodies_in).then_inc(loaded, 16)

    def fill_and_store(sync):
        sync.dma_start(info.rearrange("(p n) w -> p n w", p=NP), blank_info[:, :, :]).then_inc(cleared, 16)
        if next_list is not None:
            sync.dma_start(next_list.rearrange("(t p) w -> p t w", p=P), blank[:, :, :]).then_inc(cleared, 16)
        sync.wait_ge(made, 1)
        sync.dma_start(meta, m[:, :, :]).then_inc(stored, 16)
        if next_list is not None:
            sync.wait_ge(made, 2)
            sync.dma_start(bodies_out, bodies_i[0:1, :]).then_inc(stored, 16)
        sync.wait_ge(stored, 16 if next_list is None else 32)

    @block.sync
    def _(sync):
        load(sync)
        sync.wait_ge(const, 9)
        fill_and_store(sync)

    passes = 2 if next_list is None else 3

    @block.gpsimd
    def _(pool):
        following.pool(pool)
        pool.memset(lastp[:, :], 1.0).then_inc(const, 1)
        pool.memset(ones[:, :], 1.0).then_inc(const, 1)
        pool.memset(below[:, :], 1.0).then_inc(const, 1)
        pool.memset(blank[:, :, :], 0.0).then_inc(const, 1)
        pool.memset(blank_info[:, :, :], 0.0).then_inc(const, 1)
        pool.iota(pos[:, :], pattern=[[P, TILES]], base=0, channel_multiplier=1,
                  allow_small_or_imprecise_dtypes=True).then_inc(const, 1)
        pool.iota(starts[:, 0:BODIES], pattern=[[BODY, BODIES]], base=0, channel_multiplier=0,
                  allow_small_or_imprecise_dtypes=True)
        pool.iota(starts[:, BODIES:], pattern=[[FINE, FINES]], base=0, channel_multiplier=0,
                  allow_small_or_imprecise_dtypes=True).then_inc(const, 1)
        pool.wait_ge(const, 7)
        pool.affine_select(out=below[:, :], in_=below[:, :], compare_op=ALU.is_gt, fill=0.0, base=0,
                           pattern=[[1, P]], channel_multiplier=-1).then_inc(rooted, 1)
        pool.affine_select(out=lastp[:, :], in_=lastp[:, :], compare_op=ALU.is_ge, fill=0.0, base=-(P - 1),
                           pattern=[[0, 1]], channel_multiplier=1).then_inc(rooted, 1)
        pool.memset(blank[:, :, 0:2], float(PAD)).then_inc(rooted, 1)
        pool.memset(blank[:, :, 4:5], float(ZERO_ROW)).then_inc(rooted, 1)
        pool.memset(blank_info[:, :, 0:1], float(ZERO_ROW)).then_inc(rooted, 1)
        pool.wait_ge(rooted, 5)
        pool.sem_inc(const, 2)
        pool.wait_ge(loaded, 16 * n_loads)
        bodies = pool.value_load(given[0:1, 0:1], min_val=1, max_val=BODIES)
        pool.wait_ge(cleared, 16 if next_list is None else 32)
        for n in range(passes):
            def move(i):
                c = i + bodies * n
                for h in (0, 1):
                    st.gate(pool, staged[h], c + 1)
                    for j in range(GROUP):
                        at = bass.IndirectOffsetOnAxis(ap=slot_i[h][:, j:j + 1], axis=0)
                        if n == 0:
                            pool.indirect_dma_start(info, at, slot_2[h][:, j, :], None, bounds_check=N - 1,
                                                    oob_is_err=False).then_inc(moves[h], 16)
                        elif n == 1:
                            pool.indirect_dma_start(slot_2[h][:, j, :], None, info, at).then_inc(moves[h], 16)
                        else:
                            pool.indirect_dma_start(next_list, at, slot_r[h][:, j, :], None, bounds_check=EP - 1,
                                                    oob_is_err=False).then_inc(moves[h], 16)
            rounds(st, pool, bodies, move)
            for h in (0, 1):
                st.gate(pool, moves[h], bodies * ((n + 1) * (16 * GROUP)))

    @block.tensor
    def _(pe):
        pe.wait_ge(keyed, 1)
        following.tensor(pe, m[:, KEY, :])
        if next_list is None:
            return
        pe.wait_ge(rooted, 5)
        pe.wait_ge(flagged, 1)
        nc.tensor.matmul(pranks[:, :], below[:, :], flag[:, :], start=True, stop=True)
        nc.tensor.matmul(ptotals[:, :], ones[:, :], flag[:, :], start=True, stop=True).then_inc(ranked, 1)

    @block.vector
    def _(dve):
        ch = Chain(st, dve, step)
        link, v = ch.link, nc.vector
        dve.wait_ge(loaded, 16 * n_loads)
        dve.wait_ge(rooted, 5)
        bodies = dve.value_load(given[0:1, 0:1], min_val=1, max_val=BODIES)
        v.tensor_copy(m[:, KEY, :], given_rec[:, :, 0]).then_inc(keyed, 1)
        for to, w in ((dst[:, :], 1), (m[:, WEIGHT, :], 2), (m[:, WEIGHT2, :], 3), (pointer[:, :], 4)):
            link(v.tensor_copy(to, given_rec[:, :, w]))
        following.vector(ch, nxt)
        dve.wait_ge(keyed, 1)
        link(v.tensor_tensor(last[:, :], m[:, KEY, :], nxt[:, :], ALU.not_equal))
        link(v.tensor_scalar(same[:, :], m[:, KEY, :], 1.0, lastp[:, 0:1], ALU.add, ALU.mult))
        link(v.memset(m[:, PREV, 0:1], -1.0))
        link(v.tensor_scalar(m[:, PREV, 1:], same[:, 0:TILES - 1], -1.0, None, ALU.add))
        link(v.memset(deg[:, :], 0.0))
        link(v.tensor_copy(mi[:, OTHER, :], pointer[:, :]))
        link(v.tensor_scalar(low[:, :], m[:, KEY, :], float(N), None, ALU.is_lt))
        link(v.tensor_tensor(last[:, :], last[:, :], low[:, :], ALU.mult))
        link(v.tensor_scalar(npos[:, :], pos[:, :], float(N), None, ALU.add))
        link(v.tensor_tensor(tmp[:, :], m[:, KEY, :], npos[:, :], ALU.subtract))
        link(v.tensor_tensor(tmp[:, :], tmp[:, :], last[:, :], ALU.mult))
        link(v.tensor_tensor(tmp[:, :], tmp[:, :], npos[:, :], ALU.add))
        link(v.tensor_copy(mi[:, LAST, :], tmp[:, :]))
        link(v.tensor_scalar(tmp[:, :], m[:, KEY, :], -float(NO_ROW), None, ALU.add))
        link(v.tensor_tensor(tmp[:, :], tmp[:, :], last[:, :], ALU.mult))
        link(v.tensor_scalar(at_node[:, :], tmp[:, :], float(NO_ROW), None, ALU.add))
        link(v.tensor_scalar(at_dst[:, :], dst[:, :], float(N - 1), None, ALU.min))
        link(v.tensor_copy(pair[:, :, 0], pos[:, :]))
        link(v.tensor_copy(pair[:, :, 1], deg[:, :]))

        def send(index, rows, slots, n):
            def body(i):
                c = i + bodies * n
                for h in (0, 1):
                    if n:
                        st.gate(dve, moves[h], c * (16 * GROUP))
                    else:
                        with dve.If(i > 0):
                            st.gate(dve, moves[h], c * (16 * GROUP))
                    g = (2 * i + h) * GROUP
                    ins = v.tensor_copy(slot_i[h][:, :], index[:, bass.ds(g, GROUP)])
                    if rows is not None:
                        ins = v.tensor_copy(slots[h][:, :, :], rows[:, bass.ds(g, GROUP), :])
                    ins.then_inc(staged[h], 1)
                if rows is None:
                    for h in (0, 1):
                        st.gate(dve, moves[h], (c + 1) * (16 * GROUP))
                        ins = v.tensor_copy(found[:, bass.ds((2 * i + h) * GROUP, GROUP), :], slot_2[h][:, :, :])
                    ch.n, ch.base = 0, i + after_head
                    link(ins)
            rounds(st, dve, bodies, body)

        send(at_node, pair, slot_2, 0)
        after_head = ch.n
        link(v.memset(found[:, :, 1:2], 0.0))
        link(v.memset(found[:, :, 0:1], float(ZERO_ROW)))
        after_head = ch.n
        send(at_dst, None, None, 1)
        ch.n, ch.base = after_head, bodies
        link(v.tensor_copy(m[:, OWN, :].bitcast(U32), found[:, :, 0]))
        link(v.tensor_scalar(flag[:, :], found[:, :, 0], float(ZERO_ROW), None, ALU.is_lt))
        v.tensor_tensor(flag[:, :], flag[:, :], low[:, :], ALU.mult).then_inc(flagged, 1)
        if next_list is not None:
            link(v.tensor_copy(rec[:, :, 3], m[:, WEIGHT2, :]))
        dve.sem_inc(made, 1)
        if next_list is None:
            return
        link(v.memset(rec[:, :, 5:LIST], 0.0))
        for w, a in ((0, m[:, KEY, :]), (1, dst[:, :]), (2, m[:, WEIGHT, :]), (4, found[:, :, 0])):
            link(v.tensor_copy(rec[:, :, w], a))
        dve.wait_ge(ranked, 1)
        link(v.tensor_tensor_scan(rank[:, :], ptotals[:, :], pos[:, :], 0.0, ALU.add, ALU.bypass))
        link(v.tensor_copy(total[:, :], rank[:, TILES - 1:TILES]))
        link(v.tensor_tensor(rank[:, :], rank[:, :], ptotals[:, :], ALU.subtract))
        link(v.tensor_tensor(rank[:, :], rank[:, :], pranks[:, :], ALU.add))
        link(v.tensor_scalar(rank[:, :], rank[:, :], -float(NO_ROW), None, ALU.add))
        link(v.tensor_tensor(rank[:, :], rank[:, :], flag[:, :], ALU.mult))
        link(v.tensor_scalar(at_rank[:, :], rank[:, :], float(NO_ROW), None, ALU.add))
        link(v.tensor_scalar(counted[:, :], starts[:, :], total[:, 0:1], None, ALU.is_lt))
        link(v.tensor_reduce(bodies_f[:, 0:1], counted[:, 0:BODIES], AX.X, ALU.add))
        link(v.tensor_reduce(bodies_f[:, 1:2], counted[:, BODIES:], AX.X, ALU.add))
        link(v.tensor_scalar(bodies_i[:, :], bodies_f[:, :], 1.0, None, ALU.max))
        dve.sem_inc(made, 1)
        send(at_rank, rec, slot_r, 2)
    st.close()


class FirstLink:

    def __init__(self, nc, source, degree, info, meta, next_list, bodies_out):
        self.nc, self.source, self.degree, self.info, self.meta = nc, source, degree, info, meta
        self.next_list, self.bodies_out = next_list, bodies_out
        self.ctx = ExitStack()
        sb = lambda n, shape, dt=F32: self.ctx.enter_context(nc.sbuf_tensor(f"link1_{n}", shape, dt))
        self.m, self.rec, self.low = sb("meta", [P, META, TILES]), sb("records", [P, TILES, LIST]), sb("low", [P, TILES])
        self.pair, self.found = sb("pair", [P, TILES, 2]), sb("found", [P, TILES, 2])
        self.at_node, self.at_dst, self.at_rank = (sb(n, [P, TILES], U32) for n in ("at_node", "at_dst", "at_rank"))

    def announce(self):
        return scatter_rows(self.nc, self.at_node, self.pair, 2, self.info, N - 1)

    def find(self):
        return gather_rows(self.nc, self.at_dst, self.found, 2, self.info)

    def list_up(self):
        return scatter_rows(self.nc, self.at_rank, self.rec, LIST, self.next_list, EP - 1)

    def begin(self):
        nc, m, low = self.nc, self.m, self.low
        st = Stage(nc, "link1_begin")
        mi = m[:, :, :].bitcast(U32)
        tmp, last, pos, npos, deg = (st.sb(n, [P, TILES]) for n in ("tmp", "last", "pos", "npos", "deg"))
        blank, blank_info = st.sb("blank", [P, TILES, LIST]), st.sb("blank_info", [NP, N // NP, 2])
        loaded, const, filled, step, cleared = (st.sem(n) for n in ("loaded", "const", "filled", "step", "cleared"))
        block = st.block()

        @block.sync
        def _(sync):
            sync.dma_start(m[:, :, :], self.source).then_inc(loaded, 16)
            with nc.allow_non_contiguous_dma("one word of each record"):
                sync.dma_start(deg[:, :], self.degree.rearrange("(t p) -> p t", p=P)).then_inc(loaded, 16)
            sync.wait_ge(filled, 3)
            sync.dma_start(self.info.rearrange("(p n) w -> p n w", p=NP), blank_info[:, :, :]).then_inc(cleared, 16)
            sync.dma_start(self.next_list.rearrange("(t p) w -> p t w", p=P), blank[:, :, :]).then_inc(cleared, 16)
            sync.wait_ge(cleared, 32)

        @block.gpsimd
        def _(pool):
            pool.iota(pos[:, :], pattern=[[P, TILES]], base=0, channel_multiplier=1,
                      allow_small_or_imprecise_dtypes=True).then_inc(const, 1)
            pool.memset(blank[:, :, :], 0.0).then_inc(const, 1)
            pool.memset(blank_info[:, :, :], 0.0).then_inc(const, 1)
            pool.wait_ge(const, 3)
            pool.memset(blank[:, :, 0:2], float(PAD)).then_inc(filled, 1)
            pool.memset(blank[:, :, 4:5], float(ZERO_ROW)).then_inc(filled, 1)
            pool.memset(blank_info[:, :, 0:1], float(ZERO_ROW)).then_inc(filled, 1)

        @block.vector
        def _(dve):
            link, v = Chain(st, dve, step).link, nc.vector
            dve.wait_ge(loaded, 32)
            dve.wait_ge(const, 3)
            link(v.tensor_copy(tmp[:, :], mi[:, LAST, :]))
            link(v.tensor_scalar(last[:, :], tmp[:, :], float(NO_ROW), None, ALU.is_lt))
            link(v.tensor_scalar(low[:, :], m[:, KEY, :], float(N), None, ALU.is_lt))
            link(v.tensor_tensor(last[:, :], last[:, :], low[:, :], ALU.mult))
            link(v.tensor_scalar(npos[:, :], pos[:, :], float(N), None, ALU.add))
            link(v.tensor_tensor(tmp[:, :], m[:, KEY, :], npos[:, :], ALU.subtract))
            link(v.tensor_tensor(tmp[:, :], tmp[:, :], last[:, :], ALU.mult))
            link(v.tensor_tensor(tmp[:, :], tmp[:, :], npos[:, :], ALU.add))
            link(v.tensor_copy(mi[:, LAST, :], tmp[:, :]))
            link(v.tensor_scalar(tmp[:, :], m[:, KEY, :], -float(NO_ROW), None, ALU.add))
            link(v.tensor_tensor(tmp[:, :], tmp[:, :], last[:, :], ALU.mult))
            link(v.tensor_scalar(self.at_node[:, :], tmp[:, :], float(NO_ROW), None, ALU.add))
            link(v.tensor_copy(self.at_dst[:, :], mi[:, OTHER, :]))
            link(v.tensor_copy(self.pair[:, :, 0], pos[:, :]))
            link(v.tensor_copy(self.pair[:, :, 1], deg[:, :]))
        st.close()

    def middle(self):
        nc, m, found, rec = self.nc, self.m, self.found, self.rec
        st = Stage(nc, "link1_middle")
        tmp, std, flag, rank, spare = (st.sb(n, [P, TILES]) for n in ("tmp", "std", "flag", "rank", "spare"))
        below, ones = st.sb("below", [P, P]), st.sb("ones", [P, P])
        starts, counted, total = st.sb("starts", [P, BODIES + FINES]), st.sb("counted", [P, BODIES + FINES]), st.sb("total", [P, 1])
        bodies_f, bodies_i = st.sb("bodies_f", [P, 2]), st.sb("bodies_i", [P, 2], I32)
        pranks, ptotals = st.ps("ranks", [P, TILES]), st.ps("totals", [P, TILES])
        const, step, flagged, ranked, asked, rooted, made, stored = (
            st.sem(n) for n in ("const", "step", "flagged", "ranked", "asked", "rooted", "made", "stored"))
        block = st.block()

        @block.sync
        def _(sync):
            sync.wait_ge(made, 1)
            sync.dma_start(self.meta, m[:, :, :]).then_inc(stored, 16)
            sync.dma_start(self.bodies_out, bodies_i[0:1, :]).then_inc(stored, 16)
            sync.wait_ge(stored, 32)

        @block.gpsimd
        def _(pool):
            pool.memset(ones[:, :], 1.0).then_inc(const, 1)
            pool.memset(below[:, :], 1.0).then_inc(const, 1)
            pool.memset(spare[:, :], 0.0).then_inc(const, 1)
            pool.iota(starts[:, 0:BODIES], pattern=[[BODY, BODIES]], base=0, channel_multiplier=0,
                      allow_small_or_imprecise_dtypes=True)
            pool.iota(starts[:, BODIES:], pattern=[[FINE, FINES]], base=0, channel_multiplier=0,
                      allow_small_or_imprecise_dtypes=True).then_inc(const, 1)
            pool.wait_ge(const, 4)
            pool.affine_select(out=below[:, :], in_=below[:, :], compare_op=ALU.is_gt, fill=0.0, base=0,
                               pattern=[[1, P]], channel_multiplier=-1).then_inc(const, 1)

        @block.tensor
        def _(pe):
            pe.wait_ge(const, 5)
            pe.wait_ge(flagged, 1)
            nc.tensor.matmul(pranks[:, :], below[:, :], flag[:, :], start=True, stop=True)
            nc.tensor.matmul(ptotals[:, :], ones[:, :], flag[:, :], start=True, stop=True).then_inc(ranked, 1)

        @block.scalar
        def _(act):
            act.wait_ge(asked, 1)
            nc.scalar.activation(std[:, :], tmp[:, :], ACT.Sqrt).then_inc(rooted, 1)

        @block.vector
        def _(dve):
            link, v = Chain(st, dve, step).link, nc.vector
            dve.wait_ge(const, 5)
            link(v.tensor_copy(m[:, OWN, :].bitcast(U32), found[:, :, 0]))
            link(v.tensor_scalar(flag[:, :], found[:, :, 0], float(ZERO_ROW), None, ALU.is_lt))
            v.tensor_tensor(flag[:, :], flag[:, :], self.low[:, :], ALU.mult).then_inc(flagged, 1)
            v.tensor_scalar(tmp[:, :], found[:, :, 1], 1.0, None, ALU.max).then_inc(asked, 1)
            dve.wait_ge(rooted, 1)
            link(v.reciprocal(std[:, :], std[:, :]))
            link(v.tensor_scalar(tmp[:, :], found[:, :, 1], 0.0, None, ALU.is_gt))
            link(v.tensor_tensor(m[:, WEIGHT2, :], std[:, :], tmp[:, :], ALU.mult))
            link(v.tensor_tensor(rec[:, :, 3], m[:, WEIGHT2, :], m[:, WEIGHT2, :], ALU.mult))
            link(v.memset(rec[:, :, 5:LIST], 0.0))
            for w, a in ((0, m[:, KEY, :]), (1, self.at_dst[:, :]), (2, m[:, WEIGHT, :]), (4, found[:, :, 0])):
                link(v.tensor_copy(rec[:, :, w], a))
            dve.wait_ge(ranked, 1)
            link(v.tensor_tensor_scan(rank[:, :], ptotals[:, :], spare[:, :], 0.0, ALU.add, ALU.bypass))
            link(v.tensor_copy(total[:, :], rank[:, TILES - 1:TILES]))
            link(v.tensor_tensor(rank[:, :], rank[:, :], ptotals[:, :], ALU.subtract))
            link(v.tensor_tensor(rank[:, :], rank[:, :], pranks[:, :], ALU.add))
            link(v.tensor_scalar(rank[:, :], rank[:, :], -float(NO_ROW), None, ALU.add))
            link(v.tensor_tensor(rank[:, :], rank[:, :], flag[:, :], ALU.mult))
            link(v.tensor_scalar(self.at_rank[:, :], rank[:, :], float(NO_ROW), None, ALU.add))
            link(v.tensor_scalar(counted[:, :], starts[:, :], total[:, 0:1], None, ALU.is_lt))
            link(v.tensor_reduce(bodies_f[:, 0:1], counted[:, 0:BODIES], AX.X, ALU.add))
            link(v.tensor_reduce(bodies_f[:, 1:2], counted[:, BODIES:], AX.X, ALU.add))
            v.tensor_scalar(bodies_i[:, :], bodies_f[:, :], 1.0, None, ALU.max).then_inc(made, 1)
        st.close()

    def close(self):
        self.ctx.close()


def first_cheb_edges(nc, meta, h_table, taylor, sums_table, target):
    def setup(st, c):
        w1 = st.sb("taylor1", [D, D])
        turned = st.sb("sums_t", [D, GROUP * P])
        sent = [st.sb(f"sent{h}", [P, GROUP, D]) for h in (0, 1)]
        pt, pr = st.ps("turn", [P, 1024]), [st.ps(f"product{h}", [P, 512]) for h in (0, 1)]
        loaded_w, moved, tcopied, done = (st.sem(n) for n in ("loaded_w", "sums_turned", "turned_copied", "product_done"))
        stored = [st.sem(f"stored{h}") for h in (0, 1)]

        def sync(eng, i, h, first):
            st.gate(eng, c["copied"], (2 * i + h + 1) * GROUP)
            eng.dma_start(by_group(sums_table, 2 * i + h, 0, D), c["sums"][h][:, :, :]).then_inc(stored[h], 16)

        def pe_turn(eng, i, h, start):
            g = 2 * i + h
            st.gate(eng, c["copied"], (g + 1) * GROUP)
            if not (isinstance(g, int) and g == 0):
                st.gate(eng, tcopied, g)
            for j in range(GROUP):
                ins = nc.tensor.transpose(pt[0:D, j * P:(j + 1) * P], c["sums"][h][:, j, :], c["ident"][:, :])
            ins.then_inc(moved, 1)

        def pe_multiply(eng, i, h, start):
            g = 2 * i + h
            st.gate(eng, tcopied, g + 1)
            if not (isinstance(i, int) and i == 0):
                st.gate(eng, c["posted"], g - 1)
            for j in range(GROUP):
                ins = nc.tensor.matmul(pr[h][:, j * D:(j + 1) * D], turned[:, j * P:(j + 1) * P], w1[:, :], start=True, stop=True)
            ins.then_inc(done, 1)

        def act_post(eng, i, h, first):
            g = 2 * i + h
            st.gate(eng, moved, g + 1)
            if not (isinstance(g, int) and g == 0):
                st.gate(eng, done, g)
            nc.scalar.activation(turned[:, :], pt[0:D, 0:GROUP * P], ACT.Copy).then_inc(tcopied, 1)

        def values(eng, i, h, first):
            st.gate(eng, c["got"][h], (i + 1) * c["per"])
            w = c["m"][:, WEIGHT2, bass.ds((2 * i + h) * GROUP, GROUP)].unsqueeze(2).to_broadcast([P, GROUP, D])
            return nc.vector.tensor_tensor(c["values"][h][:, :, :], c["rows"][h][:, :, :], w, ALU.mult)

        def post(eng, i, h, first):
            st.gate(eng, done, 2 * i + h + 1)
            if not first:
                st.gate(eng, c["put"][h], i * c["put_per"])
            return nc.vector.tensor_copy(sent[h][:, :, :], pr[h][:, 0:GROUP * D].rearrange("p (j w) -> p j w", w=D))

        def sync_end(eng):
            for h in (0, 1):
                eng.wait_ge(stored[h], 16 * c["half"])
        return {"sync_start": lambda eng: eng.dma_start(w1[:, :], taylor[D:2 * D, :]).then_inc(loaded_w, 16),
                "sync": sync, "sync_end": sync_end, "pe_start": lambda eng: eng.wait_ge(loaded_w, 16),
                "pe_turn": pe_turn, "pe_multiply": pe_multiply, "act_post": act_post,
                "act_reuse": lambda eng, i, h: st.gate(eng, stored[h], i * 16),
                "values": values, "post": post, "sent": sent}
    edge_stage(nc, "cheb_first", meta, [(h_table, OTHER, 0, D)], D, D, setup, scatter=target, add=True)


def rate(nc, dve, st, sem, t_tile, out, inverse, coef):
    ch = Chain(st, dve, sem)
    ch.link(nc.vector.tensor_scalar(out[:, :], t_tile[:, :], 1e-8, -1.0, ALU.max, ALU.mult))
    ch.link(nc.vector.tensor_scalar(coef[:, :], inverse, out[:, 0:1], None, ALU.mult))


def first_expm_edges(nc, meta, h_table, t, factors, terms_table, target):
    def setup(st, c):
        K1 = factors.shape[1]
        sent = [st.sb(f"sent{h}", [P, GROUP, D]) for h in (0, 1)]
        fac, tt, mt, coef = st.sb("factors", [P, K1]), st.sb("t", [P, 1]), st.sb("minus_t", [P, 1]), st.sb("coef", [P, K1])
        loaded_w, cstep = st.sem("loaded_w"), st.sem("coef_step")
        stored = [st.sem(f"stored{h}") for h in (0, 1)]

        def sync_start(eng):
            eng.dma_start(fac[:, :], broadcast(factors[0, :], P)).then_inc(loaded_w, 16)
            eng.dma_start(tt[:, :], broadcast(t, P)).then_inc(loaded_w, 16)

        def vector_start(eng):
            eng.wait_ge(loaded_w, 32)
            rate(nc, eng, st, cstep, tt, mt, fac[:, :], coef)

        def sync(eng, i, h, first):
            st.gate(eng, c["posted"], 2 * i + h + 1)
            eng.dma_start(by_group(terms_table, 2 * i + h, 0, D), sent[h][:, :, :]).then_inc(stored[h], 16)

        def values(eng, i, h, first):
            st.gate(eng, c["got"][h], (i + 1) * c["per"])
            w = c["m"][:, WEIGHT, bass.ds((2 * i + h) * GROUP, GROUP)].unsqueeze(2).to_broadcast([P, GROUP, D])
            return nc.vector.tensor_tensor(c["values"][h][:, :, :], c["rows"][h][:, :, :], w, ALU.mult)

        def post(eng, i, h, first):
            st.gate(eng, c["copied"], (2 * i + h + 1) * GROUP)
            if not first:
                st.gate(eng, c["put"][h], i * c["put_per"])
                st.gate(eng, stored[h], i * 16)
            return nc.vector.tensor_scalar(sent[h][:, :, :], c["sums"][h][:, :, :], coef[:, 1:2], None, ALU.mult)

        def sync_end(eng):
            for h in (0, 1):
                eng.wait_ge(stored[h], 16 * c["half"])
        return {"sync_start": sync_start, "vector_start": vector_start, "sync": sync, "sync_end": sync_end,
                "values": values, "post": post, "sent": sent}
    edge_stage(nc, "expm_first", meta, [(h_table, OTHER, 0, D)], D, D, setup, scatter=target, add=True)


def tier_stage(nc, name, meta, bodies_in, before, tables, level, pairs, target, group=GROUP, taylor=None, expm=None):
    st = Stage(nc, name)
    m = st.sb("meta", [P, META, TILES + 2 * group])
    mi = m[:, :, :].bitcast(U32)
    acc = st.sb("acc", [P, TILES, D])
    ident, ones = st.sb("ident", [P, P]), st.sb("ones", [P, P])
    two = lambda n, shape, dt=F32: [st.sb(f"{n}{h}", shape, dt) for h in (0, 1)]
    index, keyslot, rows, values = two("index", [P, group], U32), two("keyslot", [P, group]), two("rows", [P, group, D]), two("values", [P, group, D])
    same, carry, sums = two("same", [P, group, P]), two("carry", [P, group, P]), two("sums", [P, group, D])
    nonzero = st.sb("nonzero", [P, group, D])
    some, any_, flag = st.sb("some", [P, 1]), st.sb("any", [P, 1]), st.sb("flag", [P, 1], I32)
    given = st.sb("given", [1, 2], I32)
    pkey = st.ps("pkey", [P, 1024])
    psum = [st.ps(f"psum{b}", [P, 512]) for b in (0, 1)]
    (const, loaded, staged, key_turned, same_made, values_ready, summed, copied, stored, step, cleared, scaled,
     turned_s, tcopied, product, checked, tested, level_ready, placed, cstep) = (st.sem(n) for n in (
         "const", "loaded", "staged", "key_turned", "same_made", "values_ready", "summed", "sum_copied",
         "stored", "step", "cleared", "scaled", "sums_turned", "turned_copied", "product", "checked", "tested",
         "level_ready", "placed", "coef_step"))
    got, sent, put = ([st.sem(f"{n}{h}") for h in (0, 1)] for n in ("gathered", "sent", "put"))
    if taylor is not None:
        v = st.sb("taylor", [D, taylor.shape[0] // D, D])
        turned = st.sb("turned", [D, group * P])
        pt = st.ps("turn", [P, 1024])
        kept = sums
        n_loads = 3
    else:
        t, factors = expm
        K1 = factors.shape[1]
        fac, tt, mt, coef = st.sb("factors", [P, 2 * K1]), st.sb("t", [P, 1]), st.sb("minus_t", [P, 1]), st.sb("coef", [P, K1])
        kept = two("term", [P, group, D])
        n_loads = 5
    pr = st.ps("product", [P, 512])
    weight = WEIGHT2 if taylor is not None else WEIGHT
    block = st.block()
    per = group * 16

    def levels(eng, run):
        run(0, level, before, tables[0], OTHER)
        if eng is vec[0]:
            eng.sem_inc(level_ready, 1)
        if not pairs:
            return
        at_once = 4 if pairs % 2 == 0 else 2
        with eng.Fori(0, 2 * pairs // at_once) as q:
            st.gate(eng, level_ready, at_once * q + 1)
            any_due = eng.value_load(flag[0:1, 0:1], min_val=0, max_val=1)
            with eng.If(any_due > 0):
                for k in range(at_once):
                    n = at_once * q + (1 + k)
                    if k:
                        st.gate(eng, level_ready, n)
                        due = eng.value_load(flag[0:1, 0:1], min_val=0, max_val=1)
                    with eng.If(due > 0) if k else nullcontext():
                        run(n, n + level, tables[k % 2], tables[1 - k % 2], OWN)
                    if eng is vec[0]:
                        eng.sem_inc(level_ready, 1)
            if eng is vec[0]:
                with eng.If(any_due < 1):
                    eng.sem_inc(level_ready, at_once)
    vec = [None]

    def count(eng):
        eng.wait_ge(loaded, 16 * n_loads)
        if group == GROUP:
            bodies = eng.value_load(given[0:1, 0:1], min_val=1, max_val=BODIES)
            return bodies, lambda body: rounds(st, eng, bodies, body)
        fine = eng.value_load(given[0:1, 1:2], min_val=1, max_val=FINES)
        return fine, lambda body: fine_rounds(eng, fine, body)

    @block.sync
    def _(sync):
        sync.dma_start(m[:, :, 0:TILES], meta).then_inc(loaded, 16)
        sync.dma_start(given[:, :], bodies_in).then_inc(loaded, 16)
        if taylor is not None:
            sync.dma_start(v[:, :, :], taylor.rearrange("(k i) o -> i k o", i=D)).then_inc(loaded, 16)
        else:
            for n in (0, 1):
                sync.dma_start(fac[:, n * K1:(n + 1) * K1], broadcast(factors[n, :], P)).then_inc(loaded, 16)
            sync.dma_start(tt[:, :], broadcast(t, P)).then_inc(loaded, 16)
        bodies, over_list = count(sync)

        def run(n, k, source, into, row):
            def body(i):
                c = n * bodies + i
                for h in (0, 1):
                    if taylor is not None:
                        st.gate(sync, copied, c * (2 * group) + (h + 1) * group)
                    else:
                        st.gate(sync, scaled, c * 2 + (h + 1))
                    sync.dma_start(by_group(into, 2 * i + h, 0, D, group), kept[h][:, :, :]).then_inc(stored, 16)
            over_list(body)
        levels(sync, run)
        st.gate(sync, stored, bodies * 32)

    @block.gpsimd
    def _(pool):
        pool.memset(sums[1][:, :, :], 0.0).then_inc(cleared, 1)
        pool.memset(ones[:, :], 1.0).then_inc(cleared, 1)
        pool.memset(some[:, :], 0.0).then_inc(cleared, 1)
        identity(st, pool, ident, const)
        bodies, over_list = count(pool)

        def run(n, k, source, into, row):
            def body(i):
                c = n * bodies + i
                st.gate(pool, staged, c + 1)
                for h in (0, 1):
                    for j in range(group):
                        pool.indirect_dma_start(rows[h][:, j, :], None, source,
                                                bass.IndirectOffsetOnAxis(ap=index[h][:, j:j + 1], axis=0)).then_inc(got[h], 16)
            over_list(body)
        levels(pool, run)

        def add(i):
            for h in (0, 1):
                st.gate(pool, sent[h], i + 1)
                for j in range(group):
                    pool.indirect_dma_start(target, bass.IndirectOffsetOnAxis(ap=index[h][:, j:j + 1], axis=0),
                                            rows[h][:, j, :], None, compute_op=ALU.add).then_inc(put[h], 16)
        over_list(add)
        for h in (0, 1):
            st.gate(pool, put[h], bodies * per)

    @block.tensor
    def _(pe):
        pe.wait_ge(const, 2)
        pe.wait_ge(cleared, 3)
        bodies, over_list = count(pe)

        def run(n, k, source, into, row):
            def body(i):
                c = n * bodies + i
                st.gate(pe, staged, c + 1)
                for h in (0, 1):
                    if h:
                        st.gate(pe, same_made, c * 2 + 1)
                    for j in range(group):
                        ins = nc.tensor.transpose(pkey[:, j * P:(j + 1) * P], keyslot[h][:, j:j + 1].to_broadcast([P, P]), ident[:, :])
                    ins.then_inc(key_turned, 1)
                for h in (0, 1):
                    st.gate(pe, values_ready, c * 2 + h + 1)
                    for j in range(group):
                        tile = h * group + j
                        if tile >= 2:
                            st.gate(pe, copied, c * (2 * group) + (tile - 1))
                        nc.tensor.matmul(psum[tile % 2][:, 0:D], same[h][:, j, :], values[h][:, j, :], start=True, stop=False)
                        if tile:
                            st.gate(pe, copied, c * (2 * group) + tile)
                        prior = sums[h][:, j - 1, :] if j else sums[1 - h][:, group - 1, :]
                        nc.tensor.matmul(psum[tile % 2][:, 0:D], carry[h][:, j, :], prior, start=False, stop=True).then_inc(summed, 1)
                if taylor is None:
                    return
                for h in (0, 1):
                    st.gate(pe, copied, c * (2 * group) + (h + 1) * group)
                    if h:
                        st.gate(pe, tcopied, c * 2 + 1)
                    for j in range(group):
                        ins = nc.tensor.transpose(pt[0:D, j * P:(j + 1) * P], sums[h][:, j, :], ident[:, :])
                    ins.then_inc(turned_s, 1)
                    st.gate(pe, tcopied, c * 2 + h + 1)
                    if h:
                        st.gate(pe, placed, c * 2 + 1)
                    for j in range(group):
                        ins = nc.tensor.matmul(pr[:, j * D:(j + 1) * D], turned[:, j * P:(j + 1) * P],
                                               v[:, bass.ds(k, 1), :].rearrange("i k o -> i (k o)"), start=True, stop=True)
                    ins.then_inc(product, 1)
            over_list(body)
            st.gate(pe, checked, n + 1)
            nc.tensor.matmul(pr[:, 0:1], ones[:, :], some[:, :], start=True, stop=True).then_inc(tested, 1)
        levels(pe, run)

    @block.scalar
    def _(act):
        act.wait_ge(cleared, 3)
        bodies, over_list = count(act)

        def run(n, k, source, into, row):
            def body(i):
                c = n * bodies + i
                for h in (0, 1):
                    for j in range(group):
                        st.gate(act, summed, c * (2 * group) + (h * group + j + 1))
                        nc.scalar.activation(sums[h][:, j, :], psum[(h * group + j) % 2][:, 0:D], ACT.Copy).then_inc(copied, 1)
                if taylor is None:
                    return
                for h in (0, 1):
                    st.gate(act, turned_s, c * 2 + h + 1)
                    if h:
                        st.gate(act, product, c * 2 + 1)
                    nc.scalar.activation(turned[:, :], pt[0:D, 0:group * P], ACT.Copy).then_inc(tcopied, 1)
            over_list(body)
        levels(act, run)

    @block.vector
    def _(dve):
        vec[0] = dve
        vx = nc.vector
        dve.wait_ge(cleared, 3)
        bodies, over_list = count(dve)
        if taylor is None:
            rate(nc, dve, st, cstep, tt, mt, fac[:, 0:K1], coef)
        steps_body, steps_level = 6, 2

        def run(n, k, source, into, row):
            opening = isinstance(n, int)

            def chain(i, at):
                return (n * bodies + i) * steps_body + n * steps_level + at

            def stage(i):
                for h in (0, 1):
                    g = (2 * i + h) * group
                    vx.tensor_copy(index[h][:, :], mi[:, row, bass.ds(g, group)])
                    ins = vx.tensor_copy(keyslot[h][:, :], m[:, KEY, bass.ds(g, group)])
                ins.then_inc(staged, 1)

            def body(i):
                c = n * bodies + i
                for h in (0, 1):
                    st.gate(dve, key_turned, c * 2 + h + 1)
                    turned_k = pkey[:, 0:group * P].rearrange("p (j e) -> p j e", e=P)
                    for r, mat in ((KEY, same), (PREV, carry)):
                        ins = vx.tensor_tensor(mat[h][:, :, :], turned_k,
                                               m[:, r, bass.ds((2 * i + h) * group, group)].unsqueeze(2).to_broadcast([P, group, P]), ALU.is_equal)
                    ins.then_inc(same_made, 1)
                for h in (0, 1):
                    st.gate(dve, got[h], (c + 1) * per)
                    w = m[:, weight, bass.ds((2 * i + h) * group, group)].unsqueeze(2).to_broadcast([P, group, D])
                    vx.tensor_tensor(values[h][:, :, :], rows[h][:, :, :], w, ALU.mult).then_inc(values_ready, 1)
                st.gate(dve, values_ready, c * 2 + 2)
                with dve.If(i + 1 < bodies):
                    stage(i + 1)
                for h in (0, 1):
                    part = acc[:, bass.ds((2 * i + h) * group, group), :]
                    if taylor is not None:
                        st.gate(dve, product, c * 2 + h + 1)
                        share = pr[:, 0:group * D].rearrange("p (j w) -> p j w", w=D)
                        if opening:
                            vx.tensor_copy(part, share).then_inc(placed, 1)
                        else:
                            vx.tensor_tensor(part, part, share, ALU.add).then_inc(placed, 1)
                    else:
                        st.gate(dve, copied, c * (2 * group) + (h + 1) * group)
                        vx.tensor_scalar(kept[h][:, :, :], sums[h][:, :, :], coef[:, bass.ds(k, 1)], None, ALU.mult).then_inc(scaled, 1)
                        st.gate(dve, scaled, c * 2 + h + 1)
                        if opening:
                            vx.tensor_scalar(part, kept[h][:, :, :], fac[:, k + K1:k + K1 + 1], None, ALU.mult).then_inc(placed, 1)
                        else:
                            vx.scalar_tensor_tensor(out=part, in0=kept[h][:, :, :], scalar=fac[:, bass.ds(k + K1, 1)], in1=part,
                                                    op0=ALU.mult, op1=ALU.add).then_inc(placed, 1)
                    vx.tensor_scalar(nonzero[:, :, :], kept[h][:, :, :], 0.0, None, ALU.not_equal).then_inc(step, 1)
                    st.gate(dve, step, chain(i, 3 * h + 1))
                    vx.tensor_reduce(any_[:, :], nonzero[:, :, :].rearrange("p j w -> p (j w)"), AX.X, ALU.max).then_inc(step, 1)
                    st.gate(dve, step, chain(i, 3 * h + 2))
                    vx.tensor_tensor(some[:, :], some[:, :], any_[:, :], ALU.max).then_inc(step, 1)
                    st.gate(dve, step, chain(i, 3 * h + 3))
                    st.gate(dve, placed, c * 2 + h + 1)
                st.gate(dve, stored, (c + 1) * 32)
            stage(0)
            over_list(body)
            dve.sem_inc(checked, 1)
            st.gate(dve, tested, n + 1)
            vx.tensor_scalar(flag[:, :], pr[:, 0:1], 1.0, None, ALU.min).then_inc(step, 1)
            st.gate(dve, step, chain(bodies, 1))
            vx.memset(some[:, :], 0.0).then_inc(step, 1)
            st.gate(dve, step, chain(bodies, 2))
        levels(dve, run)

        def give(i):
            for h in (0, 1):
                with dve.If(i > 0):
                    st.gate(dve, put[h], i * per)
                g = (2 * i + h) * group
                vx.tensor_copy(index[h][:, :], mi[:, LAST, bass.ds(g, group)])
                vx.tensor_copy(rows[h][:, :, :], acc[:, bass.ds(g, group), :]).then_inc(sent[h], 1)
        over_list(give)
    st.close()


def gnn(nc, x, src, dst, ea16, ea32, ew, w, factors, out):
    ctx = ExitStack()
    Stage.psum = ctx.enter_context(nc.psum_tensor("psum", [P, 8 * BANK], F32))
    dram = lambda name, shape: nc.dram_tensor(name, shape, F32, kind="Internal").ap()
    by_dst, half_d = dram("by_dst", [EP, REC]), dram("half_d", [EP, REC])
    by_src, half_s = dram("by_src", [EP, NARROW]), dram("half_s", [EP, NARROW])
    p1, q1, p2, q2, agg1, agg2 = (dram(n, [N, 16]) for n in ("p1", "q1", "p2", "q2", "agg1", "agg2"))
    eaw1, eaw2, ea32t = dram("eaw1", [EP, 16]), dram("eaw2", [EP, 16]), dram("ea32t", [32, EP])
    meta_d, meta_s = dram("meta_d", [P, META, TILES]), dram("meta_s", [P, META, TILES])
    x1, h1, agg3 = dram("x1", [N, D]), dram("h1", [N, D]), dram("agg3", [N, D])
    x2, h2, h3 = dram("x2", [N, D]), dram("h2", [N, D]), dram("h3", [N, D])
    aggc = dram("aggc", [N + EP, D])
    taylor = dram("taylor", [w["L2_gnn_W"].shape[0] * D, D])
    degree, info1 = dram("degree", [EP]), dram("info1", [N, 2])
    infos = [info1] + [dram(f"info{n}", [N, 2]) for n in (2, 3, 4)]
    metas = [dram(f"meta{n}", [P, META, TILES]) for n in (1, 2, 3, 4)]
    lists = [None] + [dram(f"list{n}", [EP, LIST]) for n in (2, 3, 4)]
    counts = [None] + [nc.dram_tensor(f"bodies{n}", [1, 2], I32, kind="Internal").ap() for n in (2, 3, 4)]
    level_sums = [dram(f"sums{n}", [EP + P, D]) for n in (1, 2, 3)]
    turns = [dram(f"turn{n}", [EP + P, D]) for n in (0, 1)]
    zeroes = zero_pieces(agg1, agg2, agg3, aggc, out[N:, :], level_sums[0][EP:, :], *level_sums[1:], *turns)
    ratio = [12, 11, 6, 3, 13, 8]
    shares = [-(-len(zeroes) * x // sum(ratio)) for x in ratio]
    zeroes = [zeroes[sum(shares[:n]):sum(shares[:n + 1])] for n in range(len(shares))]

    inputs = (src, dst, ew, ea16, ea32)
    next_sort = Sort(nc, "sort_src", NARROW, SRC, by_src, half_s, inputs)
    sort = Sort(nc, "sort_dst", REC, DST, by_dst, half_d, inputs)
    for n, part in enumerate(parts_of_chunks(len(DIGITS))):
        sort.ranks(n, zeroes[n])
        projection_stage(nc, "project1", part, sort.scatter(n), {"x": ([x], D)}, p1, q1, w["L0_gnn_W_msg1"][0:D, :],
                         w["L0_gnn_W_skip1"], w["L0_gnn_b_skip1"], 2, True,
                         (None, cheb_weights_work(nc, w["L2_gnn_W"], taylor), next_sort.rank_work(0))[n])
    sort.close()
    order_stage(nc, "order_dst", by_dst, DST, SRC, meta_d)
    edge_features_stage(nc, by_dst, w["L0_gnn_W_msg1"][D:D + 16, :], w["L0_gnn_W_msg2"][16:32, :],
                        w["L0_gnn_b_msg1"], w["L0_gnn_b_msg2"], eaw1, eaw2, ea32t, zeroes[len(DIGITS)])
    conv_edges(nc, "conv1", meta_d, p1, eaw1, agg1)
    sort = next_sort
    projection_stage(nc, "project2", (0, CHUNKS), sort.scatter(0), {"agg": ([agg1], 16), "q": ([q1], 16)}, p2, q2,
                     w["L0_gnn_W_msg2"][0:16, :], w["L0_gnn_W_skip2"], w["L0_gnn_b_skip2"], 8, False)
    conv_edges(nc, "conv2", meta_d, p2, eaw2, agg2)
    for n, part in enumerate(parts_of_chunks(len(DIGITS) - 1), 1):
        sort.ranks(n, zeroes[len(DIGITS) + n])
        lin3_stage(nc, part, sort.scatter(n), x, agg2, q2, w["L0_gnn_W_lin3"], w["L0_gnn_b_lin3"], x1, h1)
    sort.close()
    order_stage(nc, "order_src", by_src, SRC, DST, meta_s, degree=degree)
    message_edges(nc, meta_d, h1, ea32t, w["L1_gnn_W1"], w["L1_gnn_b1"], w["L1_gnn_W2"], w["L1_gnn_b2"], agg3)
    link = FirstLink(nc, meta_s, degree, infos[0], metas[0], lists[1], counts[1])
    link.begin()
    gru = lambda part, beside: gru_stage(nc, part, beside, x1, h1, agg3, w["L1_gnn_w_ih"], w["L1_gnn_w_hh"],
                                         w["L1_gnn_b_ih"], w["L1_gnn_b_hh"], x2, h2)
    early, late = parts_of_chunks(2)
    gru(early, one_after_the_other(link.announce(), link.find()))
    link.middle()
    gru(late, link.list_up())
    link.close()
    for n in (1, 2, 3):
        link_stage(nc, f"link{n + 1}", lists[n], infos[n], counts[n], metas[n],
                   lists[n + 1] if n < 3 else None, counts[n + 1] if n < 3 else None)
    first_cheb_edges(nc, metas[0], h2, taylor, level_sums[0], aggc)
    for n in (1, 2, 3):
        tier_stage(nc, f"cheb_tier{n + 1}", metas[n], counts[n], level_sums[n - 1], level_sums[n:n + 1] if n < 3 else turns,
                   n + 1, 0 if n < 3 else (CHEB_K - 4) // 2, aggc, GROUP if n < 3 else FEW, taylor=taylor)
    cheb_stage(nc, x2, h2, aggc, info1, taylor[0:D, :], w["L2_gnn_bias"], h3, out)
    first_expm_edges(nc, metas[0], h3, w["L3_gnn_t"], factors, level_sums[0], out)
    for n in (1, 2, 3):
        tier_stage(nc, f"expm_tier{n + 1}", metas[n], counts[n], level_sums[n - 1], level_sums[n:n + 1] if n < 3 else turns,
                   n + 1, 0 if n < 3 else (EXPM_K - 4) // 2, out, GROUP if n < 3 else FEW, expm=(w["L3_gnn_t"], factors))
    ctx.close()


INS = ['x', 'src', 'dst', 'edge_attr_16', 'edge_attr_32', 'edge_weight']
WS = ['L0_gnn_W_msg1', 'L0_gnn_b_msg1', 'L0_gnn_W_skip1', 'L0_gnn_b_skip1', 'L0_gnn_W_msg2', 'L0_gnn_b_msg2', 'L0_gnn_W_skip2', 'L0_gnn_b_skip2', 'L0_gnn_W_lin3', 'L0_gnn_b_lin3', 'L1_gnn_W1', 'L1_gnn_b1', 'L1_gnn_W2', 'L1_gnn_b2', 'L1_gnn_w_ih', 'L1_gnn_w_hh', 'L1_gnn_b_ih', 'L1_gnn_b_hh', 'L2_gnn_W', 'L2_gnn_bias', 'L3_gnn_t']


TURNED = ['L1_gnn_W1', 'L1_gnn_W2', 'L1_gnn_w_ih', 'L1_gnn_w_hh']


def kernel(**inputs):
    import numpy as np
    import concourse.bacc as bacc
    from concourse import mybir as mb
    from concourse.bass_utils import run_bass_kernel_spmd as run

    nc = bacc.Bacc("TRN2", target_bir_lowering=False, num_devices=1)
    arrays, aps = {}, {}
    for name in INS + WS:
        a = np.asarray(inputs[name])
        a = np.ascontiguousarray(a.T if name in TURNED else a)
        arrays[f"in_{name}"] = a
        aps[name] = nc.dram_tensor(f"in_{name}", a.shape, mb.dt.from_np(a.dtype), kind="ExternalInput").ap()
    series = np.array([1.0 / factorial(j) for j in range(SERIES + 1)])
    power = np.ones(1)
    for _ in range(SUBSTEPS):
        power = np.convolve(power, series)
    factors = np.ones((2, EXPM_K + 1), np.float32)
    for k in range(1, EXPM_K + 1):
        factors[0, k] = 1.0 / k
        factors[1, k] = power[k] * float(factorial(k)) / float(SUBSTEPS) ** k
    arrays["in_factors"] = factors
    fac = nc.dram_tensor("in_factors", factors.shape, mb.dt.float32, kind="ExternalInput").ap()
    out = nc.dram_tensor("out_nodes", (N + EP, D), mb.dt.float32, kind="ExternalOutput").ap()
    gnn(nc, *[aps[n] for n in INS], {n: aps[n] for n in WS}, fac, out)
    r = run(nc, [arrays], core_ids=[0])
    return r.results[0]["out_nodes"][0:N]
```
